# Optimizing a Trainium2 kernel written in Bass

```python
import numpy as np
import jax
import jax.numpy as jnp

def _softmax(x, axis=-1):
    return jax.nn.softmax(x, axis=axis)

def _gelu(x):
    return jax.nn.gelu(x, approximate=True)

def _silu(x):
    return jax.nn.silu(x)

def _sigmoid(x):
    return jax.nn.sigmoid(x)

def _layernorm(x, axis=-1, eps=1e-05):
    m = jnp.mean(x, axis=axis, keepdims=True)
    v = jnp.var(x, axis=axis, keepdims=True)
    return (x - m) / jnp.sqrt(v + eps)

def _scatter_add(tgt, idx, src, axis=0):
    return tgt.at[idx].add(src)

def _segment_sum(src, seg, n):
    return jax.ops.segment_sum(src, seg, n)
kernel_name = 'mk_early_fusion_d1_tok_img768_r4_9bf861'

def setup_inputs(seed: int=0):
    np.random.seed(seed)
    _w = jnp.asarray

    def _rec_inputs():
        import jax
        import jax.numpy as jnp
        _rk = jax.random.key(seed)
        x = -0.000356955 + 1 * jax.random.normal(jax.random.fold_in(_rk, 1), (64, 3, 224, 224), jnp.float32)
        txt = -0.00110557 + 1.15431 * jax.random.normal(jax.random.fold_in(_rk, 2), (64, 128, 192), jnp.float32)
        return (x, txt)
    x, txt = _rec_inputs()

    def _L0_tok_setup():
        import jax, jax.numpy as jnp
        import numpy as np
        P1, P2, C = (16, 16, 3)
        EMB = 192
        PATCH_DIM = P1 * P2 * C
        NUM_PATCHES = 196
        EPS = 1e-05

        def _patchify(x):
            B, c, H, Wd = x.shape
            nh, nw = (H // P1, Wd // P2)
            x = x.reshape(B, c, nh, P1, nw, P2)
            x = x.transpose(0, 2, 4, 3, 5, 1)
            return x.reshape(B, nh * nw, P1 * P2 * c)
        key = jax.random.key(seed)
        k1, k2, k3, k4 = jax.random.split(key, 4)
        x = jax.random.normal(k1, (128, C, 224, 224), dtype=jnp.float32)
        ln_w = jnp.ones((PATCH_DIM,), dtype=jnp.float32)
        ln_b = jnp.zeros((PATCH_DIM,), dtype=jnp.float32)
        lim = 1.0 / np.sqrt(PATCH_DIM)
        W = jax.random.uniform(k2, (PATCH_DIM, EMB), minval=-lim, maxval=lim, dtype=jnp.float32)
        b = jax.random.uniform(k3, (EMB,), minval=-lim, maxval=lim, dtype=jnp.float32)
        pos_emd = jax.random.normal(k4, (1, NUM_PATCHES, EMB), dtype=jnp.float32)
        return {'x': x, 'ln_w': ln_w, 'ln_b': ln_b, 'W': W, 'b': b, 'pos_emd': pos_emd}
    _L0_tok_all = _L0_tok_setup()
    _L0_tok_in = {k: v for k, v in _L0_tok_all.items() if k in ('ln_w', 'ln_b', 'W', 'b', 'pos_emd')}
    del _L0_tok_all

    def _L0_attn_setup():
        import jax, jax.numpy as jnp
        import numpy as np
        B_SZ, L, D, N = (4, 512, 192, 16)
        key = jax.random.key(seed)
        ks = jax.random.split(key, 8)
        x = jax.random.normal(ks[0], (B_SZ, L, D), dtype=jnp.float32)
        A_log = jnp.log(jnp.broadcast_to(jnp.arange(1, N + 1, dtype=jnp.float32), (D, N)))
        W_bc = jax.random.normal(ks[1], (2 * N, D), dtype=jnp.float32) / jnp.sqrt(D)
        b_bc = jnp.zeros((2 * N,), dtype=jnp.float32)
        W_1 = jax.random.normal(ks[2], (1, D), dtype=jnp.float32) / jnp.sqrt(D)
        b_1 = jnp.zeros((1,), dtype=jnp.float32)
        W_d = jax.random.normal(ks[3], (D, 1), dtype=jnp.float32)
        b_d = jnp.zeros((D,), dtype=jnp.float32)
        return {'x': x, 'A_log': A_log, 'W_bc': W_bc, 'b_bc': b_bc, 'W_1': W_1, 'b_1': b_1, 'W_d': W_d, 'b_d': b_d}
    _L0_attn_all = _L0_attn_setup()
    _L0_attn_in = {k: v for k, v in _L0_attn_all.items() if k in ('A_log', 'W_bc', 'b_bc', 'W_1', 'b_1', 'W_d', 'b_d')}
    del _L0_attn_all

    def _L0_ffn_setup():
        import jax, jax.numpy as jnp
        import numpy as np
        E = 128
        I = 464
        IS = 928
        K = 6
        G = 1
        TG = 1
        SCALE = 2.5
        CAP = 192

        def moe_forward(hidden_states, Wg, e_bias, W_gate_up, W_down, Wsg, Wsu, Wsd):
            B, S, H = hidden_states.shape
            x = hidden_states.reshape(-1, H)
            T = x.shape[0]
            logits = x.astype(jnp.float32) @ Wg.T
            sig = jax.nn.sigmoid(logits)
            choice = sig + e_bias[None, :]
            grp = choice.reshape(T, G, E // G)
            group_scores = jax.lax.top_k(grp, 2)[0].sum(-1)
            gidx = jax.lax.top_k(group_scores, TG)[1]
            gmask = jnp.zeros((T, G), jnp.float32).at[jnp.arange(T)[:, None], gidx].set(1.0)
            smask = jnp.repeat(gmask, E // G, axis=1)
            scores_for_choice = jnp.where(smask > 0, choice, 0.0)
            topk_idx = jax.lax.top_k(scores_for_choice, K)[1]
            topk_w = jnp.take_along_axis(sig, topk_idx, axis=1)
            topk_w = topk_w / (topk_w.sum(-1, keepdims=True) + 1e-20)
            topk_w = topk_w * SCALE
            P = T * K
            flat_e = topk_idx.reshape(-1)
            order = jnp.argsort(flat_e)
            se = flat_e[order]
            counts = jax.ops.segment_sum(jnp.ones(P, jnp.int32), flat_e, num_segments=E)
            starts = jnp.cumsum(counts) - counts
            pos = jnp.arange(P) - starts[se]
            buf_idx = jnp.where(pos < CAP, se * CAP + pos, E * CAP)
            tok_of_pair = (order // K).astype(jnp.int32)
            w_of_pair = topk_w.reshape(-1)[order]
            token_buf = jnp.zeros((E * CAP,), jnp.int32).at[buf_idx].set(tok_of_pair, mode='drop')
            w_buf = jnp.zeros((E * CAP,), x.dtype).at[buf_idx].set(w_of_pair.astype(x.dtype), mode='drop')
            xb = x[token_buf].reshape(E, CAP, H)
            gu = jnp.einsum('ech,ehf->ecf', xb, W_gate_up)
            g, u = jnp.split(gu, 2, axis=-1)
            inter = jax.nn.silu(g) * u
            yb = jnp.einsum('eci,eih->ech', inter, W_down)
            yb = yb * w_buf.reshape(E, CAP, 1)
            routed = jnp.zeros((T, H), x.dtype).at[token_buf].add(yb.reshape(E * CAP, H))
            shared = jax.nn.silu(x @ Wsg) * (x @ Wsu) @ Wsd
            return (routed + shared).reshape(B, S, H)
        key = jax.random.key(seed)
        ks = jax.random.split(key, 8)
        B, S, H = (1, 512, 192)
        sc = 0.02
        return {'hidden_states': jax.random.normal(ks[0], (B, S, H), jnp.float32), 'Wg': jax.random.normal(ks[1], (E, H), jnp.float32) * sc, 'e_bias': jnp.zeros((E,), jnp.float32), 'W_gate_up': jax.random.normal(ks[2], (E, H, 2 * I), jnp.float32) * sc, 'W_down': jax.random.normal(ks[3], (E, I, H), jnp.float32) * sc, 'Wsg': jax.random.normal(ks[4], (H, IS), jnp.float32) * sc, 'Wsu': jax.random.normal(ks[5], (H, IS), jnp.float32) * sc, 'Wsd': jax.random.normal(ks[6], (IS, H), jnp.float32) * sc}
    _L0_ffn_all = _L0_ffn_setup()
    _L0_ffn_in = {k: v for k, v in _L0_ffn_all.items() if k in ('Wg', 'e_bias', 'W_gate_up', 'W_down', 'Wsg', 'Wsu', 'Wsd')}
    del _L0_ffn_all
    return {'x': x, 'txt': txt, 'L0_tok_ln_w': _L0_tok_in['ln_w'], 'L0_tok_ln_b': _L0_tok_in['ln_b'], 'L0_tok_W': _L0_tok_in['W'], 'L0_tok_b': _L0_tok_in['b'], 'L0_tok_pos_emd': _L0_tok_in['pos_emd'], 'L0_attn_A_log': _L0_attn_in['A_log'], 'L0_attn_W_bc': _L0_attn_in['W_bc'], 'L0_attn_b_bc': _L0_attn_in['b_bc'], 'L0_attn_W_1': _L0_attn_in['W_1'], 'L0_attn_b_1': _L0_attn_in['b_1'], 'L0_attn_W_d': _L0_attn_in['W_d'], 'L0_attn_b_d': _L0_attn_in['b_d'], 'L0_ffn_Wg': _L0_ffn_in['Wg'], 'L0_ffn_e_bias': _L0_ffn_in['e_bias'], 'L0_ffn_W_gate_up': _L0_ffn_in['W_gate_up'], 'L0_ffn_W_down': _L0_ffn_in['W_down'], 'L0_ffn_Wsg': _L0_ffn_in['Wsg'], 'L0_ffn_Wsu': _L0_ffn_in['Wsu'], 'L0_ffn_Wsd': _L0_ffn_in['Wsd']}

def reference(x, txt, L0_tok_ln_w, L0_tok_ln_b, L0_tok_W, L0_tok_b, L0_tok_pos_emd, L0_attn_A_log, L0_attn_W_bc, L0_attn_b_bc, L0_attn_W_1, L0_attn_b_1, L0_attn_W_d, L0_attn_b_d, L0_ffn_Wg, L0_ffn_e_bias, L0_ffn_W_gate_up, L0_ffn_W_down, L0_ffn_Wsg, L0_ffn_Wsu, L0_ffn_Wsd):
    import jax
    import jax.numpy as jnp

    def _L0_tok_ref(x, ln_w, ln_b, W, b, pos_emd):
        import jax, jax.numpy as jnp
        import numpy as np
        P1, P2, C = (16, 16, 3)
        EMB = 192
        PATCH_DIM = P1 * P2 * C
        NUM_PATCHES = 196
        EPS = 1e-05

        def _patchify(x):
            B, c, H, Wd = x.shape
            nh, nw = (H // P1, Wd // P2)
            x = x.reshape(B, c, nh, P1, nw, P2)
            x = x.transpose(0, 2, 4, 3, 5, 1)
            return x.reshape(B, nh * nw, P1 * P2 * c)
        p = _patchify(x)
        mu = jnp.mean(p, axis=-1, keepdims=True)
        var = jnp.mean(jnp.square(p - mu), axis=-1, keepdims=True)
        pn = (p - mu) * jax.lax.rsqrt(var + EPS) * ln_w + ln_b
        out = jnp.einsum('bnd,de->bne', pn, W) + b
        return out + pos_emd

    def _L0_attn_ref(x, A_log, W_bc, b_bc, W_1, b_1, W_d, b_d):
        import jax, jax.numpy as jnp
        import numpy as np
        B_SZ, L, D, N = (4, 512, 192, 16)
        b, l, d = x.shape
        n = A_log.shape[1]
        A = -jnp.exp(A_log)
        BandC = x @ W_bc.T + b_bc
        Bm, Cm = (BandC[..., :n], BandC[..., n:])
        s1 = x @ W_1.T + b_1
        delta = jax.nn.softplus(s1 @ W_d.T + b_d)
        deltaA = jnp.exp(jnp.einsum('bld,dn->bldn', delta, A))
        deltaB_u = jnp.einsum('bld,bln,bld->bldn', delta, Bm, x)
        dA_t = jnp.moveaxis(deltaA, 1, 0)
        dBu_t = jnp.moveaxis(deltaB_u, 1, 0)
        C_t = jnp.moveaxis(Cm, 1, 0)

        def step(h, inp):
            dA_i, dBu_i, c_i = inp
            h = dA_i * h + dBu_i
            y = jnp.einsum('bdn,bn->bd', h, c_i)
            return (h, y)
        h0 = jnp.zeros((b, d, n), dtype=x.dtype)
        _, ys = jax.lax.scan(step, h0, (dA_t, dBu_t, C_t))
        return jnp.moveaxis(ys, 0, 1)

    def _L0_ffn_ref(hidden_states, Wg, e_bias, W_gate_up, W_down, Wsg, Wsu, Wsd):
        import jax, jax.numpy as jnp
        import numpy as np
        E = 128
        I = 464
        IS = 928
        K = 6
        G = 1
        TG = 1
        SCALE = 2.5
        CAP = 192

        def moe_forward(hidden_states, Wg, e_bias, W_gate_up, W_down, Wsg, Wsu, Wsd):
            B, S, H = hidden_states.shape
            x = hidden_states.reshape(-1, H)
            T = x.shape[0]
            logits = x.astype(jnp.float32) @ Wg.T
            sig = jax.nn.sigmoid(logits)
            choice = sig + e_bias[None, :]
            grp = choice.reshape(T, G, E // G)
            group_scores = jax.lax.top_k(grp, 2)[0].sum(-1)
            gidx = jax.lax.top_k(group_scores, TG)[1]
            gmask = jnp.zeros((T, G), jnp.float32).at[jnp.arange(T)[:, None], gidx].set(1.0)
            smask = jnp.repeat(gmask, E // G, axis=1)
            scores_for_choice = jnp.where(smask > 0, choice, 0.0)
            topk_idx = jax.lax.top_k(scores_for_choice, K)[1]
            topk_w = jnp.take_along_axis(sig, topk_idx, axis=1)
            topk_w = topk_w / (topk_w.sum(-1, keepdims=True) + 1e-20)
            topk_w = topk_w * SCALE
            P = T * K
            flat_e = topk_idx.reshape(-1)
            order = jnp.argsort(flat_e)
            se = flat_e[order]
            counts = jax.ops.segment_sum(jnp.ones(P, jnp.int32), flat_e, num_segments=E)
            starts = jnp.cumsum(counts) - counts
            pos = jnp.arange(P) - starts[se]
            buf_idx = jnp.where(pos < CAP, se * CAP + pos, E * CAP)
            tok_of_pair = (order // K).astype(jnp.int32)
            w_of_pair = topk_w.reshape(-1)[order]
            token_buf = jnp.zeros((E * CAP,), jnp.int32).at[buf_idx].set(tok_of_pair, mode='drop')
            w_buf = jnp.zeros((E * CAP,), x.dtype).at[buf_idx].set(w_of_pair.astype(x.dtype), mode='drop')
            xb = x[token_buf].reshape(E, CAP, H)
            gu = jnp.einsum('ech,ehf->ecf', xb, W_gate_up)
            g, u = jnp.split(gu, 2, axis=-1)
            inter = jax.nn.silu(g) * u
            yb = jnp.einsum('eci,eih->ech', inter, W_down)
            yb = yb * w_buf.reshape(E, CAP, 1)
            routed = jnp.zeros((T, H), x.dtype).at[token_buf].add(yb.reshape(E * CAP, H))
            shared = jax.nn.silu(x @ Wsg) * (x @ Wsu) @ Wsd
            return (routed + shared).reshape(B, S, H)
        return moe_forward(hidden_states, Wg, e_bias, W_gate_up, W_down, Wsg, Wsu, Wsd)
    h = _L0_tok_ref(x, L0_tok_ln_w, L0_tok_ln_b, L0_tok_W, L0_tok_b, L0_tok_pos_emd)
    h = jnp.concatenate([h, txt], axis=1)
    h = h + _L0_attn_ref(_layernorm(h, axis=-1), L0_attn_A_log, L0_attn_W_bc, L0_attn_b_bc, L0_attn_W_1, L0_attn_b_1, L0_attn_W_d, L0_attn_b_d)
    h = h + _L0_ffn_ref(_layernorm(h, axis=-1), L0_ffn_Wg, L0_ffn_e_bias, L0_ffn_W_gate_up, L0_ffn_W_down, L0_ffn_Wsg, L0_ffn_Wsu, L0_ffn_Wsd)
    return h

_drawn_inputs = setup_inputs


def setup_inputs(seed=0):
    import zlib

    import numpy as np

    out = dict(_drawn_inputs(seed))
    spreads = {'L0_tok_ln_w': (1.0, 0.2),
     'L0_tok_ln_b': (0.0, 0.1),
     'L0_attn_b_bc': (0.0, 0.1),
     'L0_attn_b_d': (0.0, 0.1),
     'L0_ffn_e_bias': (0.0, 0.8)}
    factors = {'L0_ffn_Wg': 8.0,
     'L0_ffn_W_gate_up': 8.0,
     'L0_ffn_W_down': 8.0,
     'L0_ffn_Wsg': 8.0,
     'L0_ffn_Wsu': 8.0,
     'L0_ffn_Wsd': 8.0}
    for name, (base, spread) in spreads.items():
        noise = np.random.default_rng([zlib.crc32(name.encode()), seed]).standard_normal(out[name].shape)
        drawn = base * np.exp(spread * noise) if base else spread * noise
        out[name] = jnp.asarray(drawn.astype(out[name].dtype))
    for name, factor in factors.items():
        out[name] = (out[name] * factor).astype(out[name].dtype)
    return out
```

```python
from contextlib import ExitStack

import concourse.bass as bass
from concourse import mybir

F32 = mybir.dt.float32
BF16 = mybir.dt.bfloat16
U32 = mybir.dt.uint32
ALU = mybir.AluOpType
ACT = mybir.ActivationFunctionType
AX = mybir.AxisListType

B, L, D, N = 64, 324, 192, 16
IMG, TXT = 196, 128
PATCH, PC = 768, 6
ROWS = (98, 98, 128)
OFF = (0, 98, 196)
PAIRS = B // 2
T_ALL = B * L
LO, HI = 128, D - 128
E, CAP, TOPK = 128, 192, 6
HID, HC = 464, 116
NF = HID // HC
SHID = 928
NJ = SHID // HC
HALF = CAP // 2
SCALE = 2.5
EPS = 1e-5
BIG = 3.0e38
XW = D + 2


class Turn:

    def __init__(self, v, p, h):
        self.v, self.p, self.h = v, p, h

    @classmethod
    def fixed(cls, n):
        return cls(n, n % 2, n // 2)

    def plus(self, k):
        return Turn(self.v + k, (self.p + k) % 2, self.h + (self.p + k) // 2)


def wait(eng, sem, value):
    if not (isinstance(value, int) and value <= 0):
        eng.wait_ge(sem, value)


def schedule():
    ups = [[] for _ in range(N)]
    for e in range(2 * NJ):
        ups[4 + e * 12 // (2 * NJ)].append(("up_g" if e % 2 == 0 else "up_u", 2, e // 2))
    slot_a = {
        0: [("down", 3, 0)], 1: [("down", 3, 1)], 2: [("down", 3, 2), ("store_out", 3, 0)],
        3: [("resid", 1, 0)], 4: [("resid", 1, 1)], 5: [("resid", 1, 2), ("load_txt", -1, 0), ("ln2_center", 1, 0)],
        6: [("ln2_var", 1, 0)], 7: [("ln2_scale", 1, 0)],
        8: [("x2_turn", 1, 0)], 9: [("x2_turn", 1, 1)], 10: [("x2_turn", 1, 2)],
        11: [("gate", 1, 0), ("gate", 1, 1)], 12: [("choose", 1, 0)], 13: [("weigh", 1, 0)],
        14: [("count", 1, 0)], 15: [("store_mid", 1, 0)],
    }
    slot_b = {
        2: [("emb", -1, 0)], 3: [("emb", -1, 1)], 4: [("emb_stats", -1, 0), ("load_x", -2, 0)], 5: [("emb_scale", -1, 0)],
        6: [("ln1_center", -1, 0)], 7: [("ln1_var", -1, 0)], 8: [("ln1_scale", -1, 0)],
        9: [("x1_turn", -1, 0)], 10: [("x1_turn", -1, 1)], 11: [("x1_turn", -1, 2)],
        12: [("bc_values", -1, 0), ("step_size", -1, 0)], 13: [("step_size", -1, 1), ("step_size", -1, 2)],
        14: [("softplus", -1, 0)],
    }
    out = []
    for n in range(N):
        if n + 1 < N:
            out.append(("decay", 0, n + 1))
        out.append(("scan", 0, n))
        if n + 2 < N:
            out.append(("fill_b", 0, n + 2))
        out += slot_a.get(n, [])
        out.append(("fill_c", 0, n))
        out += slot_b.get(n, []) + ups[n]
    return out + [("decay", -1, 0), ("fill_b", -1, 0), ("fill_b", -1, 1)]


SCHEDULE = schedule()
MISC = {"down", "resid", "x2_turn", "gate", "count", "emb", "x1_turn", "bc_values", "step_size"}
FIRST_BODY, LOOP_FROM, LOOP_TO, LAST_BODY = -2, 3, 29, PAIRS + 2


def pieces(i):
    return [x for x in SCHEDULE if 0 <= i - x[1] < PAIRS]


def shared_bank_uses(i):
    return sum(k in MISC for k, _, _ in pieces(i))


def run_bodies(eng, body):
    uses = 0
    for i in range(FIRST_BODY, LOOP_FROM):
        body(Turn.fixed(i), pieces(i), uses)
        uses += shared_bank_uses(i)
    steady = shared_bank_uses(LOOP_FROM)
    with eng.Fori(0, (LOOP_TO - LOOP_FROM) // 2) as r:
        for q in range(2):
            start = Turn.fixed(LOOP_FROM + q)
            body(Turn(start.v + 2 * r, start.p, start.h + r), pieces(LOOP_FROM), uses + q * steady + 2 * steady * r)
    uses += steady * (LOOP_TO - LOOP_FROM)
    for i in range(LOOP_TO, LAST_BODY + 1):
        body(Turn.fixed(i), pieces(i), uses)
        uses += shared_bank_uses(i)



def build(nc, a, out):
    dram_x = nc.dram_tensor("token_rows", (T_ALL + CAP, XW), F32).ap()
    dram_cnt = nc.dram_tensor("running_counts", (E * B, L), F32).ap()
    with ExitStack() as outer:
        ident = outer.enter_context(nc.sbuf_tensor("ident", [128, 128], F32))
        block_end = outer.enter_context(nc.sbuf_tensor("block_end", [E, B], F32))
        with ExitStack() as ctx:
            phase1(nc, ctx, a, out, dram_x, dram_cnt, ident, block_end)
        with ExitStack() as ctx:
            phase2(nc, ctx, a, out, dram_x, dram_cnt, ident, block_end)


class Buffers:

    def __init__(self, nc, ctx, ident, block_end):
        sb = lambda name, shape, dt=F32: ctx.enter_context(nc.sbuf_tensor(name, shape, dt))
        self.ident, self.block_end = ident, block_end
        self.ident_bf = sb("ident_bf", [128, 128], BF16)
        self.ones = sb("ones", [128, 128])
        self.zeros = sb("zeros", [128, 2 * L])
        self.w_tok = sb("w_tok", [128, PC, D + 2])
        self.pos = sb("pos", [ROWS[0], 2, D])
        self.a_neg = sb("a_neg", [128, 2, N])
        self.wbc = sb("wbc", [128, 3, 64])
        self.bc_bias = sb("bc_bias", [32, 2])
        self.w1 = sb("w1", [128, 6, 128])
        self.wd = sb("wd", [128, 2])
        self.bd = sb("bd", [128, 2])
        self.pick = sb("pick", [96, 32], BF16)
        self.wg = sb("wg", [128, 3, E])
        self.e_bias = sb("e_bias", [128, E])
        self.ws_g = sb("ws_g", [128, 3, SHID])
        self.ws_u = sb("ws_u", [128, 3, SHID])
        self.ws_d = sb("ws_d", [HC, NJ, D])
        two = lambda name, shape, dt=F32, n=2: [sb(f"{name}{p}", shape, dt) for p in range(n)]
        self.x_in = sb("x_in", [128, 2, PC, IMG])
        self.x_sq = sb("x_sq", [128, PC, IMG])
        self.emb = sb("emb", [ROWS[0], 2, 2, 196])
        self.h = two("h", [128, 2, 3, D])
        self.h2 = two("h2_", [128, 2, 3, D])
        self.xn = sb("xn", [128, 2, 3, D])
        self.xm = two("xm", [128, 3, 2, HI])
        self.x2 = sb("x2", [128, 2, 3, XW])
        self.ln_sq = sb("ln_sq", [128, 2, 3, D])
        self.xf = sb("xf", [128, 3, L])
        self.x2f = two("x2f", [128, 3, L])
        self.delta = two("delta", [128, 3, L])
        self.du = two("du", [128, 3, L])
        self.soft = sb("soft", [128, 3, L])
        self.bcv = sb("bcv", [32, 2, L])
        self.mid_part = sb("mid_part", [32, 2, L], BF16)
        self.parts = two("parts", [96, 2, L], BF16)
        self.decay = two("decay", [128, 3, L])
        self.b_wide = two("b_wide", [128, 3, L])
        self.state = two("state", [128, 3, L], n=4)
        self.y = two("y", [128, 3, L])
        self.th = sb("th", [HC, 2, L])
        self.ag = sb("ag", [HC, 2, L])
        self.inter = sb("inter", [HC, NJ, 2, L])
        self.gt = sb("gt", [128, 6, E])
        self.ch = sb("ch", [128, 6, E])
        self.mask = sb("mask", [128, 6, E], BF16)
        self.top8 = sb("top8", [128, 6, 8])
        self.stat = sb("stat", [128, 3, 6, 6])
        self.cnt = sb("cnt", [E, 2 * L])
        self.run = sb("run", [E, 1])
        self.ps = ctx.enter_context(nc.psum_tensor("ps", [128, 8, 512], F32))


def prepare(nc, ctx, a, out, dram_x, b):
    sem = lambda name: ctx.enter_context(nc.semaphore(name))
    filled, made, loaded, prepared = sem("filled"), sem("made"), sem("loaded"), sem("prepared")
    mean_full, bias_full, a_exp, padded = sem("mean_full"), sem("bias_full"), sem("a_exp"), sem("padded")
    with ExitStack() as tmp:
        sb = lambda name, shape, dt=F32: tmp.enter_context(nc.sbuf_tensor(name, shape, dt))
        w_raw = b.x_in[:].rearrange("p b c t -> p (b c t)")[:, 0:PC * D].rearrange("p (c d) -> p c d", c=PC)
        small = b.x_sq[:].rearrange("p c t -> p (c t)")
        ln_w, ln_b, w1c = small[:, 0:PC], small[:, PC:2 * PC], small[:, 12:14]
        b1 = small[:, 14:15]
        b_tok = b.ln_sq[0:ROWS[0], 0, 0, :]
        mean_w = b.soft[:, 0, 0:128]
        zero_tiles = [b.ident, b.ident_bf, b.pick, b.wbc, b.w1, b.wg, b.ws_g, b.ws_u, b.zeros, b.gt, b.x2, b.run, b.stat,
                      b.xn, *b.xm, b.ln_sq, b.x_in, b.x_sq, *b.h, *b.h2, *b.decay]
        loads = [
            (w_raw, a["w_tok"]), (ln_w, a["ln_w"]), (ln_b, a["ln_b"]), (b_tok, a["b_tok"].broadcast_to([ROWS[0], D])),
            (b.pos[:], a["pos"]), (b.a_neg[:, 0, :], a["a_log"][0:LO]),
            (b1, a["b_1"].broadcast_to([128, 1])),
            (w1c[:, 0:1], a["w_1"][0:LO]), (b.wd[:, 0:1], a["w_d"][0:LO]), (b.bd[:, 0:1], a["b_d"][0:LO]),
            (b.e_bias[:], a["e_bias"].broadcast_to([128, E])), (b.ws_d[:], a["ws_d"]),
            (b.wg[:, 0, :], a["wg_t"][0:LO]), (b.ws_g[:, 0, :], a["ws_g"][0:LO]), (b.ws_u[:, 0, :], a["ws_u"][0:LO]),
        ]
        for half in range(2):
            at = slice(HI * half, HI * half + HI)
            loads += [
                (b.a_neg[at, 1, :], a["a_log"][LO:D]), (w1c[at, 1:2], a["w_1"][LO:D]),
                (b.wd[at, 1:2], a["w_d"][LO:D]), (b.bd[at, 1:2], a["b_d"][LO:D]),
                (b.wg[at, 1 + half, :], a["wg_t"][LO:D]), (b.ws_g[at, 1 + half, :], a["ws_g"][LO:D]),
                (b.ws_u[at, 1 + half, :], a["ws_u"][LO:D]),
            ]
            for c in range(2):
                col = slice(32 * c + 16 * half, 32 * c + 16 * half + 16)
                loads += [
                    (b.wbc[:, half, col], a["w_bc_t"][0:LO, 16 * c:16 * c + 16]),
                    (b.wbc[at, 2, col], a["w_bc_t"][LO:D, 16 * c:16 * c + 16]),
                    (b.bc_bias[16 * half:16 * half + 16, c:c + 1], a["b_bc"][16 * c:16 * c + 16]),
                ]
        with nc.Block() as block:

            @block.gpsimd
            def _(pool):
                pool.wait_ge(filled, len(zero_tiles))
                for tile in (b.ident, b.ident_bf):
                    nc.gpsimd.affine_select(out=tile[:], in_=tile[:], compare_op=ALU.not_equal, fill=1.0, base=0,
                                            pattern=[[-1, 128]], channel_multiplier=1).then_inc(made, 1)
                for part in range(3):
                    pool.wait_ge(made, 2 + part)
                    rows = b.pick[32 * part:32 * part + 32, :]
                    nc.gpsimd.affine_select(out=rows, in_=rows, compare_op=ALU.not_equal, fill=1.0, base=0,
                                            pattern=[[-1, 32]], channel_multiplier=1).then_inc(made, 1)
                pool.wait_ge(made, 5)

            @block.sync
            def _(sp):
                sp.wait_ge(filled, len(zero_tiles))
                for to, source in loads:
                    sp.dma_start(to, source).then_inc(loaded, 16)
                for k in range(2):
                    rows = slice(T_ALL + HALF * k, T_ALL + HALF * k + HALF)
                    sp.dma_start(dram_x[rows], b.zeros[0:HALF, 0:XW]).then_inc(padded, 16)
                    sp.dma_start(out[rows], b.zeros[0:HALF, 0:D]).then_inc(padded, 16)
                sp.wait_ge(padded, 64)

            @block.vector
            def _(dve):
                done = [0]

                def step(ins):
                    done[0] += 1
                    ins.then_inc(prepared, 1)
                    dve.wait_ge(prepared, done[0])

                for tile in zero_tiles:
                    nc.vector.memset(tile[:], 0.0).then_inc(filled, 1)
                step(nc.vector.memset(b.ones[:], 1.0))
                step(nc.vector.memset(mean_w, 1.0 / PATCH))
                step(nc.vector.memset(b.w_tok[:, :, D:D + 2], 1.0))
                dve.wait_ge(loaded, 16 * len(loads))
                for c in range(PC):
                    step(nc.vector.tensor_scalar(b.w_tok[:, c, 0:D], w_raw[:, c, :], ln_w[:, c:c + 1], None, ALU.mult))
                for c in range(PC):
                    step(nc.vector.tensor_scalar(b.xf[:].rearrange("p a b -> p (a b)")[:, 128 * c:128 * c + 128],
                                                 b.ones[:], ln_b[:, c:c + 1], None, ALU.mult))
                dve.wait_ge(mean_full, 1)
                step(nc.vector.tensor_tensor(b.w_tok[:, :, 0:D], b.w_tok[:, :, 0:D],
                                             b.ps[:, 0, 0:D].unsqueeze(1).broadcast_to([128, PC, D]), ALU.subtract))
                dve.wait_ge(bias_full, 1)
                for k in range(2):
                    step(nc.vector.tensor_tensor(b.pos[:, k, :], b.pos[:, k, :], b.ps[0:ROWS[0], 1, 0:D], ALU.add))
                    step(nc.vector.tensor_tensor(b.pos[:, k, :], b.pos[:, k, :], b_tok, ALU.add))
                dve.wait_ge(a_exp, 1)
                step(nc.vector.tensor_scalar(b.a_neg[:], b.a_neg[:], -1.0, None, ALU.mult))
                step(nc.vector.scalar_tensor_tensor(b.bd[:], b.wd[:], b1, b.bd[:], ALU.mult, ALU.add))
                step(nc.vector.tensor_scalar(b.ws_d[:], b.ws_d[:], 0.5, None, ALU.mult))
                low, high = slice(0, HI), slice(HI, 128)
                for k, rows, cols, col in ((0, slice(0, 128), slice(0, 128), 0), (1, slice(0, 128), low, 0), (2, slice(0, 128), high, 0),
                                           (3, low, slice(0, 128), 1), (4, high, slice(0, 128), 1), (5, low, low, 1), (5, high, high, 1)):
                    step(nc.vector.tensor_scalar(b.w1[rows, k, cols], b.ones[rows, cols], w1c[rows, col:col + 1], None, ALU.mult))

            @block.scalar
            def _(act):
                act.wait_ge(loaded, 16 * len(loads))
                nc.scalar.activation(b.a_neg[:], b.a_neg[:], ACT.Exp).then_inc(a_exp, 1)

            @block.tensor
            def _(pe):
                pe.wait_ge(prepared, 3 + PC)
                for c in range(PC):
                    mm = nc.tensor.matmul(b.ps[:, 0, 0:D], mean_w, b.w_tok[:, c, 0:D], start=(c == 0), stop=(c == PC - 1))
                mm.then_inc(mean_full, 1)
                pe.wait_ge(prepared, 3 + 2 * PC)
                for c in range(PC):
                    wide = b.xf[:].rearrange("p a b -> p (a b)")[:, 128 * c:128 * c + ROWS[0]]
                    mm = nc.tensor.matmul(b.ps[0:ROWS[0], 1, 0:D], wide, w_raw[:, c, :], start=(c == 0), stop=(c == PC - 1))
                mm.then_inc(bias_full, 1)


def phase1(nc, ctx, a, out, dram_x, dram_cnt, ident, block_end):
    b = Buffers(nc, ctx, ident, block_end)
    prepare(nc, ctx, a, out, dram_x, b)
    sem = lambda name: ctx.enter_context(nc.semaphore(name))
    ps, stat = b.ps, b.stat
    wide = ps[:, 0:3, 0:L]
    g_ps, u_ps = ps[0:HC, 3:5, 0:L], ps[0:HC, 5:7, 0:L]
    misc = ps[:, 7, :]

    x_loaded, sq_ready, sq_used = sem("x_loaded"), sem("sq_ready"), sem("sq_used")
    txt_loaded = [sem(f"txt_loaded{p}") for p in range(2)]
    misc_full, misc_free = sem("misc_full"), sem("misc_free")
    emb_var, emb_log, emb_r0, emb_done = sem("emb_var"), sem("emb_log"), sem("emb_r0"), sem("emb_done")
    ln_centered = [sem(f"ln{k}_centered") for k in (1, 2)]
    ln_squared = [sem(f"ln{k}_squared") for k in (1, 2)]
    ln_var = [sem(f"ln{k}_var") for k in (1, 2)]
    ln_log = [sem(f"ln{k}_log") for k in (1, 2)]
    ln_r0 = [sem(f"ln{k}_r0") for k in (1, 2)]
    ln_done = [sem(f"ln{k}_done") for k in (1, 2)]
    parts_ready = sem("parts_ready")
    soft_abs, soft_exp, soft_ready, du_ready = sem("soft_abs"), sem("soft_exp"), sem("soft_ready"), sem("du_ready")
    decay_ready, scan_done = sem("decay_ready"), sem("scan_done")
    b_full, b_copied, input_ready = sem("b_full"), sem("b_copied"), sem("input_ready")
    c_full, c_used, y_added = sem("c_full"), sem("c_used"), sem("y_added")
    resid_done = sem("resid_done")
    mask_ready, factor_ready, cnt_ready = sem("mask_ready"), sem("factor_ready"), sem("cnt_ready")
    g_full, th_ready, g_used = sem("g_full"), sem("th_ready"), sem("g_used")
    u_full, inter_ready, out_ready = sem("u_full"), sem("inter_ready"), sem("out_ready")
    out_stored = [sem(f"out_stored{p}") for p in range(2)]
    rows_stored, cnt_stored = sem("rows_stored"), sem("cnt_stored")
    waited = sem("waited")
    LINKS = {"emb": 7, "ln1": 7, "ln2": 7, "bc": 4, "soft": 1, "choose": 5, "weigh": 4}
    chains = {k: sem(f"chain_{k}") for k in LINKS}

    class Chain:

        def __init__(self, eng, name, t, start=0):
            self.eng, self.sem, self.base, self.n = eng, chains[name], LINKS[name] * t.v, start

        def __call__(self, ins, alone=False):
            self.n += 1
            ins.then_inc(self.sem, 1)
            self.eng.wait_ge(self.sem, self.base + self.n)
            if alone:
                self.eng.sem_inc(waited, 1)

    def token_rows(dram, t, k):
        return dram[bass.ds(t.v * (2 * L), 2 * L)].rearrange("(b r) d -> r b d", b=2)[OFF[k]:OFF[k] + ROWS[k]]

    with nc.Block() as block:

        @block.sync
        def _(sp):
            def body(i, todo, uses):
                for kind, lag, k in todo:
                    t = i.plus(-lag)
                    if kind == "load_x":
                        wait(sp, emb_var, t.v)
                        sp.dma_start(b.x_in[:], a["x"][bass.ds(t.v * 2, 2)].rearrange("b p c t -> p b c t")).then_inc(x_loaded, 16)
                    elif kind == "load_txt":
                        wait(sp, resid_done, t.v - 1)
                        sp.dma_start(b.h[t.p][:, :, 2, :], a["txt"][bass.ds(t.v * 2, 2)].rearrange("b r d -> r b d")).then_inc(txt_loaded[t.p], 16)
                    elif kind == "store_out":
                        sp.wait_ge(out_ready, t.v + 1)
                        for c in range(3):
                            sp.dma_start(token_rows(out, t, c), b.h2[t.p][0:ROWS[c], :, c, :]).then_inc(out_stored[t.p], 16)
                    elif kind == "store_mid":
                        sp.wait_ge(factor_ready, t.v + 1)
                        for c in range(3):
                            sp.dma_start(token_rows(dram_x, t, c), b.x2[0:ROWS[c], :, c, :]).then_inc(rows_stored, 16)
                        sp.wait_ge(cnt_ready, t.v + 1)
                        sp.dma_start(dram_cnt.rearrange("(e b) l -> e b l", e=E)[:, bass.ds(t.v * 2, 2), :],
                                     b.cnt[:].rearrange("e (b l) -> e b l", b=2)).then_inc(cnt_stored, 16)

            run_bodies(sp, body)
            for p in range(2):
                sp.wait_ge(out_stored[p], 48 * PAIRS // 2)
            sp.wait_ge(rows_stored, 48 * PAIRS)
            sp.wait_ge(cnt_stored, 16 * PAIRS)

        @block.gpsimd
        def _(pool):
            def body(i, todo, uses):
                for kind, lag, n in todo:
                    t = i.plus(-lag)
                    if kind == "fill_b":
                        if n == 0:
                            pool.wait_ge(du_ready, t.v + 1)
                        pool.wait_ge(b_copied, N * t.v + n + 1)
                        wait(pool, y_added, 15 * t.v + (max(n - 4, 1) if n >= 4 else n - 3))
                        nc.gpsimd.tensor_tensor(b.state[n % 4][:], b.du[t.p][:], b.b_wide[n % 2][:], ALU.mult).then_inc(input_ready, 1)
                    elif kind == "fill_c" and n > 0:
                        pool.wait_ge(c_used, N * t.v + n + 1)
                        y = b.y[t.p][:]
                        if n == 1:
                            wait(pool, resid_done, t.v - 1)
                            nc.gpsimd.tensor_tensor(y, b.state[0][:], b.state[1][:], ALU.add).then_inc(y_added, 1)
                        else:
                            pool.wait_ge(y_added, 15 * t.v + n - 1)
                            nc.gpsimd.tensor_tensor(y, y, b.state[n % 4][:], ALU.add).then_inc(y_added, 1)

            run_bodies(pool, body)

        @block.scalar
        def _(act):
            def rsqrt_guess(m, rows, cols, var_sem, log_sem, out_sem, t):
                act.wait_ge(var_sem, t.v + 1)
                nc.scalar.activation(stat[0:rows, m, 5, 0:cols], stat[0:rows, m, 4, 0:cols], ACT.Ln).then_inc(log_sem, 1)
                act.wait_ge(log_sem, t.v + 1)
                nc.scalar.activation(stat[0:rows, m, 5, 0:cols], stat[0:rows, m, 5, 0:cols], ACT.Exp, scale=-0.5).then_inc(out_sem, 1)

            def body(i, todo, uses):
                for kind, lag, k in todo:
                    t = i.plus(-lag)
                    if kind in MISC:
                        uses = uses + 1
                    if kind == "decay":
                        if k == 0:
                            act.wait_ge(du_ready, t.v + 1)
                        wait(act, scan_done, N * t.v + k - 1)
                        to = b.decay[k % 2]
                        nc.scalar.activation(to[:, 0:2, 1:L], b.delta[t.p][:, 0:2, 1:L], ACT.Exp, scale=b.a_neg[:, 0, k:k + 1])
                        nc.scalar.activation(to[:, 2, 1:L], b.delta[t.p][:, 2, 1:L], ACT.Exp, scale=b.a_neg[:, 1, k:k + 1]).then_inc(decay_ready, 1)
                    elif kind == "fill_b":
                        act.wait_ge(b_full, N * t.v + k + 1)
                        wait(act, input_ready, N * t.v + k - 1)
                        nc.scalar.activation(b.b_wide[k % 2][:], wide, ACT.Copy).then_inc(b_copied, 1)
                    elif kind == "emb":
                        act.wait_ge(x_loaded, 16 * t.v + 16)
                        wait(act, sq_used, 2 * t.v + k)
                        nc.scalar.activation(b.x_sq[:], b.x_in[:, k], ACT.Square).then_inc(sq_ready, 1)
                        act.wait_ge(misc_full, uses)
                        if k == 0:
                            wait(act, emb_done, t.v)
                        nc.scalar.activation(b.emb[:, k].rearrange("p a b -> p (a b)"), misc[0:ROWS[0], 0:392], ACT.Copy).then_inc(misc_free, 1)
                    elif kind == "emb_stats":
                        rsqrt_guess(0, ROWS[0], 4, emb_var, emb_log, emb_r0, t)
                    elif kind in ("ln1_center", "ln2_center"):
                        m = int(kind[2]) - 1
                        act.wait_ge(ln_centered[m], t.v + 1)
                        if m == 0:
                            wait(act, ln_var[1], t.v - 1)
                        else:
                            wait(act, ln_var[0], min(t.v + 2, PAIRS) if isinstance(t.v, int) else t.v + 2)
                        centered = b.xn[:] if m == 0 else b.x2[:, :, :, 0:D]
                        nc.scalar.activation(b.ln_sq[:], centered, ACT.Square).then_inc(ln_squared[m], 1)
                    elif kind in ("ln1_var", "ln2_var"):
                        m = int(kind[2]) - 1
                        rsqrt_guess(m + 1, 128, 6, ln_var[m], ln_log[m], ln_r0[m], t)
                    elif kind == "x1_turn":
                        act.wait_ge(misc_full, uses)
                        if k == 0:
                            wait(act, du_ready, t.v)
                        nc.scalar.activation(b.xf[:, k, :], misc[:, 0:L], ACT.Copy).then_inc(misc_free, 1)
                    elif kind == "x2_turn":
                        act.wait_ge(misc_full, uses)
                        if k == 0:
                            wait(act, u_full, NJ * (t.v - 1))
                        nc.scalar.activation(b.x2f[t.p][:, k, :], misc[:, 0:L], ACT.Copy).then_inc(misc_free, 1)
                    elif kind == "bc_values":
                        act.wait_ge(misc_full, uses)
                        wait(act, parts_ready, t.v)
                        nc.scalar.activation(b.bcv[:, 0, :], misc[0:32, 0:L], ACT.Identity, bias=b.bc_bias[:, 0:1])
                        nc.scalar.activation(b.bcv[:, 1, :], misc[32:64, 0:L], ACT.Identity, bias=b.bc_bias[:, 1:2]).then_inc(misc_free, 1)
                    elif kind == "step_size":
                        col = 1 if k == 2 else 0
                        act.wait_ge(misc_full, uses)
                        if k == 0:
                            wait(act, du_ready, t.v)
                            wait(act, decay_ready, N * (t.v - 1))
                        scale, bias = b.wd[:, col:col + 1], b.bd[:, col:col + 1]
                        nc.scalar.activation(b.soft[:, k, :], misc[:, 0:L], ACT.Abs, scale=scale, bias=bias).then_inc(soft_abs, 1)
                        nc.scalar.activation(b.delta[t.p][:, k, :], misc[:, 0:L], ACT.Relu, scale=scale, bias=bias).then_inc(misc_free, 1)
                    elif kind == "softplus":
                        act.wait_ge(soft_abs, 3 * t.v + 3)
                        nc.scalar.activation(b.soft[:], b.soft[:], ACT.Exp, scale=-1.0).then_inc(soft_exp, 1)
                        act.wait_ge(soft_exp, t.v + 1)
                        nc.scalar.activation(b.soft[:], b.soft[:], ACT.Ln, bias=1.0).then_inc(soft_ready, 1)
                    elif kind == "gate":
                        act.wait_ge(misc_full, uses)
                        if k == 0:
                            wait(act, factor_ready, t.v)
                        nc.scalar.activation(b.gt[0:98, 3 * k:3 * k + 2, :], misc[0:98, 0:256].rearrange("p (k e) -> p k e", k=2), ACT.Tanh, scale=0.5)
                        nc.scalar.activation(b.gt[:, 3 * k + 2, :], misc[:, 256:384], ACT.Tanh, scale=0.5).then_inc(misc_free, 1)
                    elif kind == "up_g":
                        act.wait_ge(g_full, NJ * t.v + k + 1)
                        wait(act, g_used, NJ * t.v + k)
                        nc.scalar.activation(b.th[:], g_ps, ACT.Tanh, scale=0.5).then_inc(th_ready, 1)

            run_bodies(act, body)

        @block.vector
        def _(dve):
            def newton(m, rows, cols, link):
                s = stat[0:rows, m, :, 0:cols]
                link(nc.vector.tensor_tensor(s[:, 0, :], s[:, 5, :], s[:, 5, :], ALU.mult))
                link(nc.vector.scalar_tensor_tensor(s[:, 1, :], s[:, 0, :], -0.5, s[:, 4, :], ALU.mult, ALU.mult))
                link(nc.vector.scalar_tensor_tensor(s[:, 3, :], s[:, 1, :], 1.5, s[:, 5, :], ALU.add, ALU.mult))
                return s[:, 3, :]

            def body(i, todo, uses):
                for kind, lag, k in todo:
                    t = i.plus(-lag)
                    if kind in MISC:
                        uses = uses + 1
                    if kind == "scan":
                        dve.wait_ge(decay_ready, N * t.v + k + 1)
                        dve.wait_ge(input_ready, N * t.v + k + 1)
                        s = b.state[k % 4][:].rearrange("p a t -> p (a t)")
                        nc.vector.tensor_tensor_scan(s, b.decay[k % 2][:].rearrange("p a t -> p (a t)"), s, 0.0,
                                                     ALU.mult, ALU.add).then_inc(scan_done, 1)
                    elif kind == "fill_c":
                        dve.wait_ge(c_full, N * t.v + k + 1)
                        dve.wait_ge(scan_done, N * t.v + k + 1)
                        nc.vector.tensor_tensor(b.state[k % 4][:], b.state[k % 4][:], wide, ALU.mult).then_inc(c_used, 1)
                    elif kind == "down":
                        dve.wait_ge(misc_full, uses)
                        r, to = ROWS[k], b.h2[t.p]
                        ins = nc.vector.tensor_tensor(to[0:r, :, k, :], to[0:r, :, k, :], misc[0:r, 0:2 * D].rearrange("p (b d) -> p b d", b=2), ALU.add)
                        ins.then_inc(misc_free, 1)
                        if k == 2:
                            dve.wait_ge(misc_free, uses)
                            nc.vector.memset(stat[0:1, 0, 2, 4:5], 0.0).then_inc(out_ready, 1)
                    elif kind == "resid":
                        dve.wait_ge(misc_full, uses)
                        if k == 0:
                            wait(dve, out_stored[t.p], 48 * t.h)
                        r = ROWS[k]
                        nc.vector.tensor_tensor(b.h2[t.p][0:r, :, k, 0:LO], b.h[t.p][0:r, :, k, 0:LO],
                                                misc[0:r, 0:2 * LO].rearrange("p (b d) -> p b d", b=2), ALU.add)
                        nc.vector.tensor_tensor(b.h2[t.p][0:r, :, k, LO:D], b.h[t.p][0:r, :, k, LO:D],
                                                misc[0:r, 2 * LO:2 * LO + 2 * HI].rearrange("p (b d) -> p b d", b=2), ALU.add).then_inc(misc_free, 1)
                        if k == 2:
                            dve.wait_ge(misc_free, uses)
                            nc.vector.memset(stat[0:1, 0, 2, 5:6], 0.0).then_inc(resid_done, 1)
                    elif kind == "emb_stats":
                        dve.wait_ge(misc_free, uses)
                        link = Chain(dve, "emb", t)
                        col = lambda c: b.emb[:, :, :, c:c + 1].rearrange("p b k c -> p (b k) c")[:, :, 0]
                        s = stat[0:ROWS[0], 0, :, 0:4]
                        link(nc.vector.tensor_scalar(s[:, 0, :], col(D), 1.0 / PATCH, None, ALU.mult))
                        link(nc.vector.tensor_tensor(s[:, 1, :], s[:, 0, :], s[:, 0, :], ALU.mult))
                        link(nc.vector.scalar_tensor_tensor(s[:, 2, :], col(D + 2), 1.0 / PATCH, s[:, 1, :], ALU.mult, ALU.subtract))
                        nc.vector.tensor_scalar(s[:, 4, :], s[:, 2, :], 0.0, EPS, ALU.max, ALU.add).then_inc(emb_var, 1)
                    elif kind == "emb_scale":
                        dve.wait_ge(emb_r0, t.v + 1)
                        wait(dve, resid_done, t.v - 1)
                        link = Chain(dve, "emb", t, 3)
                        r = newton(0, ROWS[0], 4, link).rearrange("p (b k) -> p b k", b=2).unsqueeze(3).broadcast_to([ROWS[0], 2, 2, D])
                        to = b.h[t.p][0:ROWS[0], :, 0:2, :]
                        link(nc.vector.tensor_tensor(to, b.emb[:, :, :, 0:D], r, ALU.mult))
                        nc.vector.tensor_tensor(to, to, b.pos[:].unsqueeze(1).broadcast_to([ROWS[0], 2, 2, D]), ALU.add).then_inc(emb_done, 1)
                    elif kind in ("ln1_center", "ln2_center"):
                        m = int(kind[2]) - 1
                        if m == 0:
                            dve.wait_ge(emb_done, t.v + 1)
                            dve.wait_ge(txt_loaded[t.p], 16 * t.h + 16)
                            wait(dve, du_ready, t.v)
                            source, to = b.h[t.p][:], b.xn[:]
                        else:
                            dve.wait_ge(resid_done, t.v + 1)
                            wait(dve, cnt_ready, t.v)
                            wait(dve, rows_stored, 48 * t.v)
                            source, to = b.h2[t.p][:], b.x2[:, :, :, 0:D]
                        link = Chain(dve, kind[:3], t)
                        s = stat[:, m + 1]
                        link(nc.vector.tensor_reduce(s[:, 0, :], source, AX.X, ALU.add))
                        link(nc.vector.tensor_scalar(s[:, 1, :], s[:, 0, :], 1.0 / D, None, ALU.mult))
                        mean = s[:, 1, :].rearrange("p (b k) -> p b k", b=2).unsqueeze(3).broadcast_to([128, 2, 3, D])
                        nc.vector.tensor_tensor(to, source, mean, ALU.subtract).then_inc(ln_centered[m], 1)
                    elif kind in ("ln1_var", "ln2_var"):
                        m = int(kind[2]) - 1
                        dve.wait_ge(ln_squared[m], t.v + 1)
                        s = stat[:, m + 1]
                        link = Chain(dve, kind[:3], t, 2)
                        link(nc.vector.tensor_reduce(s[:, 2, :], b.ln_sq[:], AX.X, ALU.add))
                        nc.vector.tensor_scalar(s[:, 4, :], s[:, 2, :], 1.0 / D, EPS, ALU.mult, ALU.add).then_inc(ln_var[m], 1)
                    elif kind in ("ln1_scale", "ln2_scale"):
                        m = int(kind[2]) - 1
                        dve.wait_ge(ln_r0[m], t.v + 1)
                        link = Chain(dve, kind[:3], t, 3)
                        r = newton(m + 1, 128, 6, link).rearrange("p (b k) -> p b k", b=2)
                        x = b.xn if m == 0 else b.x2
                        link(nc.vector.tensor_tensor(b.xm[m][:].rearrange("p k b d -> p b k d"), x[:, :, :, LO:D], r.unsqueeze(3).broadcast_to([128, 2, 3, HI]), ALU.mult))
                        if m == 0:
                            nc.vector.tensor_tensor(x[:, :, :, 0:LO], x[:, :, :, 0:LO], r.unsqueeze(3).broadcast_to([128, 2, 3, LO]), ALU.mult).then_inc(ln_done[m], 1)
                        else:
                            nc.vector.tensor_tensor(x[:, :, :, 0:D], x[:, :, :, 0:D], r.unsqueeze(3).broadcast_to([128, 2, 3, D]), ALU.mult).then_inc(ln_done[m], 1)
                    elif kind == "bc_values":
                        dve.wait_ge(misc_free, uses)
                        wait(dve, c_full, N * (t.v - 1))
                        p, v = b.parts[t.p], b.bcv[:]
                        link = Chain(dve, "bc", t)
                        link(nc.vector.tensor_copy(p[0:32], v))
                        link(nc.vector.tensor_tensor(v, v, p[0:32], ALU.subtract))
                        link(nc.vector.tensor_copy(b.mid_part[:], v))
                        nc.vector.tensor_copy(p[32:64], b.mid_part[:])
                        link(nc.vector.tensor_tensor(v, v, b.mid_part[:], ALU.subtract))
                        nc.vector.tensor_copy(p[64:96], v).then_inc(parts_ready, 1)
                    elif kind == "softplus":
                        dve.wait_ge(soft_ready, t.v + 1)
                        dve.wait_ge(misc_free, uses)
                        wait(dve, input_ready, N * (t.v - 1))
                        link = Chain(dve, "soft", t)
                        link(nc.vector.tensor_tensor(b.delta[t.p][:], b.delta[t.p][:], b.soft[:], ALU.add))
                        nc.vector.tensor_tensor(b.du[t.p][:], b.delta[t.p][:], b.xf[:], ALU.mult).then_inc(du_ready, 1)
                    elif kind == "choose":
                        dve.wait_ge(misc_free, uses)
                        wait(dve, cnt_ready, t.v)
                        link = Chain(dve, "choose", t)
                        link(nc.vector.tensor_scalar(b.gt[:], b.gt[:], 0.5, 0.5, ALU.mult, ALU.add))
                        link(nc.vector.tensor_tensor(b.ch[:], b.gt[:], b.e_bias[:].unsqueeze(1).broadcast_to([128, 6, E]), ALU.add), alone=True)
                        for c in range(6):
                            ins = nc.vector.max(b.top8[:, c, :], b.ch[:, c, :])
                        link(ins)
                        link(nc.vector.memset(b.top8[:, :, TOPK:8], -BIG), alone=True)
                        for c in range(6):
                            ins = nc.vector.match_replace(b.ch[:, c, :], b.top8[:, c, :], b.ch[:, c, :], BIG)
                        link(ins)
                        nc.vector.tensor_scalar(b.mask[:], b.ch[:], BIG / 2, None, ALU.is_ge).then_inc(mask_ready, 1)
                    elif kind == "weigh":
                        dve.wait_ge(mask_ready, t.v + 1)
                        link = Chain(dve, "weigh", t)
                        den = b.top8[:, :, 0]
                        link(nc.vector.tensor_tensor(b.ch[:], b.gt[:], b.mask[:], ALU.mult))
                        link(nc.vector.tensor_reduce(den, b.ch[:], AX.X, ALU.add))
                        link(nc.vector.tensor_scalar(den, den, 1e-20, None, ALU.add))
                        link(nc.vector.reciprocal(b.top8[:, :, 1], den))
                        nc.vector.tensor_scalar(b.x2[:, :, :, D], b.top8[:, :, 1].rearrange("p (b k) -> p b k", b=2), SCALE / 4, None, ALU.mult).then_inc(factor_ready, 1)
                    elif kind == "count":
                        dve.wait_ge(misc_full, uses)
                        wait(dve, cnt_ready, t.v)
                        wait(dve, cnt_stored, 16 * t.v)
                        nc.vector.tensor_tensor_scan(b.cnt[:], misc.bitcast(BF16)[:, 0:2 * L], b.zeros[:], b.run[:, 0:1], ALU.add, ALU.add).then_inc(misc_free, 1)
                        dve.wait_ge(misc_free, uses)
                        nc.vector.tensor_copy(b.run[:], b.cnt[:, 2 * L - 1:2 * L])
                        nc.vector.tensor_copy(b.block_end[:, bass.ds(t.v * 2, 2)], b.cnt[:, L - 1:2 * L:L]).then_inc(cnt_ready, 1)
                    elif kind == "up_g":
                        dve.wait_ge(th_ready, NJ * t.v + k + 1)
                        wait(dve, inter_ready, NJ * t.v + k)
                        nc.vector.scalar_tensor_tensor(b.ag[:], b.th[:], 1.0, g_ps, ALU.add, ALU.mult).then_inc(g_used, 1)
                    elif kind == "up_u":
                        dve.wait_ge(u_full, NJ * t.v + k + 1)
                        dve.wait_ge(g_used, NJ * t.v + k + 1)
                        if k == 0:
                            wait(dve, out_ready, t.v)
                        nc.vector.tensor_tensor(b.inter[:, k], b.ag[:], u_ps, ALU.mult).then_inc(inter_ready, 1)

            run_bodies(dve, body)

        @block.tensor
        def _(pe):
            def both(to, weights, tiles, batch, cols):
                nc.tensor.matmul(to, weights[:, 0, cols], tiles[:, batch, :], start=True, stop=False)
                return nc.tensor.matmul(to, weights[:, 1 + batch, cols], tiles[:, 2, :], start=False, stop=True)

            def spread(t, n, c):
                rhs = b.parts[t.p][:, c, :]
                for q in range(2):
                    nc.tensor.matmul(ps[:, q, 0:L], b.pick[:, 16 * q + n:16 * q + n + 1].broadcast_to([96, 128]), rhs, start=True, stop=True)
                for q in range(2):
                    mm = nc.tensor.matmul(ps[HI * q:HI * q + HI, 2, 0:L], b.pick[:, 16 * q + n:16 * q + n + 1].broadcast_to([96, HI]), rhs, start=True, stop=True)
                return mm

            def body(i, todo, uses):
                for kind, lag, k in todo:
                    t = i.plus(-lag)
                    if kind in MISC:
                        wait(pe, misc_free, uses)
                        uses = uses + 1
                    if kind == "fill_b":
                        if k == 0:
                            pe.wait_ge(parts_ready, t.v + 1)
                        if k in (1, 2):
                            pe.wait_ge(b_copied, N * t.v + k)
                        else:
                            wait(pe, c_used, N * t.v + (k - 2 if k else 0))
                        spread(t, k, 0).then_inc(b_full, 1)
                    elif kind == "fill_c":
                        if k + 2 < N:
                            pe.wait_ge(b_copied, N * t.v + k + 3)
                        else:
                            pe.wait_ge(c_used, N * t.v + k)
                        spread(t, k, 1).then_inc(c_full, 1)
                    elif kind == "down":
                        pe.wait_ge(inter_ready, NJ * (t.v + 1))
                        for q in range(2):
                            for j in range(NJ):
                                mm = nc.tensor.matmul(misc[0:ROWS[k], D * q:D * q + D], b.inter[:, j, q, OFF[k]:OFF[k] + ROWS[k]], b.ws_d[:, j, :],
                                                      start=(j == 0), stop=(j == NJ - 1))
                        mm.then_inc(misc_full, 1)
                    elif kind == "resid":
                        pe.wait_ge(y_added, 15 * (t.v + 1))
                        for q in range(3):
                            mm = nc.tensor.transpose(misc[0:ROWS[k], 128 * q:128 * q + 128], b.y[t.p][:, q, OFF[k]:OFF[k] + ROWS[k]], b.ident[:])
                        mm.then_inc(misc_full, 1)
                    elif kind in ("x1_turn", "x2_turn"):
                        m = int(kind[1]) - 1
                        pe.wait_ge(ln_done[m], t.v + 1)
                        x = (b.xn, b.x2)[m]
                        for c in range(3):
                            r = ROWS[c]
                            source = x[0:r, k, c, 0:LO] if k < 2 else b.xm[m][0:r, c].rearrange("p b d -> p (b d)")
                            mm = nc.tensor.transpose(misc[:, OFF[c]:OFF[c] + r], source, b.ident[0:r, 0:r])
                        mm.then_inc(misc_full, 1)
                    elif kind == "gate":
                        for c in range(3):
                            to, at = misc[0:ROWS[c], E * c:E * c + E], slice(OFF[c], OFF[c] + ROWS[c])
                            nc.tensor.matmul(to, b.x2f[t.p][:, k, at], b.wg[:, 0, :], start=True, stop=False)
                            mm = nc.tensor.matmul(to, b.x2f[t.p][:, 2, at], b.wg[:, 1 + k, :], start=False, stop=True)
                        mm.then_inc(misc_full, 1)
                    elif kind == "count":
                        pe.wait_ge(mask_ready, t.v + 1)
                        turned = misc.bitcast(BF16)
                        for q in range(2):
                            for c in range(3):
                                r = ROWS[c]
                                mm = nc.tensor.transpose(turned[:, L * q + OFF[c]:L * q + OFF[c] + r], b.mask[0:r, 3 * q + c, :], b.ident_bf[0:r, 0:r])
                        mm.then_inc(misc_full, 1)
                    elif kind == "emb":
                        pe.wait_ge(sq_ready, 2 * t.v + k + 1)
                        for c in range(2):
                            at = slice(98 * c, 98 * c + 98)
                            for f in range(PC):
                                mm = nc.tensor.matmul(misc[0:98, 196 * c + D + 2:196 * c + D + 4], b.x_sq[:, f, at], b.ones[:, 0:2], start=(f == 0), stop=(f == PC - 1))
                            if c == 1:
                                mm.then_inc(sq_used, 1)
                            for f in range(PC):
                                mm = nc.tensor.matmul(misc[0:98, 196 * c:196 * c + D + 2], b.x_in[:, k, f, at], b.w_tok[:, f, :], start=(f == 0), stop=(f == PC - 1))
                        mm.then_inc(misc_full, 1)
                    elif kind == "bc_values":
                        for q in range(3):
                            mm = nc.tensor.matmul(misc[0:64, 0:L], b.wbc[:, q, :], b.xf[:, q, :], start=(q == 0), stop=(q == 2))
                        mm.then_inc(misc_full, 1)
                    elif kind == "step_size":
                        terms = (((0, 0), (3, 2)), ((0, 1), (4, 2)), ((1, 0), (2, 1), (5, 2)))[k]
                        for n, (w, q) in enumerate(terms):
                            mm = nc.tensor.matmul(misc[:, 0:L], b.w1[:, w, :], b.xf[:, q, :], start=(n == 0), stop=(n == len(terms) - 1))
                        mm.then_inc(misc_full, 1)
                    elif kind == "up_g":
                        pe.wait_ge(factor_ready, t.v + 1)
                        wait(pe, g_used, NJ * t.v + k)
                        for q in range(2):
                            mm = both(ps[0:HC, 3 + q, 0:L], b.ws_g, b.x2f[t.p], q, slice(HC * k, HC * k + HC))
                        mm.then_inc(g_full, 1)
                    elif kind == "up_u":
                        wait(pe, inter_ready, NJ * t.v + k)
                        for q in range(2):
                            mm = both(ps[0:HC, 5 + q, 0:L], b.ws_u, b.x2f[t.p], q, slice(HC * k, HC * k + HC))
                        mm.then_inc(u_full, 1)

            run_bodies(pe, body)


EXPERT_ORDER = [
    ("load_up", -1), ("token", -2), ("row", -3), ("up_g", 0), ("down", 1), ("load_down", -1),
    ("up_u", 0), ("scatter", 1), ("turn", -1),
]
E_FIRST, E_FROM, E_TO, E_LAST = -3, 1, 125, E


def run_experts(eng, body):
    def todo(i):
        return [x for x in EXPERT_ORDER if 0 <= i - x[1] < E]

    for i in range(E_FIRST, E_FROM):
        body(Turn.fixed(i), todo(i))
    with eng.Fori(0, (E_TO - E_FROM) // 2) as r:
        for q in range(2):
            start = Turn.fixed(E_FROM + q)
            body(Turn(start.v + 2 * r, start.p, start.h + r), EXPERT_ORDER)
    for i in range(E_TO, E_LAST + 1):
        body(Turn.fixed(i), todo(i))


def phase2(nc, ctx, a, out, dram_x, dram_cnt, ident, block_end):
    sb = lambda name, shape, dt=F32: ctx.enter_context(nc.sbuf_tensor(name, shape, dt))
    sem = lambda name: ctx.enter_context(nc.semaphore(name))
    KC = D // 2
    slot_int = sb("slot_int", [128, CAP], U32)
    slot = sb("slot", [128, CAP])
    lane_int = sb("lane_int", [128, 3], U32)
    lane = sb("lane", [128, 3])
    less = sb("less", [E, HALF, B])
    block_of = sb("block_of", [E, 2, 2, HALF])
    base = sb("base", [HALF, 2, E])
    row = sb("row", [HALF, 2, E])
    tokens = sb("tokens", [HALF, 2, E])
    two = lambda name, shape, dt=F32: [sb(f"{name}{p}", shape, dt) for p in range(2)]
    row_idx, gather_idx, scatter_idx = (two(n, [HALF, 2], U32) for n in ("row_idx", "gather_idx", "scatter_idx"))
    counts = two("counts", [HALF, 2, L])
    passed = sb("passed", [HALF, 2, L])
    tk = sb("tk", [HALF, 3, 2])
    xg = two("xg", [HALF, 2, XW])
    xgt = two("xgt", [KC, 2, CAP])
    w_up = two("w_up", [KC, 2, 2 * HID + 1])
    w_down = two("w_down", [HC, NF, D])
    tw = sb("tw", [HALF, 2])
    weight = two("weight", [HALF, 2])
    th = sb("e_th", [HC, 2, 2 * CAP])
    ag = sb("e_ag", [HC, 2, 2 * CAP])
    inter = sb("e_inter", [HC, 2, 2 * CAP])
    yo = two("yo", [HALF, 2, D])
    ps = ctx.enter_context(nc.psum_tensor("e_ps", [128, 8, 512], F32))
    g_ps, u_ps = ps[0:HC, 0:2, 0:2 * CAP], ps[0:HC, 2:4, 0:2 * CAP]

    iota_done, slots_ready, found, turned_in, table_ready = (sem(n) for n in ("iota_done", "slots_ready", "found", "turned_in", "table_ready"))

    with nc.Block() as block:

        @block.gpsimd
        def _(pool):
            nc.gpsimd.iota(slot_int[:], [[1, CAP]], base=0, channel_multiplier=0).then_inc(iota_done, 1)
            nc.gpsimd.iota(lane_int[:, 0:1], [[0, 1]], base=0, channel_multiplier=B).then_inc(iota_done, 1)
            nc.gpsimd.iota(lane_int[:, 1:3], [[HALF, 2]], base=0, channel_multiplier=1).then_inc(iota_done, 1)

        @block.vector
        def _(dve):
            n = [0]

            def step(ins):
                n[0] += 1
                ins.then_inc(found, 1)
                dve.wait_ge(found, n[0])

            dve.wait_ge(iota_done, 3)
            step(nc.vector.tensor_copy(slot[:], slot_int[:]))
            step(nc.vector.tensor_copy(lane[:], lane_int[:]))
            for q in range(2):
                step(nc.vector.tensor_tensor(less[:], block_end[:].unsqueeze(1).broadcast_to([E, HALF, B]),
                                             slot[:, HALF * q:HALF * q + HALF].unsqueeze(2).broadcast_to([E, HALF, B]), ALU.is_le))
                step(nc.vector.tensor_reduce(block_of[:, q, 0, :], less[:], AX.X, ALU.add))
                step(nc.vector.tensor_scalar(block_of[:, q, 0, :], block_of[:, q, 0, :], B - 1.0, None, ALU.min))
                step(nc.vector.tensor_scalar(block_of[:, q, 1, :], block_of[:, q, 0, :], lane[:, 0:1], None, ALU.add))
            nc.vector.tensor_copy(tk[:, 0, :], lane[0:HALF, 1:3]).then_inc(slots_ready, 1)
            dve.wait_ge(turned_in, 1)
            step(nc.vector.tensor_scalar(base[:], ps[0:HALF, 0, 0:2 * E].rearrange("p (q e) -> p q e", q=2), float(L), None, ALU.mult))
            step(nc.vector.tensor_copy(row[:], ps[0:HALF, 0, 2 * E:4 * E].rearrange("p (q e) -> p q e", q=2)))

        @block.tensor
        def _(pe):
            pe.wait_ge(slots_ready, 1)
            for c in range(2):
                for q in range(2):
                    mm = nc.tensor.transpose(ps[0:HALF, 0, (2 * c + q) * E:(2 * c + q + 1) * E], block_of[:, q, c, :], ident[:])
            mm.then_inc(turned_in, 1)

    up_loaded = [sem(f"up_loaded{p}") for p in range(2)]
    down_loaded = [sem(f"down_loaded{p}") for p in range(2)]
    row_ready, counts_loaded = sem("row_ready"), [sem(f"counts_loaded{p}") for p in range(2)]
    passed_ready, sum_ready, token_steps = sem("passed_ready"), sem("sum_ready"), sem("token_steps")
    token_ready, x_gathered = sem("token_ready"), [sem(f"x_gathered{p}") for p in range(2)]
    turn_full, xgt_ready, gate_full, tw_ready, weight_ready = (sem(n) for n in ("turn_full", "xgt_ready", "gate_full", "tw_ready", "weight_ready"))
    e_g_full, e_th_ready, e_g_used, e_u_full, e_inter_ready = (sem(n) for n in ("e_g_full", "e_th_ready", "e_g_used", "e_u_full", "e_inter_ready"))
    down_full, yo_ready, scatter_ready = sem("down_full"), sem("yo_ready"), sem("scatter_ready")
    added = [sem(f"added{p}") for p in range(2)]
    waited = sem("e_waited")

    with nc.Block() as block:

        @block.sync
        def _(sp):
            def body(i, todo):
                for kind, lag in todo:
                    t = i.plus(-lag)
                    if kind == "load_up":
                        wait(sp, e_u_full, t.v - 1)
                        sp.dma_start(w_up[t.p][:], a["we_up"][bass.ds(t.v, 1)].rearrange("o p c f -> p (o c) f")).then_inc(up_loaded[t.p], 16)
                    elif kind == "load_down":
                        wait(sp, down_full, t.v - 1)
                        sp.dma_start(w_down[t.p][:], a["we_down"][bass.ds(t.v, 1)].rearrange("o p c f -> p (o c) f")).then_inc(down_loaded[t.p], 16)

            run_experts(sp, body)

        @block.gpsimd
        def _(pool):
            def body(i, todo):
                for kind, lag in todo:
                    t = i.plus(-lag)
                    if kind == "row":
                        pool.wait_ge(row_ready, t.v + 1)
                        wait(pool, passed_ready, t.v - 1)
                        pool.sem_inc(waited, 1)
                        for q in range(2):
                            nc.gpsimd.indirect_dma_start(counts[t.p][:, q, :], None, dram_cnt, bass.IndirectOffsetOnAxis(ap=row_idx[t.p][:, q:q + 1], axis=0)).then_inc(counts_loaded[t.p], 16)
                    elif kind == "token":
                        pool.wait_ge(token_ready, t.v + 1)
                        wait(pool, weight_ready, t.v - 1)
                        pool.sem_inc(waited, 1)
                        for q in range(2):
                            nc.gpsimd.indirect_dma_start(xg[t.p][:, q, :], None, dram_x, bass.IndirectOffsetOnAxis(ap=gather_idx[t.p][:, q:q + 1], axis=0)).then_inc(x_gathered[t.p], 16)
                    elif kind == "scatter":
                        pool.wait_ge(scatter_ready, t.v + 1)
                        pool.wait_ge(yo_ready, t.v + 1)
                        before = t.plus(-1)
                        wait(pool, added[before.p], 32 * before.h + 32)
                        pool.sem_inc(waited, 1)
                        for q in range(2):
                            nc.gpsimd.indirect_dma_start(out, bass.IndirectOffsetOnAxis(ap=scatter_idx[t.p][:, q:q + 1], axis=0), yo[t.p][:, q, :], None, compute_op=ALU.add).then_inc(added[t.p], 16)

            run_experts(pool, body)
            for p in range(2):
                pool.wait_ge(added[p], 32 * E // 2)

        @block.scalar
        def _(act):
            def body(i, todo):
                for kind, lag in todo:
                    t = i.plus(-lag)
                    if kind == "turn":
                        act.wait_ge(turn_full, t.v + 1)
                        wait(act, e_u_full, t.v - 1)
                        nc.scalar.activation(xgt[t.p][:].rearrange("p c s -> p (c s)"), ps[0:KC, 5, 0:2 * CAP], ACT.Copy).then_inc(xgt_ready, 1)
                        act.wait_ge(gate_full, t.v + 1)
                        wait(act, weight_ready, t.v)
                        nc.scalar.activation(tw[:], ps[0:HALF, 6, 0:2], ACT.Tanh, scale=0.5).then_inc(tw_ready, 1)
                    elif kind == "up_g":
                        act.wait_ge(e_g_full, t.v + 1)
                        wait(act, e_g_used, t.v)
                        nc.scalar.activation(th[:], g_ps, ACT.Tanh, scale=0.5).then_inc(e_th_ready, 1)

            run_experts(act, body)

        @block.vector
        def _(dve):
            def body(i, todo):
                for kind, lag in todo:
                    t = i.plus(-lag)
                    if kind == "row":
                        wait(dve, counts_loaded[t.p], 32 * t.h)
                        nc.vector.tensor_copy(row_idx[t.p][:], row[:, :, bass.ds(t.v, 1)].rearrange("p q o -> p (q o)")).then_inc(row_ready, 1)
                    elif kind == "token":
                        dve.wait_ge(counts_loaded[t.p], 32 * t.h + 32)
                        slots = tk[:, 0, :].unsqueeze(2).broadcast_to([HALF, 2, L])
                        nc.vector.tensor_tensor(passed[:], counts[t.p][:], slots, ALU.is_le).then_inc(passed_ready, 1)
                        dve.wait_ge(passed_ready, t.v + 1)
                        nc.vector.tensor_reduce(tk[:, 1, :], passed[:], AX.X, ALU.add).then_inc(sum_ready, 1)
                        dve.wait_ge(sum_ready, t.v + 1)
                        nc.vector.tensor_tensor(tk[:, 1, :], tk[:, 1, :], base[:, :, bass.ds(t.v, 1)].rearrange("p q o -> p (q o)"), ALU.add).then_inc(token_steps, 1)
                        dve.wait_ge(token_steps, 2 * t.v + 1)
                        nc.vector.scalar_tensor_tensor(tk[:, 2, :], tk[:, 1, :], float(T_ALL), tk[:, 0, :], ALU.is_ge, ALU.mult).then_inc(token_steps, 1)
                        dve.wait_ge(token_steps, 2 * t.v + 2)
                        wait(dve, x_gathered[t.p], 32 * t.h)
                        nc.vector.tensor_tensor(tokens[:, :, bass.ds(t.v, 1)].rearrange("p q o -> p (q o)"), tk[:, 1, :], tk[:, 2, :], ALU.add)
                        nc.vector.tensor_tensor(gather_idx[t.p][:], tk[:, 1, :], tk[:, 2, :], ALU.add).then_inc(token_ready, 1)
                    elif kind == "up_g":
                        dve.wait_ge(e_th_ready, t.v + 1)
                        wait(dve, e_inter_ready, t.v)
                        nc.vector.scalar_tensor_tensor(ag[:], th[:], 1.0, g_ps, ALU.add, ALU.mult).then_inc(e_g_used, 1)
                    elif kind == "down":
                        dve.wait_ge(down_full, t.v + 1)
                        dve.wait_ge(weight_ready, t.v + 1)
                        wait(dve, added[t.p], 32 * t.h)
                        nc.vector.tensor_tensor(yo[t.p][:], ps[0:HALF, 4, 0:2 * D].rearrange("p (q d) -> p q d", q=2),
                                                weight[t.p][:].unsqueeze(2).broadcast_to([HALF, 2, D]), ALU.mult).then_inc(yo_ready, 1)
                        nc.vector.tensor_copy(scatter_idx[t.p][:], tokens[:, :, bass.ds(t.v, 1)].rearrange("p q o -> p (q o)")).then_inc(scatter_ready, 1)
                    elif kind == "up_u":
                        dve.wait_ge(e_u_full, t.v + 1)
                        dve.wait_ge(e_g_used, t.v + 1)
                        wait(dve, down_full, t.v)
                        nc.vector.tensor_tensor(inter[:], ag[:], u_ps, ALU.mult).then_inc(e_inter_ready, 1)
                    elif kind == "turn":
                        dve.wait_ge(tw_ready, t.v + 1)
                        dve.wait_ge(x_gathered[t.p], 32 * t.h + 32)
                        wait(dve, yo_ready, t.v - 1)
                        nc.vector.scalar_tensor_tensor(weight[t.p][:], tw[:], 1.0, xg[t.p][:, :, D], ALU.add, ALU.mult).then_inc(weight_ready, 1)

            run_experts(dve, body)

        @block.tensor
        def _(pe):
            def apply(to_bank, t, first):
                for f in range(NF):
                    for c in range(2):
                        mm = nc.tensor.matmul(ps[0:HC, to_bank + f // 2, CAP * (f % 2):CAP * (f % 2) + CAP],
                                              w_up[t.p][:, c, first + HC * f:first + HC * f + HC], xgt[t.p][:, c, :], start=(c == 0), stop=(c == 1))
                return mm

            def body(i, todo):
                for kind, lag in todo:
                    t = i.plus(-lag)
                    if kind == "turn":
                        pe.wait_ge(x_gathered[t.p], 32 * t.h + 32)
                        wait(pe, xgt_ready, t.v)
                        for c in range(2):
                            for q in range(2):
                                mm = nc.tensor.transpose(ps[0:KC, 5, CAP * c + HALF * q:CAP * c + HALF * q + HALF], xg[t.p][:, q, KC * c:KC * c + KC], ident[0:HALF, 0:HALF])
                        mm.then_inc(turn_full, 1)
                        pe.wait_ge(xgt_ready, t.v + 1)
                        pe.wait_ge(up_loaded[t.p], 16 * t.h + 16)
                        wait(pe, tw_ready, t.v)
                        for q in range(2):
                            for c in range(2):
                                mm = nc.tensor.matmul(ps[0:HALF, 6, q:q + 1], xgt[t.p][:, c, HALF * q:HALF * q + HALF], w_up[t.p][:, c, 2 * HID:2 * HID + 1], start=(c == 0), stop=(c == 1))
                        mm.then_inc(gate_full, 1)
                    elif kind == "up_g":
                        wait(pe, e_g_used, t.v)
                        apply(0, t, 0).then_inc(e_g_full, 1)
                    elif kind == "up_u":
                        wait(pe, e_inter_ready, t.v)
                        apply(2, t, HID).then_inc(e_u_full, 1)
                    elif kind == "down":
                        pe.wait_ge(e_inter_ready, t.v + 1)
                        pe.wait_ge(down_loaded[t.p], 16 * t.h + 16)
                        wait(pe, yo_ready, t.v)
                        for q in range(2):
                            for f in range(NF):
                                at = CAP * (f % 2) + HALF * q
                                mm = nc.tensor.matmul(ps[0:HALF, 4, D * q:D * q + D], inter[:, f // 2, at:at + HALF], w_down[t.p][:, f, :], start=(f == 0), stop=(f == NF - 1))
                        mm.then_inc(down_full, 1)

            run_experts(pe, body)


def _layout(i):
    import numpy as np

    x = np.asarray(i["x"]).reshape(B, 3, 14, 16, 14, 16).transpose(0, 3, 5, 1, 2, 4).reshape(B, PC, 128, IMG).transpose(0, 2, 1, 3)
    up = np.concatenate([np.asarray(i["L0_ffn_W_gate_up"]), np.asarray(i["L0_ffn_Wg"])[:, :, None]], axis=2)
    n = lambda k: np.asarray(i["L0_" + k])
    return {
        "x": x,
        "txt": np.asarray(i["txt"]),
        "ln_w": n("tok_ln_w").reshape(PC, 128).T,
        "ln_b": n("tok_ln_b").reshape(PC, 128).T,
        "w_tok": n("tok_W").reshape(PC, 128, D).transpose(1, 0, 2),
        "b_tok": n("tok_b").reshape(1, D),
        "pos": n("tok_pos_emd").reshape(2, 98, D).transpose(1, 0, 2),
        "a_log": n("attn_A_log"),
        "w_bc_t": n("attn_W_bc").T,
        "b_bc": n("attn_b_bc").reshape(2 * N, 1),
        "w_1": n("attn_W_1").reshape(D, 1),
        "b_1": n("attn_b_1").reshape(1, 1),
        "w_d": n("attn_W_d").reshape(D, 1),
        "b_d": n("attn_b_d").reshape(D, 1),
        "wg_t": n("ffn_Wg").T,
        "e_bias": n("ffn_e_bias").reshape(1, E),
        "we_up": up.reshape(E, 2, 96, 2 * HID + 1).transpose(0, 2, 1, 3),
        "we_down": n("ffn_W_down").reshape(E, NF, HC, D).transpose(0, 2, 1, 3),
        "ws_g": n("ffn_Wsg"),
        "ws_u": n("ffn_Wsu"),
        "ws_d": n("ffn_Wsd").reshape(NJ, HC, D).transpose(1, 0, 2),
    }


def kernel(**inputs):
    import numpy as np
    import concourse.bacc as bacc
    from concourse.bass_utils import run_bass_kernel_spmd

    nc = bacc.Bacc("TRN2", target_bir_lowering=False, num_devices=1)
    arrays, args = {}, {}
    for name, value in _layout(inputs).items():
        arrays[f"in_{name}"] = np.ascontiguousarray(value)
        args[name] = nc.dram_tensor(f"in_{name}", value.shape, mybir.dt.from_np(value.dtype), kind="ExternalInput").ap()
    out = nc.dram_tensor("out_rows", (T_ALL + CAP, D), F32, kind="ExternalOutput").ap()
    build(nc, args, out)
    got = run_bass_kernel_spmd(nc, [arrays], core_ids=[0]).results[0]["out_rows"]
    return got[0:T_ALL].reshape(B, L, D)
```

```python
from contextlib import ExitStack

import concourse.bass as bass
from concourse import mybir

F32 = mybir.dt.float32
BF16 = mybir.dt.bfloat16
U32 = mybir.dt.uint32
ALU = mybir.AluOpType
ACT = mybir.ActivationFunctionType
AX = mybir.AxisListType

B, L, D, N = 64, 324, 192, 16
IMG, TXT = 196, 128
PATCH, PC = 768, 6
ROWS = (98, 98, 128)
OFF = (0, 98, 196)
PAIRS = B // 2
T_ALL = B * L
LO, HI = 128, D - 128
E, CAP, TOPK = 128, 192, 6
HID, HC = 464, 116
NF = HID // HC
SHID = 928
NJ = SHID // HC
HALF = CAP // 2
SCALE = 2.5
EPS = 1e-5
BIG = 3.0e38
XW = D + 2


class Turn:

    def __init__(self, v, p, h):
        self.v, self.p, self.h = v, p, h

    @classmethod
    def fixed(cls, n):
        return cls(n, n % 2, n // 2)

    def plus(self, k):
        return Turn(self.v + k, (self.p + k) % 2, self.h + (self.p + k) // 2)


def wait(eng, sem, value):
    if not (isinstance(value, int) and value <= 0):
        eng.wait_ge(sem, value)


def schedule(engine):
    at = []

    def put(piece, lag, k, **steps):
        if engine in steps:
            at.append((steps[engine], len(at), (piece, lag, k)))

    for n in range(N):
        b, lag = 2 * (n - 2) + 1, 0
        if b < 0:
            b, lag = b + 32, -1
        put("fill_b", lag, n, pe=b, act=b + 1, pool=b + 2)
        d, lag = (2 * n - 1.5, 0) if n else (30.5, -1)
        put("decay", lag, n, act=d)
        put("scan", 0, n, dve=2 * n)
        put("fill_c", 0, n, pe=2 * n, dve=2 * n + 1, pool=2 * n + 2)
    for k in range(3):
        put("down_a", 3, k, pe=2 * k + 0.1)
        put("down", 3, k, pe=2 * k + 1.1, dve=2 * k + 2.1)
        put("store_out", 3, k, sp=2 * k + 2.2)
        put("resid", 1, k, pe=4.9 + 1.8 * k, dve=5.7 + 1.8 * k)
        put("x2_turn", 1, k, pe=16.2 + k, act=17.2 + k)
        put("x1_turn", -1, k, pe=19.2 + k, act=20.2 + k)
        put("step_size", -1, k, pe=25.2 + k, act=26.2 + k)
    put("load_x", -2, 0, sp=1)
    put("load_txt", -1, 0, sp=10)
    put("ln2_center", 1, 0, dve=10.3, act=11.3)
    put("ln2_var", 1, 0, dve=12.3, act=13.3)
    put("ln2_scale", 1, 0, dve=14.3)
    put("emb_scale", -1, 0, dve=11.4)
    put("ln1_center", -1, 0, dve=12.4, act=13.4)
    put("ln1_var", -1, 0, dve=15.4, act=16.4)
    put("ln1_scale", -1, 0, dve=17.4)
    for k in range(2):
        put("gate", 1, k, pe=22.3 + k, act=23.3 + k)
        put("emb_a", -2, k, pe=8.5 + 6 * k, act=7.5 + 5.2 * k)
        put("emb", -2, k, pe=11.5 + 6 * k, act=12.6 + 6 * k)
    put("bc_values", -1, 0, pe=24.3, act=25.3, dve=26.3)
    put("softplus", -1, 0, act=28.3, dve=29.2)
    put("choose", 1, 0, dve=24.4)
    put("weigh", 1, 0, dve=27.4)
    put("count", 1, 0, pe=28.4, dve=29.4)
    put("store_mid", 1, 0, sp=30.4)
    put("emb_stats", -2, 0, dve=20.4, act=21.4)
    for k in range(NJ):
        for n, piece in enumerate(("up_g", "up_u")):
            step = 6.6 + 1.6 * (2 * k + n)
            put(piece, 2, k, pe=step, act=step + 0.9, dve=step + 1)
    return [piece for _, _, piece in sorted(at)]


SCHEDULE = {engine: schedule(engine) for engine in ("pe", "act", "dve", "pool", "sp")}
WORK, SUMS = 0, 1
BANK = {"resid": WORK, "x2_turn": WORK, "gate": WORK, "count": WORK, "x1_turn": WORK, "bc_values": WORK, "step_size": WORK,
        "down": SUMS, "emb": SUMS}
FIRST_BODY, LOOP_FROM, LOOP_TO, LAST_BODY = -2, 3, 29, PAIRS + 2


def pieces(engine, i):
    return [x for x in SCHEDULE[engine] if 0 <= i - x[1] < PAIRS]


def bank_uses(i):
    return [sum(BANK.get(kind) == bank for kind, _, _ in pieces("pe", i)) for bank in (WORK, SUMS)]


def use_number(i, before):
    def use(piece, k):
        same = [x for x in pieces("pe", i) if BANK.get(x[0]) == BANK[piece]]
        return before[BANK[piece]] + [(kind, n) for kind, _, n in same].index((piece, k)) + 1
    return use


def run_bodies(eng, engine, body):
    before = [0, 0]
    add = lambda n, times: [b + x * times for b, x in zip(before, n)]
    for i in range(FIRST_BODY, LOOP_FROM):
        body(Turn.fixed(i), pieces(engine, i), use_number(i, before))
        before = add(bank_uses(i), 1)
    steady = bank_uses(LOOP_FROM)
    with eng.Fori(0, (LOOP_TO - LOOP_FROM) // 2) as r:
        for q in range(2):
            start = Turn.fixed(LOOP_FROM + q)
            so_far = [x + 2 * n * r for x, n in zip(add(steady, q), steady)]
            body(Turn(start.v + 2 * r, start.p, start.h + r), pieces(engine, LOOP_FROM), use_number(LOOP_FROM, so_far))
    before = add(steady, LOOP_TO - LOOP_FROM)
    for i in range(LOOP_TO, LAST_BODY + 1):
        body(Turn.fixed(i), pieces(engine, i), use_number(i, before))
        before = add(bank_uses(i), 1)


def build(nc, a, out):
    dram_x = nc.dram_tensor("token_rows", (T_ALL + CAP, XW), F32).ap()
    dram_cnt = nc.dram_tensor("running_counts", (E * B, L), F32).ap()
    with ExitStack() as outer:
        ident = outer.enter_context(nc.sbuf_tensor("ident", [128, 128], F32))
        block_end = outer.enter_context(nc.sbuf_tensor("block_end", [E, B], F32))
        with ExitStack() as ctx:
            phase1(nc, ctx, a, out, dram_x, dram_cnt, ident, block_end)
        with ExitStack() as ctx:
            phase2(nc, ctx, a, out, dram_x, dram_cnt, ident, block_end)


class Buffers:

    def __init__(self, nc, ctx, ident, block_end):
        sb = lambda name, shape, dt=F32: ctx.enter_context(nc.sbuf_tensor(name, shape, dt))
        self.ident, self.block_end = ident, block_end
        self.ident_bf = sb("ident_bf", [128, 128], BF16)
        self.ones = sb("ones", [128, 128])
        self.zeros = sb("zeros", [128, 2 * L])
        self.w_tok = sb("w_tok", [128, PC, D + 2])
        self.pos = sb("pos", [ROWS[0], 2, D])
        self.a_neg = sb("a_neg", [128, 2, N])
        self.wbc = sb("wbc", [128, 3, 64])
        self.bc_bias = sb("bc_bias", [32, 2])
        self.w1 = sb("w1", [128, 6, 128])
        self.wd = sb("wd", [128, 2])
        self.bd = sb("bd", [128, 2])
        self.pick = sb("pick", [96, 32], BF16)
        self.pick2 = sb("pick2", [96, N, 128], BF16)
        self.wg = sb("wg", [128, 3, E])
        self.e_bias = sb("e_bias", [128, E])
        self.ws_g = sb("ws_g", [128, 3, SHID])
        self.ws_u = sb("ws_u", [128, 3, SHID])
        self.ws_d = sb("ws_d", [HC, NJ, D])
        two = lambda name, shape, dt=F32, n=2: [sb(f"{name}{p}", shape, dt) for p in range(n)]
        self.x_in = sb("x_in", [128, 2, PC, IMG])
        self.x_sq = sb("x_sq", [128, PC, IMG])
        self.emb = sb("emb", [ROWS[0], 2, 2, 196])
        self.h = two("h", [128, 2, 3, D])
        self.h2 = two("h2_", [128, 2, 3, D])
        self.xn = sb("xn", [128, 2, 3, D])
        self.xm = two("xm", [128, 3, 2, HI])
        self.x2 = sb("x2", [128, 2, 3, XW])
        self.ln_sq = sb("ln_sq", [128, 2, 3, D])
        self.xf = sb("xf", [128, 3, L])
        self.x2f = two("x2f", [128, 3, L])
        self.delta = two("delta", [128, 3, L])
        self.du = two("du", [128, 3, L])
        self.soft = sb("soft", [128, 3, L])
        self.bcv = self.ln_sq[0:32].rearrange("p b k d -> p (b k d)")[:, 0:2 * L].rearrange("p (c t) -> p c t", c=2)
        self.mid_part = sb("mid_part", [32, 2, L], BF16)
        self.parts = two("parts", [96, 2, L], BF16)
        self.decay = two("decay", [128, 3, L])
        self.b_wide = two("b_wide", [128, 3, L])
        self.state = two("state", [128, 3, L], n=4)
        self.y = two("y", [128, 3, L])
        self.th = sb("th", [HC, 2, L])
        self.ag = sb("ag", [HC, 2, L])
        self.inter = sb("inter", [HC, NJ, 2, L])
        self.gt = sb("gt", [128, 6, E])
        self.ch = sb("ch", [128, 6, E])
        self.mask = sb("mask", [128, 6, E], BF16)
        self.top8 = sb("top8", [128, 6, 8])
        self.stat = sb("stat", [128, 3, 6, 6])
        self.cnt = sb("cnt", [E, 2 * L])
        self.run = sb("run", [E, 1])
        self.ps = ctx.enter_context(nc.psum_tensor("ps", [128, 8, 512], F32))


def prepare(nc, ctx, a, out, dram_x, b):
    sem = lambda name: ctx.enter_context(nc.semaphore(name))
    filled, made, loaded, prepared = sem("filled"), sem("made"), sem("loaded"), sem("prepared")
    mean_full, bias_full, a_exp, padded = sem("mean_full"), sem("bias_full"), sem("a_exp"), sem("padded")
    with ExitStack() as tmp:
        sb = lambda name, shape, dt=F32: tmp.enter_context(nc.sbuf_tensor(name, shape, dt))
        w_raw = b.x_in[:].rearrange("p b c t -> p (b c t)")[:, 0:PC * D].rearrange("p (c d) -> p c d", c=PC)
        small = b.x_sq[:].rearrange("p c t -> p (c t)")
        ln_w, ln_b, w1c = small[:, 0:PC], small[:, PC:2 * PC], small[:, 12:14]
        b1 = small[:, 14:15]
        b_tok = b.ln_sq[0:ROWS[0], 0, 0, :]
        mean_w = b.soft[:, 0, 0:128]
        zero_tiles = [b.ident, b.ident_bf, b.pick, b.wbc, b.w1, b.wg, b.ws_g, b.ws_u, b.zeros, b.gt, b.x2, b.run, b.stat,
                      b.xn, *b.xm, b.ln_sq, b.x_in, b.x_sq, *b.h, *b.h2, *b.decay]
        loads = [
            (w_raw, a["w_tok"]), (ln_w, a["ln_w"]), (ln_b, a["ln_b"]), (b_tok, a["b_tok"].broadcast_to([ROWS[0], D])),
            (b.pos[:], a["pos"]), (b.a_neg[:, 0, :], a["a_log"][0:LO]),
            (b1, a["b_1"].broadcast_to([128, 1])),
            (w1c[:, 0:1], a["w_1"][0:LO]), (b.wd[:, 0:1], a["w_d"][0:LO]), (b.bd[:, 0:1], a["b_d"][0:LO]),
            (b.e_bias[:], a["e_bias"].broadcast_to([128, E])), (b.ws_d[:], a["ws_d"]),
            (b.wg[:, 0, :], a["wg_t"][0:LO]), (b.ws_g[:, 0, :], a["ws_g"][0:LO]), (b.ws_u[:, 0, :], a["ws_u"][0:LO]),
        ]
        for half in range(2):
            at = slice(HI * half, HI * half + HI)
            loads += [
                (b.a_neg[at, 1, :], a["a_log"][LO:D]), (w1c[at, 1:2], a["w_1"][LO:D]),
                (b.wd[at, 1:2], a["w_d"][LO:D]), (b.bd[at, 1:2], a["b_d"][LO:D]),
                (b.wg[at, 1 + half, :], a["wg_t"][LO:D]), (b.ws_g[at, 1 + half, :], a["ws_g"][LO:D]),
                (b.ws_u[at, 1 + half, :], a["ws_u"][LO:D]),
            ]
            for c in range(2):
                col = slice(32 * c + 16 * half, 32 * c + 16 * half + 16)
                loads += [
                    (b.wbc[:, half, col], a["w_bc_t"][0:LO, 16 * c:16 * c + 16]),
                    (b.wbc[at, 2, col], a["w_bc_t"][LO:D, 16 * c:16 * c + 16]),
                    (b.bc_bias[16 * half:16 * half + 16, c:c + 1], a["b_bc"][16 * c:16 * c + 16]),
                ]
        with nc.Block() as block:

            @block.gpsimd
            def _(pool):
                pool.wait_ge(filled, len(zero_tiles))
                for tile in (b.ident, b.ident_bf):
                    nc.gpsimd.affine_select(out=tile[:], in_=tile[:], compare_op=ALU.not_equal, fill=1.0, base=0,
                                            pattern=[[-1, 128]], channel_multiplier=1).then_inc(made, 1)
                for part in range(3):
                    pool.wait_ge(made, 2 + part)
                    rows = b.pick[32 * part:32 * part + 32, :]
                    nc.gpsimd.affine_select(out=rows, in_=rows, compare_op=ALU.not_equal, fill=1.0, base=0,
                                            pattern=[[-1, 32]], channel_multiplier=1).then_inc(made, 1)
                pool.wait_ge(made, 5)

            @block.sync
            def _(sp):
                sp.wait_ge(filled, len(zero_tiles))
                for to, source in loads:
                    sp.dma_start(to, source).then_inc(loaded, 16)
                for k in range(2):
                    rows = slice(T_ALL + HALF * k, T_ALL + HALF * k + HALF)
                    sp.dma_start(dram_x[rows], b.zeros[0:HALF, 0:XW]).then_inc(padded, 16)
                    sp.dma_start(out[rows], b.zeros[0:HALF, 0:D]).then_inc(padded, 16)
                sp.wait_ge(padded, 64)

            @block.vector
            def _(dve):
                done = [0]

                def step(ins):
                    done[0] += 1
                    ins.then_inc(prepared, 1)
                    dve.wait_ge(prepared, done[0])

                for tile in zero_tiles:
                    nc.vector.memset(tile[:], 0.0).then_inc(filled, 1)
                step(nc.vector.memset(b.ones[:], 1.0))
                step(nc.vector.memset(mean_w, 1.0 / PATCH))
                step(nc.vector.memset(b.w_tok[:, :, D:D + 2], 1.0))
                dve.wait_ge(loaded, 16 * len(loads))
                for c in range(PC):
                    step(nc.vector.tensor_scalar(b.w_tok[:, c, 0:D], w_raw[:, c, :], ln_w[:, c:c + 1], None, ALU.mult))
                for c in range(PC):
                    step(nc.vector.tensor_scalar(b.xf[:].rearrange("p a b -> p (a b)")[:, 128 * c:128 * c + 128],
                                                 b.ones[:], ln_b[:, c:c + 1], None, ALU.mult))
                dve.wait_ge(mean_full, 1)
                step(nc.vector.tensor_tensor(b.w_tok[:, :, 0:D], b.w_tok[:, :, 0:D],
                                             b.ps[:, 0, 0:D].unsqueeze(1).broadcast_to([128, PC, D]), ALU.subtract))
                dve.wait_ge(bias_full, 1)
                for k in range(2):
                    step(nc.vector.tensor_tensor(b.pos[:, k, :], b.pos[:, k, :], b.ps[0:ROWS[0], 1, 0:D], ALU.add))
                    step(nc.vector.tensor_tensor(b.pos[:, k, :], b.pos[:, k, :], b_tok, ALU.add))
                dve.wait_ge(made, 5)
                for half in range(2):
                    step(nc.vector.tensor_copy(b.pick2[:, :, HI * half:HI * half + HI],
                                               b.pick[:, N * half:N * half + N].unsqueeze(2).broadcast_to([96, N, HI])))
                dve.wait_ge(a_exp, 1)
                step(nc.vector.tensor_scalar(b.a_neg[:], b.a_neg[:], -1.0, None, ALU.mult))
                step(nc.vector.scalar_tensor_tensor(b.bd[:], b.wd[:], b1, b.bd[:], ALU.mult, ALU.add))
                step(nc.vector.tensor_scalar(b.ws_d[:], b.ws_d[:], 0.5, None, ALU.mult))
                low, high = slice(0, HI), slice(HI, 128)
                for k, rows, cols, col in ((0, slice(0, 128), slice(0, 128), 0), (1, slice(0, 128), low, 0), (2, slice(0, 128), high, 0),
                                           (3, low, slice(0, 128), 1), (4, high, slice(0, 128), 1), (5, low, low, 1), (5, high, high, 1)):
                    step(nc.vector.tensor_scalar(b.w1[rows, k, cols], b.ones[rows, cols], w1c[rows, col:col + 1], None, ALU.mult))

            @block.scalar
            def _(act):
                act.wait_ge(loaded, 16 * len(loads))
                nc.scalar.activation(b.a_neg[:], b.a_neg[:], ACT.Exp).then_inc(a_exp, 1)

            @block.tensor
            def _(pe):
                pe.wait_ge(prepared, 3 + PC)
                for c in range(PC):
                    mm = nc.tensor.matmul(b.ps[:, 0, 0:D], mean_w, b.w_tok[:, c, 0:D], start=(c == 0), stop=(c == PC - 1))
                mm.then_inc(mean_full, 1)
                pe.wait_ge(prepared, 3 + 2 * PC)
                for c in range(PC):
                    wide = b.xf[:].rearrange("p a b -> p (a b)")[:, 128 * c:128 * c + ROWS[0]]
                    mm = nc.tensor.matmul(b.ps[0:ROWS[0], 1, 0:D], wide, w_raw[:, c, :], start=(c == 0), stop=(c == PC - 1))
                mm.then_inc(bias_full, 1)


def phase1(nc, ctx, a, out, dram_x, dram_cnt, ident, block_end):
    b = Buffers(nc, ctx, ident, block_end)
    prepare(nc, ctx, a, out, dram_x, b)
    sem = lambda name: ctx.enter_context(nc.semaphore(name))
    ps, stat = b.ps, b.stat
    flat = ps[:].rearrange("p b c -> p (b c)")
    b_bank, c_bank = 0, 2 * 512
    gu_ps = ps[0:HC, 4:6, 0:L]
    work, sums = ps[:, 6, :], ps[:, 7, :]

    x_loaded, sq_ready, sq_used = sem("x_loaded"), sem("sq_ready"), sem("sq_used")
    txt_loaded = [sem(f"txt_loaded{p}") for p in range(2)]
    work_full, work_free = sem("work_full"), sem("work_free")
    sums_full, sums_free = sem("sums_full"), sem("sums_free")
    emb_var, emb_log, emb_r0, emb_done = sem("emb_var"), sem("emb_log"), sem("emb_r0"), sem("emb_done")
    ln_centered = [sem(f"ln{k}_centered") for k in (1, 2)]
    ln_squared = [sem(f"ln{k}_squared") for k in (1, 2)]
    ln_var = [sem(f"ln{k}_var") for k in (1, 2)]
    ln_log = [sem(f"ln{k}_log") for k in (1, 2)]
    ln_r0 = [sem(f"ln{k}_r0") for k in (1, 2)]
    ln_done = [sem(f"ln{k}_done") for k in (1, 2)]
    parts_ready = sem("parts_ready")
    soft_abs, soft_exp, soft_ready, du_ready = sem("soft_abs"), sem("soft_exp"), sem("soft_ready"), sem("du_ready")
    decay_ready, scan_done = sem("decay_ready"), sem("scan_done")
    b_full, b_copied, input_ready = sem("b_full"), sem("b_copied"), sem("input_ready")
    c_full, c_used, y_added = sem("c_full"), sem("c_used"), sem("y_added")
    resid_done = sem("resid_done")
    mask_ready, factor_ready, cnt_ready = sem("mask_ready"), sem("factor_ready"), sem("cnt_ready")
    g_full, th_ready, g_used = sem("g_full"), sem("th_ready"), sem("g_used")
    u_full, inter_ready, out_ready = sem("u_full"), sem("inter_ready"), sem("out_ready")
    out_stored = [[sem(f"out_stored{p}{k}") for k in range(3)] for p in range(2)]
    rows_stored, cnt_stored = sem("rows_stored"), sem("cnt_stored")
    waited = sem("waited")
    LINKS = {"emb": 7, "ln1": 7, "ln2": 7, "bc": 4, "soft": 1, "choose": 5, "weigh": 4}
    chains = {k: sem(f"chain_{k}") for k in LINKS}

    class Chain:

        def __init__(self, eng, name, t, start=0):
            self.eng, self.sem, self.base, self.n = eng, chains[name], LINKS[name] * t.v, start

        def __call__(self, ins, alone=False):
            self.n += 1
            ins.then_inc(self.sem, 1)
            self.eng.wait_ge(self.sem, self.base + self.n)
            if alone:
                self.eng.sem_inc(waited, 1)

    def token_rows(dram, t, k):
        return dram[bass.ds(t.v * (2 * L), 2 * L)].rearrange("(b r) d -> r b d", b=2)[OFF[k]:OFF[k] + ROWS[k]]

    with nc.Block() as block:

        @block.sync
        def _(sp):
            def body(i, todo, use):
                for kind, lag, k in todo:
                    t = i.plus(-lag)
                    if kind == "load_x":
                        wait(sp, emb_var, t.v)
                        sp.dma_start(b.x_in[:], a["x"][bass.ds(t.v * 2, 2)].rearrange("b p c t -> p b c t")).then_inc(x_loaded, 16)
                    elif kind == "load_txt":
                        wait(sp, resid_done, t.v - 1)
                        sp.dma_start(b.h[t.p][:, :, 2, :], a["txt"][bass.ds(t.v * 2, 2)].rearrange("b r d -> r b d")).then_inc(txt_loaded[t.p], 16)
                    elif kind == "store_out":
                        sp.wait_ge(sums_free, use("down", k))
                        sp.dma_start(token_rows(out, t, k), b.h2[t.p][0:ROWS[k], :, k, :]).then_inc(out_stored[t.p][k], 16)
                    elif kind == "store_mid":
                        sp.wait_ge(factor_ready, t.v + 1)
                        for c in range(3):
                            sp.dma_start(token_rows(dram_x, t, c), b.x2[0:ROWS[c], :, c, :]).then_inc(rows_stored, 16)
                        sp.wait_ge(cnt_ready, t.v + 1)
                        sp.dma_start(dram_cnt.rearrange("(e b) l -> e b l", e=E)[:, bass.ds(t.v * 2, 2), :],
                                     b.cnt[:].rearrange("e (b l) -> e b l", b=2)).then_inc(cnt_stored, 16)

            run_bodies(sp, "sp", body)
            for p in range(2):
                for k in range(3):
                    sp.wait_ge(out_stored[p][k], 16 * PAIRS // 2)
            sp.wait_ge(rows_stored, 48 * PAIRS)
            sp.wait_ge(cnt_stored, 16 * PAIRS)

        @block.gpsimd
        def _(pool):
            def body(i, todo, use):
                for kind, lag, n in todo:
                    t = i.plus(-lag)
                    if kind == "fill_b":
                        if n == 0:
                            pool.wait_ge(du_ready, t.v + 1)
                        pool.wait_ge(b_copied, N * t.v + n + 1)
                        wait(pool, y_added, 15 * t.v + (max(n - 4, 1) if n >= 4 else n - 3))
                        nc.gpsimd.tensor_tensor(b.state[n % 4][:], b.du[t.p][:], b.b_wide[n % 2][:], ALU.mult).then_inc(input_ready, 1)
                    elif kind == "fill_c" and n > 0:
                        pool.wait_ge(c_used, N * t.v + n + 1)
                        y = b.y[t.p][:]
                        if n == 1:
                            wait(pool, resid_done, t.v - 1)
                            nc.gpsimd.tensor_tensor(y, b.state[0][:], b.state[1][:], ALU.add).then_inc(y_added, 1)
                        else:
                            pool.wait_ge(y_added, 15 * t.v + n - 1)
                            nc.gpsimd.tensor_tensor(y, y, b.state[n % 4][:], ALU.add).then_inc(y_added, 1)

            run_bodies(pool, "pool", body)

        @block.scalar
        def _(act):
            def rsqrt_guess(m, rows, cols, var_sem, log_sem, out_sem, t):
                act.wait_ge(var_sem, t.v + 1)
                nc.scalar.activation(stat[0:rows, m, 5, 0:cols], stat[0:rows, m, 4, 0:cols], ACT.Ln).then_inc(log_sem, 1)
                act.wait_ge(log_sem, t.v + 1)
                nc.scalar.activation(stat[0:rows, m, 5, 0:cols], stat[0:rows, m, 5, 0:cols], ACT.Exp, scale=-0.5).then_inc(out_sem, 1)

            def body(i, todo, use):
                for kind, lag, k in todo:
                    t = i.plus(-lag)
                    if kind == "decay":
                        if k == 0:
                            act.wait_ge(du_ready, t.v + 1)
                        wait(act, scan_done, N * t.v + k - 1)
                        to = b.decay[k % 2]
                        nc.scalar.activation(to[:, 0:2, 1:L], b.delta[t.p][:, 0:2, 1:L], ACT.Exp, scale=b.a_neg[:, 0, k:k + 1])
                        nc.scalar.activation(to[:, 2, 1:L], b.delta[t.p][:, 2, 1:L], ACT.Exp, scale=b.a_neg[:, 1, k:k + 1]).then_inc(decay_ready, 1)
                    elif kind == "fill_b":
                        act.wait_ge(b_full, N * t.v + k + 1)
                        wait(act, input_ready, N * t.v + k - 1)
                        nc.scalar.activation(b.b_wide[k % 2][:].rearrange("p a t -> p (a t)"), flat[:, b_bank:b_bank + 3 * L], ACT.Copy).then_inc(b_copied, 1)
                    elif kind == "emb_a":
                        act.wait_ge(x_loaded, 16 * t.v + 16)
                        wait(act, sq_used, 2 * t.v + k)
                        nc.scalar.activation(b.x_sq[:], b.x_in[:, k], ACT.Square).then_inc(sq_ready, 1)
                    elif kind == "emb":
                        act.wait_ge(sums_full, use(kind, k))
                        if k == 0:
                            wait(act, emb_done, t.v)
                        nc.scalar.activation(b.emb[:, k].rearrange("p a b -> p (a b)"), sums[0:ROWS[0], 0:392], ACT.Copy).then_inc(sums_free, 1)
                    elif kind == "emb_stats":
                        rsqrt_guess(0, ROWS[0], 4, emb_var, emb_log, emb_r0, t)
                    elif kind in ("ln1_center", "ln2_center"):
                        m = int(kind[2]) - 1
                        act.wait_ge(ln_centered[m], t.v + 1)
                        if m == 0:
                            wait(act, ln_var[1], t.v - 1)
                        else:
                            wait(act, parts_ready, min(t.v + 2, PAIRS) if isinstance(t.v, int) else t.v + 2)
                        centered = b.xn[:] if m == 0 else b.x2[:, :, :, 0:D]
                        nc.scalar.activation(b.ln_sq[:], centered, ACT.Square).then_inc(ln_squared[m], 1)
                    elif kind in ("ln1_var", "ln2_var"):
                        m = int(kind[2]) - 1
                        rsqrt_guess(m + 1, 128, 6, ln_var[m], ln_log[m], ln_r0[m], t)
                    elif kind == "x1_turn":
                        act.wait_ge(work_full, use(kind, k))
                        if k == 0:
                            wait(act, du_ready, t.v)
                        nc.scalar.activation(b.xf[:, k, :], work[:, 0:L], ACT.Copy).then_inc(work_free, 1)
                    elif kind == "x2_turn":
                        act.wait_ge(work_full, use(kind, k))
                        if k == 0:
                            wait(act, u_full, NJ * (t.v - 1))
                        nc.scalar.activation(b.x2f[t.p][:, k, :], work[:, 0:L], ACT.Copy).then_inc(work_free, 1)
                    elif kind == "bc_values":
                        act.wait_ge(work_full, use(kind, k))
                        wait(act, parts_ready, t.v)
                        nc.scalar.activation(b.bcv[:, 0, :], work[0:32, 0:L], ACT.Identity, bias=b.bc_bias[:, 0:1])
                        nc.scalar.activation(b.bcv[:, 1, :], work[32:64, 0:L], ACT.Identity, bias=b.bc_bias[:, 1:2]).then_inc(work_free, 1)
                    elif kind == "step_size":
                        col = 1 if k == 2 else 0
                        act.wait_ge(work_full, use(kind, k))
                        if k == 0:
                            wait(act, du_ready, t.v)
                            wait(act, decay_ready, N * (t.v - 1))
                        scale, bias = b.wd[:, col:col + 1], b.bd[:, col:col + 1]
                        nc.scalar.activation(b.soft[:, k, :], work[:, 0:L], ACT.Abs, scale=scale, bias=bias).then_inc(soft_abs, 1)
                        nc.scalar.activation(b.delta[t.p][:, k, :], work[:, 0:L], ACT.Relu, scale=scale, bias=bias).then_inc(work_free, 1)
                    elif kind == "softplus":
                        act.wait_ge(soft_abs, 3 * t.v + 3)
                        nc.scalar.activation(b.soft[:], b.soft[:], ACT.Exp, scale=-1.0).then_inc(soft_exp, 1)
                        act.wait_ge(soft_exp, t.v + 1)
                        nc.scalar.activation(b.soft[:], b.soft[:], ACT.Ln, bias=1.0).then_inc(soft_ready, 1)
                    elif kind == "gate":
                        act.wait_ge(work_full, use(kind, k))
                        if k == 0:
                            wait(act, factor_ready, t.v)
                        nc.scalar.activation(b.gt[0:98, 3 * k:3 * k + 2, :], work[0:98, 0:256].rearrange("p (k e) -> p k e", k=2), ACT.Tanh, scale=0.5)
                        nc.scalar.activation(b.gt[:, 3 * k + 2, :], work[:, 256:384], ACT.Tanh, scale=0.5).then_inc(work_free, 1)
                    elif kind == "up_g":
                        act.wait_ge(g_full, NJ * t.v + k + 1)
                        wait(act, g_used, NJ * t.v + k)
                        nc.scalar.activation(b.th[:], gu_ps, ACT.Tanh, scale=0.5).then_inc(th_ready, 1)

            run_bodies(act, "act", body)

        @block.vector
        def _(dve):
            def newton(m, rows, cols, link):
                s = stat[0:rows, m, :, 0:cols]
                link(nc.vector.tensor_tensor(s[:, 0, :], s[:, 5, :], s[:, 5, :], ALU.mult))
                link(nc.vector.scalar_tensor_tensor(s[:, 1, :], s[:, 0, :], -0.5, s[:, 4, :], ALU.mult, ALU.mult))
                link(nc.vector.scalar_tensor_tensor(s[:, 3, :], s[:, 1, :], 1.5, s[:, 5, :], ALU.add, ALU.mult))
                return s[:, 3, :]

            def body(i, todo, use):
                for kind, lag, k in todo:
                    t = i.plus(-lag)
                    if kind == "scan":
                        dve.wait_ge(decay_ready, N * t.v + k + 1)
                        dve.wait_ge(input_ready, N * t.v + k + 1)
                        s = b.state[k % 4][:].rearrange("p a t -> p (a t)")
                        nc.vector.tensor_tensor_scan(s, b.decay[k % 2][:].rearrange("p a t -> p (a t)"), s, 0.0,
                                                     ALU.mult, ALU.add).then_inc(scan_done, 1)
                    elif kind == "fill_c":
                        dve.wait_ge(c_full, N * t.v + k + 1)
                        dve.wait_ge(scan_done, N * t.v + k + 1)
                        s = b.state[k % 4][:].rearrange("p a t -> p (a t)")
                        nc.vector.tensor_tensor(s, s, flat[:, c_bank:c_bank + 3 * L], ALU.mult).then_inc(c_used, 1)
                    elif kind == "down":
                        dve.wait_ge(sums_full, use(kind, k))
                        r, to = ROWS[k], b.h2[t.p]
                        ins = nc.vector.tensor_tensor(to[0:r, :, k, :], to[0:r, :, k, :], sums[0:r, 0:2 * D].rearrange("p (b d) -> p b d", b=2), ALU.add)
                        ins.then_inc(sums_free, 1)
                        if k == 2:
                            dve.wait_ge(sums_free, use(kind, k))
                            nc.vector.memset(stat[0:1, 0, 2, 4:5], 0.0).then_inc(out_ready, 1)
                    elif kind == "resid":
                        dve.wait_ge(work_full, use(kind, k))
                        wait(dve, out_stored[t.p][k], 16 * t.h)
                        r = ROWS[k]
                        nc.vector.tensor_tensor(b.h2[t.p][0:r, :, k, 0:LO], b.h[t.p][0:r, :, k, 0:LO],
                                                work[0:r, 0:2 * LO].rearrange("p (b d) -> p b d", b=2), ALU.add)
                        nc.vector.tensor_tensor(b.h2[t.p][0:r, :, k, LO:D], b.h[t.p][0:r, :, k, LO:D],
                                                work[0:r, 2 * LO:2 * LO + 2 * HI].rearrange("p (b d) -> p b d", b=2), ALU.add).then_inc(work_free, 1)
                        if k == 2:
                            dve.wait_ge(work_free, use(kind, k))
                            nc.vector.memset(stat[0:1, 0, 2, 5:6], 0.0).then_inc(resid_done, 1)
                    elif kind == "emb_stats":
                        dve.wait_ge(sums_free, use("emb", 1))
                        link = Chain(dve, "emb", t)
                        col = lambda c: b.emb[:, :, :, c:c + 1].rearrange("p b k c -> p (b k) c")[:, :, 0]
                        s = stat[0:ROWS[0], 0, :, 0:4]
                        link(nc.vector.tensor_scalar(s[:, 0, :], col(D), 1.0 / PATCH, None, ALU.mult))
                        link(nc.vector.tensor_tensor(s[:, 1, :], s[:, 0, :], s[:, 0, :], ALU.mult))
                        link(nc.vector.scalar_tensor_tensor(s[:, 2, :], col(D + 2), 1.0 / PATCH, s[:, 1, :], ALU.mult, ALU.subtract))
                        nc.vector.tensor_scalar(s[:, 4, :], s[:, 2, :], 0.0, EPS, ALU.max, ALU.add).then_inc(emb_var, 1)
                    elif kind == "emb_scale":
                        dve.wait_ge(emb_r0, t.v + 1)
                        wait(dve, resid_done, t.v - 1)
                        link = Chain(dve, "emb", t, 3)
                        r = newton(0, ROWS[0], 4, link).rearrange("p (b k) -> p b k", b=2).unsqueeze(3).broadcast_to([ROWS[0], 2, 2, D])
                        to = b.h[t.p][0:ROWS[0], :, 0:2, :]
                        link(nc.vector.tensor_tensor(to, b.emb[:, :, :, 0:D], r, ALU.mult))
                        nc.vector.tensor_tensor(to, to, b.pos[:].unsqueeze(1).broadcast_to([ROWS[0], 2, 2, D]), ALU.add).then_inc(emb_done, 1)
                    elif kind in ("ln1_center", "ln2_center"):
                        m = int(kind[2]) - 1
                        if m == 0:
                            dve.wait_ge(emb_done, t.v + 1)
                            dve.wait_ge(txt_loaded[t.p], 16 * t.h + 16)
                            wait(dve, du_ready, t.v)
                            source, to = b.h[t.p][:], b.xn[:]
                        else:
                            dve.wait_ge(resid_done, t.v + 1)
                            wait(dve, cnt_ready, t.v)
                            wait(dve, rows_stored, 48 * t.v)
                            source, to = b.h2[t.p][:], b.x2[:, :, :, 0:D]
                        link = Chain(dve, kind[:3], t)
                        s = stat[:, m + 1]
                        link(nc.vector.tensor_reduce(s[:, 0, :], source, AX.X, ALU.add))
                        link(nc.vector.tensor_scalar(s[:, 1, :], s[:, 0, :], 1.0 / D, None, ALU.mult))
                        mean = s[:, 1, :].rearrange("p (b k) -> p b k", b=2).unsqueeze(3).broadcast_to([128, 2, 3, D])
                        nc.vector.tensor_tensor(to, source, mean, ALU.subtract).then_inc(ln_centered[m], 1)
                    elif kind in ("ln1_var", "ln2_var"):
                        m = int(kind[2]) - 1
                        dve.wait_ge(ln_squared[m], t.v + 1)
                        s = stat[:, m + 1]
                        link = Chain(dve, kind[:3], t, 2)
                        link(nc.vector.tensor_reduce(s[:, 2, :], b.ln_sq[:], AX.X, ALU.add))
                        nc.vector.tensor_scalar(s[:, 4, :], s[:, 2, :], 1.0 / D, EPS, ALU.mult, ALU.add).then_inc(ln_var[m], 1)
                    elif kind in ("ln1_scale", "ln2_scale"):
                        m = int(kind[2]) - 1
                        dve.wait_ge(ln_r0[m], t.v + 1)
                        link = Chain(dve, kind[:3], t, 3)
                        r = newton(m + 1, 128, 6, link).rearrange("p (b k) -> p b k", b=2)
                        x = b.xn if m == 0 else b.x2
                        link(nc.vector.tensor_tensor(b.xm[m][:].rearrange("p k b d -> p b k d"), x[:, :, :, LO:D], r.unsqueeze(3).broadcast_to([128, 2, 3, HI]), ALU.mult))
                        if m == 0:
                            nc.vector.tensor_tensor(x[:, :, :, 0:LO], x[:, :, :, 0:LO], r.unsqueeze(3).broadcast_to([128, 2, 3, LO]), ALU.mult).then_inc(ln_done[m], 1)
                        else:
                            nc.vector.tensor_tensor(x[:, :, :, 0:D], x[:, :, :, 0:D], r.unsqueeze(3).broadcast_to([128, 2, 3, D]), ALU.mult).then_inc(ln_done[m], 1)
                    elif kind == "bc_values":
                        dve.wait_ge(work_free, use(kind, k))
                        wait(dve, c_full, N * (t.v - 1))
                        p, v = b.parts[t.p], b.bcv
                        link = Chain(dve, "bc", t)
                        link(nc.vector.tensor_copy(p[0:32], v))
                        link(nc.vector.tensor_tensor(v, v, p[0:32], ALU.subtract))
                        link(nc.vector.tensor_copy(b.mid_part[:], v))
                        nc.vector.tensor_copy(p[32:64], b.mid_part[:])
                        link(nc.vector.tensor_tensor(v, v, b.mid_part[:], ALU.subtract))
                        nc.vector.tensor_copy(p[64:96], v).then_inc(parts_ready, 1)
                    elif kind == "softplus":
                        dve.wait_ge(soft_ready, t.v + 1)
                        dve.wait_ge(work_free, use("step_size", 2))
                        wait(dve, input_ready, N * (t.v - 1))
                        link = Chain(dve, "soft", t)
                        link(nc.vector.tensor_tensor(b.delta[t.p][:], b.delta[t.p][:], b.soft[:], ALU.add))
                        nc.vector.tensor_tensor(b.du[t.p][:], b.delta[t.p][:], b.xf[:], ALU.mult).then_inc(du_ready, 1)
                    elif kind == "choose":
                        dve.wait_ge(work_free, use("gate", 1))
                        wait(dve, cnt_ready, t.v)
                        link = Chain(dve, "choose", t)
                        link(nc.vector.tensor_scalar(b.gt[:], b.gt[:], 0.5, 0.5, ALU.mult, ALU.add))
                        link(nc.vector.tensor_tensor(b.ch[:], b.gt[:], b.e_bias[:].unsqueeze(1).broadcast_to([128, 6, E]), ALU.add), alone=True)
                        for c in range(6):
                            ins = nc.vector.max(b.top8[:, c, :], b.ch[:, c, :])
                        link(ins)
                        link(nc.vector.memset(b.top8[:, :, TOPK:8], -BIG), alone=True)
                        for c in range(6):
                            ins = nc.vector.match_replace(b.ch[:, c, :], b.top8[:, c, :], b.ch[:, c, :], BIG)
                        link(ins)
                        nc.vector.tensor_scalar(b.mask[:], b.ch[:], BIG / 2, None, ALU.is_ge).then_inc(mask_ready, 1)
                    elif kind == "weigh":
                        dve.wait_ge(mask_ready, t.v + 1)
                        link = Chain(dve, "weigh", t)
                        den = b.top8[:, :, 0]
                        link(nc.vector.tensor_tensor(b.ch[:], b.gt[:], b.mask[:], ALU.mult))
                        link(nc.vector.tensor_reduce(den, b.ch[:], AX.X, ALU.add))
                        link(nc.vector.tensor_scalar(den, den, 1e-20, None, ALU.add))
                        link(nc.vector.reciprocal(b.top8[:, :, 1], den))
                        nc.vector.tensor_scalar(b.x2[:, :, :, D], b.top8[:, :, 1].rearrange("p (b k) -> p b k", b=2), SCALE / 4, None, ALU.mult).then_inc(factor_ready, 1)
                    elif kind == "count":
                        dve.wait_ge(work_full, use(kind, k))
                        wait(dve, cnt_ready, t.v)
                        wait(dve, cnt_stored, 16 * t.v)
                        nc.vector.tensor_tensor_scan(b.cnt[:], work.bitcast(BF16)[:, 0:2 * L], b.zeros[:], b.run[:, 0:1], ALU.add, ALU.add).then_inc(work_free, 1)
                        dve.wait_ge(work_free, use(kind, k))
                        nc.vector.tensor_copy(b.run[:], b.cnt[:, 2 * L - 1:2 * L])
                        nc.vector.tensor_copy(b.block_end[:, bass.ds(t.v * 2, 2)], b.cnt[:, L - 1:2 * L:L]).then_inc(cnt_ready, 1)
                    elif kind == "up_g":
                        dve.wait_ge(th_ready, NJ * t.v + k + 1)
                        wait(dve, inter_ready, NJ * t.v + k)
                        nc.vector.scalar_tensor_tensor(b.ag[:], b.th[:], 1.0, gu_ps, ALU.add, ALU.mult).then_inc(g_used, 1)
                    elif kind == "up_u":
                        dve.wait_ge(u_full, NJ * t.v + k + 1)
                        dve.wait_ge(g_used, NJ * t.v + k + 1)
                        if k == 0:
                            wait(dve, out_ready, t.v)
                        nc.vector.tensor_tensor(b.inter[:, k], b.ag[:], gu_ps, ALU.mult).then_inc(inter_ready, 1)

            run_bodies(dve, "dve", body)

        @block.tensor
        def _(pe):
            def both(to, weights, tiles, batch, cols):
                nc.tensor.matmul(to, weights[:, 0, cols], tiles[:, batch, :], start=True, stop=False)
                return nc.tensor.matmul(to, weights[:, 1 + batch, cols], tiles[:, 2, :], start=False, stop=True)

            def spread(t, n, c, bank):
                rhs, edge = b.parts[t.p][:, c, :], 512 - L
                row = lambda q: b.pick[:, 16 * q + n:16 * q + n + 1].broadcast_to([96, 128])
                to = lambda first, last: flat[:, bank + first:bank + last]
                nc.tensor.matmul(to(0, L), row(0), rhs, start=True, stop=True)
                nc.tensor.matmul(to(L, 512), row(1), rhs[:, 0:edge], start=True, stop=True)
                nc.tensor.matmul(to(512, 2 * L), row(1), rhs[:, edge:L], start=True, stop=True)
                return nc.tensor.matmul(to(2 * L, 3 * L), b.pick2[:, n, :], rhs, start=True, stop=True)

            def body(i, todo, use):
                for kind, lag, k in todo:
                    t = i.plus(-lag)
                    if BANK.get(kind) == WORK:
                        wait(pe, work_free, use(kind, k) - 1)
                    elif kind in ("down_a", "emb_a"):
                        wait(pe, sums_free, use(kind[:-2], k) - 1)
                    if kind == "fill_b":
                        if k == 0:
                            pe.wait_ge(parts_ready, t.v + 1)
                        wait(pe, b_copied, N * t.v + k)
                        spread(t, k, 0, b_bank).then_inc(b_full, 1)
                    elif kind == "fill_c":
                        wait(pe, c_used, N * t.v + k)
                        spread(t, k, 1, c_bank).then_inc(c_full, 1)
                    elif kind in ("down_a", "down"):
                        pe.wait_ge(inter_ready, NJ * (t.v + 1))
                        q = 0 if kind == "down_a" else 1
                        for j in range(NJ):
                            mm = nc.tensor.matmul(sums[0:ROWS[k], D * q:D * q + D], b.inter[:, j, q, OFF[k]:OFF[k] + ROWS[k]], b.ws_d[:, j, :],
                                                  start=(j == 0), stop=(j == NJ - 1))
                        if q == 1:
                            mm.then_inc(sums_full, 1)
                    elif kind == "resid":
                        pe.wait_ge(y_added, 15 * (t.v + 1))
                        for q in range(3):
                            mm = nc.tensor.transpose(work[0:ROWS[k], 128 * q:128 * q + 128], b.y[t.p][:, q, OFF[k]:OFF[k] + ROWS[k]], b.ident[:])
                        mm.then_inc(work_full, 1)
                    elif kind in ("x1_turn", "x2_turn"):
                        m = int(kind[1]) - 1
                        pe.wait_ge(ln_done[m], t.v + 1)
                        x = (b.xn, b.x2)[m]
                        for c in range(3):
                            r = ROWS[c]
                            source = x[0:r, k, c, 0:LO] if k < 2 else b.xm[m][0:r, c].rearrange("p b d -> p (b d)")
                            mm = nc.tensor.transpose(work[:, OFF[c]:OFF[c] + r], source, b.ident[0:r, 0:r])
                        mm.then_inc(work_full, 1)
                    elif kind == "gate":
                        for c in range(3):
                            to, at = work[0:ROWS[c], E * c:E * c + E], slice(OFF[c], OFF[c] + ROWS[c])
                            nc.tensor.matmul(to, b.x2f[t.p][:, k, at], b.wg[:, 0, :], start=True, stop=False)
                            mm = nc.tensor.matmul(to, b.x2f[t.p][:, 2, at], b.wg[:, 1 + k, :], start=False, stop=True)
                        mm.then_inc(work_full, 1)
                    elif kind == "count":
                        pe.wait_ge(mask_ready, t.v + 1)
                        turned = work.bitcast(BF16)
                        for q in range(2):
                            for c in range(3):
                                r = ROWS[c]
                                mm = nc.tensor.transpose(turned[:, L * q + OFF[c]:L * q + OFF[c] + r], b.mask[0:r, 3 * q + c, :], b.ident_bf[0:r, 0:r])
                        mm.then_inc(work_full, 1)
                    elif kind in ("emb_a", "emb"):
                        pe.wait_ge(sq_ready, 2 * t.v + k + 1)
                        c = 0 if kind == "emb_a" else 1
                        at = slice(98 * c, 98 * c + 98)
                        for f in range(PC):
                            mm = nc.tensor.matmul(sums[0:98, 196 * c + D + 2:196 * c + D + 4], b.x_sq[:, f, at], b.ones[:, 0:2], start=(f == 0), stop=(f == PC - 1))
                        if c == 1:
                            mm.then_inc(sq_used, 1)
                        for f in range(PC):
                            mm = nc.tensor.matmul(sums[0:98, 196 * c:196 * c + D + 2], b.x_in[:, k, f, at], b.w_tok[:, f, :], start=(f == 0), stop=(f == PC - 1))
                        if c == 1:
                            mm.then_inc(sums_full, 1)
                    elif kind == "bc_values":
                        for q in range(3):
                            mm = nc.tensor.matmul(work[0:64, 0:L], b.wbc[:, q, :], b.xf[:, q, :], start=(q == 0), stop=(q == 2))
                        mm.then_inc(work_full, 1)
                    elif kind == "step_size":
                        terms = (((0, 0), (3, 2)), ((0, 1), (4, 2)), ((1, 0), (2, 1), (5, 2)))[k]
                        for n, (w, q) in enumerate(terms):
                            mm = nc.tensor.matmul(work[:, 0:L], b.w1[:, w, :], b.xf[:, q, :], start=(n == 0), stop=(n == len(terms) - 1))
                        mm.then_inc(work_full, 1)
                    elif kind == "up_g":
                        pe.wait_ge(factor_ready, t.v + 1)
                        wait(pe, inter_ready, NJ * t.v + k)
                        for q in range(2):
                            mm = both(gu_ps[:, q, :], b.ws_g, b.x2f[t.p], q, slice(HC * k, HC * k + HC))
                        mm.then_inc(g_full, 1)
                    elif kind == "up_u":
                        pe.wait_ge(g_used, NJ * t.v + k + 1)
                        for q in range(2):
                            mm = both(gu_ps[:, q, :], b.ws_u, b.x2f[t.p], q, slice(HC * k, HC * k + HC))
                        mm.then_inc(u_full, 1)

            run_bodies(pe, "pe", body)


EXPERT_ORDER = [
    ("load_up", -1), ("token", -2), ("row", -3), ("up_g", 0), ("down", 1), ("load_down", -1),
    ("up_u", 0), ("scatter", 1), ("turn", -1),
]
E_FIRST, E_FROM, E_TO, E_LAST = -3, 3, 125, E


def run_experts(eng, body):
    def todo(i):
        return [x for x in EXPERT_ORDER if 0 <= i - x[1] < E]

    for i in range(E_FIRST, E_FROM):
        body(Turn.fixed(i), todo(i))
    with eng.Fori(0, (E_TO - E_FROM) // 2) as r:
        for q in range(2):
            start = Turn.fixed(E_FROM + q)
            body(Turn(start.v + 2 * r, start.p, start.h + r), EXPERT_ORDER)
    for i in range(E_TO, E_LAST + 1):
        body(Turn.fixed(i), todo(i))


def phase2(nc, ctx, a, out, dram_x, dram_cnt, ident, block_end):
    sb = lambda name, shape, dt=F32: ctx.enter_context(nc.sbuf_tensor(name, shape, dt))
    sem = lambda name: ctx.enter_context(nc.semaphore(name))
    KC = D // 2
    slot_int = sb("slot_int", [128, CAP], U32)
    slot = sb("slot", [128, CAP])
    lane_int = sb("lane_int", [128, 3], U32)
    lane = sb("lane", [128, 3])
    less = sb("less", [E, HALF, B])
    block_of = sb("block_of", [E, 2, 2, HALF])
    base = sb("base", [HALF, 2, E])
    row = sb("row", [HALF, 2, E])
    tokens = sb("tokens", [HALF, 2, E])
    two = lambda name, shape, dt=F32: [sb(f"{name}{p}", shape, dt) for p in range(2)]
    row_idx, gather_idx, scatter_idx = (two(n, [HALF, 2], U32) for n in ("row_idx", "gather_idx", "scatter_idx"))
    counts = two("counts", [HALF, 2, L])
    passed = sb("passed", [HALF, 2, L])
    tk = sb("tk", [HALF, 3, 2])
    xg = two("xg", [HALF, 2, XW])
    xgt = two("xgt", [KC, 2, CAP])
    w_up = two("w_up", [KC, 2, 2 * HID + 1])
    w_down = two("w_down", [HC, NF, D])
    tw = sb("tw", [HALF, 2])
    weight = two("weight", [HALF, 2])
    th = sb("e_th", [HC, 2, 2 * CAP])
    ag = sb("e_ag", [HC, 2, 2 * CAP])
    inter = sb("e_inter", [HC, 2, 2 * CAP])
    yo = two("yo", [HALF, 2, D])
    ps = ctx.enter_context(nc.psum_tensor("e_ps", [128, 8, 512], F32))
    g_ps, u_ps = ps[0:HC, 0:2, 0:2 * CAP], ps[0:HC, 2:4, 0:2 * CAP]

    iota_done, slots_ready, found, turned_in, table_ready = (sem(n) for n in ("iota_done", "slots_ready", "found", "turned_in", "table_ready"))

    with nc.Block() as block:

        @block.gpsimd
        def _(pool):
            nc.gpsimd.iota(slot_int[:], [[1, CAP]], base=0, channel_multiplier=0).then_inc(iota_done, 1)
            nc.gpsimd.iota(lane_int[:, 0:1], [[0, 1]], base=0, channel_multiplier=B).then_inc(iota_done, 1)
            nc.gpsimd.iota(lane_int[:, 1:3], [[HALF, 2]], base=0, channel_multiplier=1).then_inc(iota_done, 1)

        @block.vector
        def _(dve):
            n = [0]

            def step(ins):
                n[0] += 1
                ins.then_inc(found, 1)
                dve.wait_ge(found, n[0])

            dve.wait_ge(iota_done, 3)
            step(nc.vector.tensor_copy(slot[:], slot_int[:]))
            step(nc.vector.tensor_copy(lane[:], lane_int[:]))
            for q in range(2):
                step(nc.vector.tensor_tensor(less[:], block_end[:].unsqueeze(1).broadcast_to([E, HALF, B]),
                                             slot[:, HALF * q:HALF * q + HALF].unsqueeze(2).broadcast_to([E, HALF, B]), ALU.is_le))
                step(nc.vector.tensor_reduce(block_of[:, q, 0, :], less[:], AX.X, ALU.add))
                step(nc.vector.tensor_scalar(block_of[:, q, 0, :], block_of[:, q, 0, :], B - 1.0, None, ALU.min))
                step(nc.vector.tensor_scalar(block_of[:, q, 1, :], block_of[:, q, 0, :], lane[:, 0:1], None, ALU.add))
            nc.vector.tensor_copy(tk[:, 0, :], lane[0:HALF, 1:3]).then_inc(slots_ready, 1)
            dve.wait_ge(turned_in, 1)
            step(nc.vector.tensor_scalar(base[:], ps[0:HALF, 0, 0:2 * E].rearrange("p (q e) -> p q e", q=2), float(L), None, ALU.mult))
            step(nc.vector.tensor_copy(row[:], ps[0:HALF, 0, 2 * E:4 * E].rearrange("p (q e) -> p q e", q=2)))

        @block.tensor
        def _(pe):
            pe.wait_ge(slots_ready, 1)
            for c in range(2):
                for q in range(2):
                    mm = nc.tensor.transpose(ps[0:HALF, 0, (2 * c + q) * E:(2 * c + q + 1) * E], block_of[:, q, c, :], ident[:])
            mm.then_inc(turned_in, 1)

    up_loaded = [sem(f"up_loaded{p}") for p in range(2)]
    down_loaded = [sem(f"down_loaded{p}") for p in range(2)]
    row_ready, counts_loaded = sem("row_ready"), [sem(f"counts_loaded{p}") for p in range(2)]
    passed_ready, sum_ready, token_steps = sem("passed_ready"), sem("sum_ready"), sem("token_steps")
    token_ready, x_gathered = sem("token_ready"), [sem(f"x_gathered{p}") for p in range(2)]
    turn_full, xgt_ready, gate_full, tw_ready, weight_ready = (sem(n) for n in ("turn_full", "xgt_ready", "gate_full", "tw_ready", "weight_ready"))
    e_g_full, e_th_ready, e_g_used, e_u_full, e_inter_ready = (sem(n) for n in ("e_g_full", "e_th_ready", "e_g_used", "e_u_full", "e_inter_ready"))
    down_full, yo_ready, scatter_ready = sem("down_full"), sem("yo_ready"), sem("scatter_ready")
    added = [sem(f"added{p}") for p in range(2)]
    waited = sem("e_waited")

    with nc.Block() as block:

        @block.sync
        def _(sp):
            def body(i, todo):
                for kind, lag in todo:
                    t = i.plus(-lag)
                    if kind == "load_up":
                        wait(sp, e_u_full, t.v - 1)
                        sp.dma_start(w_up[t.p][:], a["we_up"][bass.ds(t.v, 1)].rearrange("o p c f -> p (o c) f")).then_inc(up_loaded[t.p], 16)
                    elif kind == "load_down":
                        wait(sp, down_full, t.v - 1)
                        sp.dma_start(w_down[t.p][:], a["we_down"][bass.ds(t.v, 1)].rearrange("o p c f -> p (o c) f")).then_inc(down_loaded[t.p], 16)

            run_experts(sp, body)

        @block.gpsimd
        def _(pool):
            def body(i, todo):
                for kind, lag in todo:
                    t = i.plus(-lag)
                    if kind == "row":
                        pool.wait_ge(row_ready, t.v + 1)
                        wait(pool, passed_ready, t.v - 1)
                        pool.sem_inc(waited, 1)
                        for q in range(2):
                            nc.gpsimd.indirect_dma_start(counts[t.p][:, q, :], None, dram_cnt, bass.IndirectOffsetOnAxis(ap=row_idx[t.p][:, q:q + 1], axis=0)).then_inc(counts_loaded[t.p], 16)
                    elif kind == "token":
                        pool.wait_ge(token_ready, t.v + 1)
                        wait(pool, weight_ready, t.v - 1)
                        pool.sem_inc(waited, 1)
                        for q in range(2):
                            nc.gpsimd.indirect_dma_start(xg[t.p][:, q, :], None, dram_x, bass.IndirectOffsetOnAxis(ap=gather_idx[t.p][:, q:q + 1], axis=0)).then_inc(x_gathered[t.p], 16)
                    elif kind == "scatter":
                        pool.wait_ge(scatter_ready, t.v + 1)
                        pool.wait_ge(yo_ready, t.v + 1)
                        before = t.plus(-1)
                        wait(pool, added[before.p], 32 * before.h + 32)
                        pool.sem_inc(waited, 1)
                        for q in range(2):
                            nc.gpsimd.indirect_dma_start(out, bass.IndirectOffsetOnAxis(ap=scatter_idx[t.p][:, q:q + 1], axis=0), yo[t.p][:, q, :], None, compute_op=ALU.add).then_inc(added[t.p], 16)

            run_experts(pool, body)
            for p in range(2):
                pool.wait_ge(added[p], 32 * E // 2)

        @block.scalar
        def _(act):
            def body(i, todo):
                for kind, lag in todo:
                    t = i.plus(-lag)
                    if kind == "turn":
                        act.wait_ge(turn_full, t.v + 1)
                        wait(act, e_u_full, t.v - 1)
                        nc.scalar.activation(xgt[t.p][:].rearrange("p c s -> p (c s)"), ps[0:KC, 5, 0:2 * CAP], ACT.Copy).then_inc(xgt_ready, 1)
                        act.wait_ge(gate_full, t.v + 1)
                        wait(act, weight_ready, t.v)
                        nc.scalar.activation(tw[:], ps[0:HALF, 6, 0:2], ACT.Tanh, scale=0.5).then_inc(tw_ready, 1)
                    elif kind == "up_g":
                        act.wait_ge(e_g_full, t.v + 1)
                        wait(act, e_g_used, t.v)
                        nc.scalar.activation(th[:], g_ps, ACT.Tanh, scale=0.5).then_inc(e_th_ready, 1)

            run_experts(act, body)

        @block.vector
        def _(dve):
            def body(i, todo):
                for kind, lag in todo:
                    t = i.plus(-lag)
                    if kind == "row":
                        wait(dve, counts_loaded[t.p], 32 * t.h)
                        nc.vector.tensor_copy(row_idx[t.p][:], row[:, :, bass.ds(t.v, 1)].rearrange("p q o -> p (q o)")).then_inc(row_ready, 1)
                    elif kind == "token":
                        dve.wait_ge(counts_loaded[t.p], 32 * t.h + 32)
                        slots = tk[:, 0, :].unsqueeze(2).broadcast_to([HALF, 2, L])
                        nc.vector.tensor_tensor(passed[:], counts[t.p][:], slots, ALU.is_le).then_inc(passed_ready, 1)
                        dve.wait_ge(passed_ready, t.v + 1)
                        nc.vector.tensor_reduce(tk[:, 1, :], passed[:], AX.X, ALU.add).then_inc(sum_ready, 1)
                        dve.wait_ge(sum_ready, t.v + 1)
                        nc.vector.tensor_tensor(tk[:, 1, :], tk[:, 1, :], base[:, :, bass.ds(t.v, 1)].rearrange("p q o -> p (q o)"), ALU.add).then_inc(token_steps, 1)
                        dve.wait_ge(token_steps, 2 * t.v + 1)
                        nc.vector.scalar_tensor_tensor(tk[:, 2, :], tk[:, 1, :], float(T_ALL), tk[:, 0, :], ALU.is_ge, ALU.mult).then_inc(token_steps, 1)
                        dve.wait_ge(token_steps, 2 * t.v + 2)
                        wait(dve, x_gathered[t.p], 32 * t.h)
                        nc.vector.tensor_tensor(tokens[:, :, bass.ds(t.v, 1)].rearrange("p q o -> p (q o)"), tk[:, 1, :], tk[:, 2, :], ALU.add)
                        nc.vector.tensor_tensor(gather_idx[t.p][:], tk[:, 1, :], tk[:, 2, :], ALU.add).then_inc(token_ready, 1)
                    elif kind == "up_g":
                        dve.wait_ge(e_th_ready, t.v + 1)
                        wait(dve, e_inter_ready, t.v)
                        nc.vector.scalar_tensor_tensor(ag[:], th[:], 1.0, g_ps, ALU.add, ALU.mult).then_inc(e_g_used, 1)
                    elif kind == "down":
                        dve.wait_ge(down_full, t.v + 1)
                        dve.wait_ge(weight_ready, t.v + 1)
                        wait(dve, added[t.p], 32 * t.h)
                        nc.vector.tensor_tensor(yo[t.p][:], ps[0:HALF, 4, 0:2 * D].rearrange("p (q d) -> p q d", q=2),
                                                weight[t.p][:].unsqueeze(2).broadcast_to([HALF, 2, D]), ALU.mult).then_inc(yo_ready, 1)
                        nc.vector.tensor_copy(scatter_idx[t.p][:], tokens[:, :, bass.ds(t.v, 1)].rearrange("p q o -> p (q o)")).then_inc(scatter_ready, 1)
                    elif kind == "up_u":
                        dve.wait_ge(e_u_full, t.v + 1)
                        dve.wait_ge(e_g_used, t.v + 1)
                        wait(dve, down_full, t.v)
                        nc.vector.tensor_tensor(inter[:], ag[:], u_ps, ALU.mult).then_inc(e_inter_ready, 1)
                    elif kind == "turn":
                        dve.wait_ge(tw_ready, t.v + 1)
                        dve.wait_ge(x_gathered[t.p], 32 * t.h + 32)
                        wait(dve, yo_ready, t.v - 1)
                        nc.vector.scalar_tensor_tensor(weight[t.p][:], tw[:], 1.0, xg[t.p][:, :, D], ALU.add, ALU.mult).then_inc(weight_ready, 1)

            run_experts(dve, body)

        @block.tensor
        def _(pe):
            def apply(to_bank, t, first):
                for f in range(NF):
                    for c in range(2):
                        mm = nc.tensor.matmul(ps[0:HC, to_bank + f // 2, CAP * (f % 2):CAP * (f % 2) + CAP],
                                              w_up[t.p][:, c, first + HC * f:first + HC * f + HC], xgt[t.p][:, c, :], start=(c == 0), stop=(c == 1))
                return mm

            def body(i, todo):
                for kind, lag in todo:
                    t = i.plus(-lag)
                    if kind == "turn":
                        pe.wait_ge(x_gathered[t.p], 32 * t.h + 32)
                        wait(pe, xgt_ready, t.v)
                        for c in range(2):
                            for q in range(2):
                                mm = nc.tensor.transpose(ps[0:KC, 5, CAP * c + HALF * q:CAP * c + HALF * q + HALF], xg[t.p][:, q, KC * c:KC * c + KC], ident[0:HALF, 0:HALF])
                        mm.then_inc(turn_full, 1)
                        pe.wait_ge(xgt_ready, t.v + 1)
                        pe.wait_ge(up_loaded[t.p], 16 * t.h + 16)
                        wait(pe, tw_ready, t.v)
                        for q in range(2):
                            for c in range(2):
                                mm = nc.tensor.matmul(ps[0:HALF, 6, q:q + 1], xgt[t.p][:, c, HALF * q:HALF * q + HALF], w_up[t.p][:, c, 2 * HID:2 * HID + 1], start=(c == 0), stop=(c == 1))
                        mm.then_inc(gate_full, 1)
                    elif kind == "up_g":
                        wait(pe, e_g_used, t.v)
                        apply(0, t, 0).then_inc(e_g_full, 1)
                    elif kind == "up_u":
                        wait(pe, e_inter_ready, t.v)
                        apply(2, t, HID).then_inc(e_u_full, 1)
                    elif kind == "down":
                        pe.wait_ge(e_inter_ready, t.v + 1)
                        pe.wait_ge(down_loaded[t.p], 16 * t.h + 16)
                        wait(pe, yo_ready, t.v)
                        for q in range(2):
                            for f in range(NF):
                                at = CAP * (f % 2) + HALF * q
                                mm = nc.tensor.matmul(ps[0:HALF, 4, D * q:D * q + D], inter[:, f // 2, at:at + HALF], w_down[t.p][:, f, :], start=(f == 0), stop=(f == NF - 1))
                        mm.then_inc(down_full, 1)

            run_experts(pe, body)


def _layout(i):
    import numpy as np

    x = np.asarray(i["x"]).reshape(B, 3, 14, 16, 14, 16).transpose(0, 3, 5, 1, 2, 4).reshape(B, PC, 128, IMG).transpose(0, 2, 1, 3)
    up = np.concatenate([np.asarray(i["L0_ffn_W_gate_up"]), np.asarray(i["L0_ffn_Wg"])[:, :, None]], axis=2)
    n = lambda k: np.asarray(i["L0_" + k])
    return {
        "x": x,
        "txt": np.asarray(i["txt"]),
        "ln_w": n("tok_ln_w").reshape(PC, 128).T,
        "ln_b": n("tok_ln_b").reshape(PC, 128).T,
        "w_tok": n("tok_W").reshape(PC, 128, D).transpose(1, 0, 2),
        "b_tok": n("tok_b").reshape(1, D),
        "pos": n("tok_pos_emd").reshape(2, 98, D).transpose(1, 0, 2),
        "a_log": n("attn_A_log"),
        "w_bc_t": n("attn_W_bc").T,
        "b_bc": n("attn_b_bc").reshape(2 * N, 1),
        "w_1": n("attn_W_1").reshape(D, 1),
        "b_1": n("attn_b_1").reshape(1, 1),
        "w_d": n("attn_W_d").reshape(D, 1),
        "b_d": n("attn_b_d").reshape(D, 1),
        "wg_t": n("ffn_Wg").T,
        "e_bias": n("ffn_e_bias").reshape(1, E),
        "we_up": up.reshape(E, 2, 96, 2 * HID + 1).transpose(0, 2, 1, 3),
        "we_down": n("ffn_W_down").reshape(E, NF, HC, D).transpose(0, 2, 1, 3),
        "ws_g": n("ffn_Wsg"),
        "ws_u": n("ffn_Wsu"),
        "ws_d": n("ffn_Wsd").reshape(NJ, HC, D).transpose(1, 0, 2),
    }


def kernel(**inputs):
    import numpy as np
    import concourse.bacc as bacc
    from concourse.bass_utils import run_bass_kernel_spmd

    nc = bacc.Bacc("TRN2", target_bir_lowering=False, num_devices=1)
    arrays, args = {}, {}
    for name, value in _layout(inputs).items():
        arrays[f"in_{name}"] = np.ascontiguousarray(value)
        args[name] = nc.dram_tensor(f"in_{name}", value.shape, mybir.dt.from_np(value.dtype), kind="ExternalInput").ap()
    out = nc.dram_tensor("out_rows", (T_ALL + CAP, D), F32, kind="ExternalOutput").ap()
    build(nc, args, out)
    got = run_bass_kernel_spmd(nc, [arrays], core_ids=[0]).results[0]["out_rows"]
    return got[0:T_ALL].reshape(B, L, D)
```

```python
from contextlib import ExitStack

import concourse.bass as bass
from concourse import mybir

F32 = mybir.dt.float32
BF16 = mybir.dt.bfloat16
U32 = mybir.dt.uint32
ALU = mybir.AluOpType
ACT = mybir.ActivationFunctionType
AX = mybir.AxisListType

B, L, D, N = 64, 324, 192, 16
IMG, TXT = 196, 128
PATCH, PC = 768, 6
ROWS = (98, 98, 128)
OFF = (0, 98, 196)
PAIRS = B // 2
T_ALL = B * L
LO, HI = 128, D - 128
E, CAP, TOPK = 128, 192, 6
HID, HC = 464, 116
NF = HID // HC
SHID = 928
NJ = SHID // HC
HALF = CAP // 2
SCALE = 2.5
EPS = 1e-5
BIG = 3.0e38
XW = D + 2


class Turn:

    def __init__(self, v, p, h):
        self.v, self.p, self.h = v, p, h

    @classmethod
    def fixed(cls, n):
        return cls(n, n % 2, n // 2)

    def plus(self, k):
        return Turn(self.v + k, (self.p + k) % 2, self.h + (self.p + k) // 2)


def wait(eng, sem, value):
    if not (isinstance(value, int) and value <= 0):
        eng.wait_ge(sem, value)


def schedule(engine):
    at = []

    def put(piece, lag, k, **steps):
        if engine in steps:
            at.append((steps[engine], len(at), (piece, lag, k)))

    for n in range(N):
        b, lag = 2 * (n - 2) + 1, 0
        if b < 0:
            b, lag = b + 32, -1
        put("fill_b", lag, n, pe=b, act=b + 1, pool=b + 2)
        d, lag = (2 * n - 1.5, 0) if n else (30.5, -1)
        put("decay", lag, n, act=d + 0.3)
        put("scan", 0, n, dve=2 * n)
        put("fill_c", 0, n, pe=2 * n, dve=2 * n + 1.2, pool=2 * n + 2)
    for k in range(3):
        put("down_a", 3, k, pe=0.1 + 2 * k)
        put("down", 3, k, pe=1.1 + 2 * k, dve=2.1 + 2 * k)
        put("store_out", 3, k, sp=2.6 + 2 * k)
        put("resid", 1, k, pe=4.9 + 1.8 * k, dve=5.7 + 1.8 * k)
        put("x2_turn", 1, k, pe=15.2 + 1.1 * k, act=16.2 + 1.1 * k)
        put("x1_turn", -1, k, pe=18.2 + 1.1 * k, act=19.2 + 1.1 * k)
        put("step_size", -1, k, pe=25.2 + k, act=26.2 + k)
    put("load_x", -2, 0, sp=1.5)
    put("load_txt", -1, 0, sp=14)
    put("ln2_stats", 1, 0, dve=10.3, act=11.3)
    put("ln2_apply", 1, 0, dve=12.3, act=13)
    put("emb_scale", -1, 0, dve=11.1)
    put("ln1_stats", -1, 0, dve=12.4, act=13.4)
    put("ln1_apply", -1, 0, dve=14.4, act=15.4)
    for k in range(2):
        put("gate", 1, k, pe=22.1 + k, act=23.3 + k)
        put("emb_a", -2, k, pe=8.5 + 6 * k, act=7.5 + 5.2 * k)
        put("emb", -2, k, pe=9.5 + 5.85 * k, act=13.2 + 5.85 * k)
    put("bc_values", -1, 0, pe=21.5, act=22.3, dve=23.4)
    put("softplus", -1, 0, act=28.5, dve=29.2)
    for k in range(3):
        put("choose", 2, k, dve=1.3 + k)
    put("weigh", 2, 0, dve=5)
    put("weigh", 2, 1, dve=6)
    put("count", 2, 0, pe=3.2, dve=5.2)
    put("store_mid", 2, 0, sp=5.5)
    put("find_a", 2, 0, dve=7.5)
    put("find", 2, 0, pe=7.6, dve=8.6)
    put("emb_stats", -2, 0, dve=20.4, act=21.4)
    for k in range(2 * NJ):
        for n, piece in enumerate(("up_g", "up_u")):
            step = 6.6 + 0.8 * (2 * (k // 2 * 2 + n) + k % 2)
            put(piece, 2, k, pe=step, act=step + 0.6, dve=step + 0.8)
    return [piece for _, _, piece in sorted(at)]


SCHEDULE = {engine: schedule(engine) for engine in ("pe", "act", "dve", "pool", "sp")}
WORK, SUMS = 0, 1
BANK = {"resid": WORK, "x2_turn": WORK, "gate": WORK, "count": WORK, "x1_turn": WORK, "bc_values": WORK, "step_size": WORK, "find": WORK,
        "down": SUMS, "emb": SUMS}
FIRST_BODY, LOOP_FROM, LOOP_TO, LAST_BODY = -2, 3, 29, PAIRS + 2


def pieces(engine, i):
    return [x for x in SCHEDULE[engine] if (PAIRS - 1 if x[0] in ("find_a", "find") else 0) <= i - x[1] < PAIRS]


def bank_uses(i):
    return [sum(BANK.get(kind) == bank for kind, _, _ in pieces("pe", i)) for bank in (WORK, SUMS)]


def use_number(i, before):
    def use(piece, k, ago=0):
        bank = BANK[piece]
        same = [(x[0], x[2]) for x in pieces("pe", i - ago) if BANK.get(x[0]) == bank]
        return before[bank] - (len(same) if ago else 0) + same.index((piece, k)) + 1
    return use


def run_bodies(eng, engine, body):
    before = [0, 0]
    add = lambda n, times: [b + x * times for b, x in zip(before, n)]
    for i in range(FIRST_BODY, LOOP_FROM):
        body(Turn.fixed(i), pieces(engine, i), use_number(i, before))
        before = add(bank_uses(i), 1)
    steady = bank_uses(LOOP_FROM)
    with eng.Fori(0, (LOOP_TO - LOOP_FROM) // 2) as r:
        for q in range(2):
            start = Turn.fixed(LOOP_FROM + q)
            so_far = [x + 2 * n * r for x, n in zip(add(steady, q), steady)]
            body(Turn(start.v + 2 * r, start.p, start.h + r), pieces(engine, LOOP_FROM), use_number(LOOP_FROM, so_far))
    before = add(steady, LOOP_TO - LOOP_FROM)
    for i in range(LOOP_TO, LAST_BODY + 1):
        body(Turn.fixed(i), pieces(engine, i), use_number(i, before))
        before = add(bank_uses(i), 1)


def build(nc, a, out):
    dram_x = nc.dram_tensor("token_rows", (T_ALL + CAP, XW), F32).ap()
    dram_cnt = nc.dram_tensor("running_counts", (E * B, L), F32).ap()
    with ExitStack() as outer:
        ident = outer.enter_context(nc.sbuf_tensor("ident", [128, 128], F32))
        found = tuple(outer.enter_context(nc.sbuf_tensor(name, [HALF, 2, E], F32)) for name in ("base", "row"))
        with ExitStack() as ctx:
            phase1(nc, ctx, a, out, dram_x, dram_cnt, ident, found)
        with ExitStack() as ctx:
            phase2(nc, ctx, a, out, dram_x, dram_cnt, ident, found)


class Buffers:

    def __init__(self, nc, ctx, ident, found):
        sb = lambda name, shape, dt=F32: ctx.enter_context(nc.sbuf_tensor(name, shape, dt))
        self.ident, (self.base, self.row) = ident, found
        self.slot = sb("slot", [E, CAP])
        self.lane = sb("lane", [E, 1])
        self.block_of = sb("block_of", [E, 2, CAP])
        self.ident_bf = sb("ident_bf", [128, 128], BF16)
        self.ones = sb("ones", [128, 128])
        self.zeros = sb("zeros", [128, XW])
        self.w_tok = sb("w_tok", [128, PC, D + 2])
        self.pos = sb("pos", [ROWS[0], 2, D])
        self.a_neg = sb("a_neg", [128, 2, N])
        self.wbc = sb("wbc", [128, 3, 96])
        self.bc_bias = sb("bc_bias", [32, 2])
        self.wd = sb("wd", [128, 2])
        self.bd = sb("bd", [128, 2])
        self.pick = sb("pick", [96, 32], BF16)
        self.pick2 = sb("pick2", [96, N, 128], BF16)
        self.wg = sb("wg", [128, 3, E])
        self.e_bias = sb("e_bias", [128, E])
        self.ws_g = sb("ws_g", [128, 3, SHID])
        self.ws_u = sb("ws_u", [128, 3, SHID])
        self.ws_d = sb("ws_d", [HC, NJ, D])
        two = lambda name, shape, dt=F32, n=2: [sb(f"{name}{p}", shape, dt) for p in range(n)]
        self.x_in = sb("x_in", [128, 2, PC, IMG])
        self.x_sq = sb("x_sq", [128, PC, IMG])
        self.emb = sb("emb", [ROWS[0], 2, 2, 196])
        self.h = two("h", [128, 2, 3, D])
        self.h2 = two("h2_", [128, 2, 3, D])
        self.xn = sb("xn", [128, 2, 3, LO])
        self.xm = two("xm", [128, 3, 2, HI])
        self.x2 = sb("x2", [128, 2, 3, XW])
        self.moments = two("moments", [128, 6, 6])
        self.mean_var = two("mean_var", [128, 6, 2])
        self.xf = sb("xf", [128, 3, L])
        self.x2f = two("x2f", [128, 3, L])
        self.delta = two("delta", [128, 3, L])
        self.du = two("du", [128, 3, L])
        self.soft = sb("soft", [128, 3, L])
        self.bcv = sb("bcv", [32, 3, L])[:]
        self.mid_part = sb("mid_part", [32, 3, L], BF16)
        self.parts = two("parts", [96, 3, L], BF16)
        self.decay = two("decay", [128, 3, L])
        self.b_wide = two("b_wide", [128, 3, L])
        self.state = two("state", [128, 3, L], n=4)
        self.y = two("y", [128, 3, L])
        self.th = sb("th", [HC, 2, L])
        self.ag = sb("ag", [HC, 2, L])
        self.inter = sb("inter", [HC, NJ, 2, L])
        self.gt = sb("gt", [128, 6, E])
        self.ch = sb("ch", [128, 6, E])
        self.mask = sb("mask", [128, 6, E], BF16)
        self.top8 = sb("top8", [128, 6, 8])
        self.stat = sb("stat", [128, 3, 6, 6])
        self.cnt = sb("cnt", [E, 2 * L])
        self.run = sb("run", [E, 1])
        self.ps = ctx.enter_context(nc.psum_tensor("ps", [128, 8, 512], F32))


def prepare(nc, ctx, a, out, dram_x, b):
    sem = lambda name: ctx.enter_context(nc.semaphore(name))
    counted, filled, made, loaded, prepared = sem("counted"), sem("filled"), sem("made"), sem("loaded"), sem("prepared")
    mean_full, bias_full, a_exp, padded = sem("mean_full"), sem("bias_full"), sem("a_exp"), sem("padded")
    with ExitStack() as tmp:
        sb = lambda name, shape, dt=F32: tmp.enter_context(nc.sbuf_tensor(name, shape, dt))
        w_raw = b.x_in[:].rearrange("p b c t -> p (b c t)")[:, 0:PC * D].rearrange("p (c d) -> p c d", c=PC)
        small = b.x_sq[:].rearrange("p c t -> p (c t)")
        ln_w, ln_b = small[:, 0:PC], small[:, PC:2 * PC]
        b1 = small[:, 14:15]
        b_tok = b.emb[0:ROWS[0], 0, 0, 0:D]
        mean_w = b.soft[:, 0, 0:128]
        slot_int, lane_int = small[:, 200:200 + CAP].bitcast(U32), small[:, 400:401].bitcast(U32)
        zero_tiles = [b.ident[:], b.ident_bf[:], b.pick[:], b.wbc[:], b.wg[:, 1:3], b.ws_g[:, 1:3], b.ws_u[:, 1:3], b.zeros[:],
                      b.gt[:], b.x2[:, :, :, D:XW], b.run[:], b.stat[:], b.block_of[:], *(t[:, :, 0:2, :] for t in (*b.h, *b.h2)),
                      *(t[:, :, 0:1] for t in b.decay)]
        loads = [
            (w_raw, a["w_tok"]), (ln_w, a["ln_w"]), (ln_b, a["ln_b"]), (b_tok, a["b_tok"].broadcast_to([ROWS[0], D])),
            (b.pos[:], a["pos"]), (b.a_neg[:, 0, :], a["a_log"][0:LO]),
            (b1, a["b_1"].broadcast_to([128, 1])),
            (b.wd[:, 0:1], a["w_d"][0:LO]), (b.bd[:, 0:1], a["b_d"][0:LO]),
            (b.e_bias[:], a["e_bias"].broadcast_to([128, E])), (b.ws_d[:], a["ws_d"]),
            (b.wg[:, 0, :], a["wg_t"][0:LO]), (b.ws_g[:, 0, :], a["ws_g"][0:LO]), (b.ws_u[:, 0, :], a["ws_u"][0:LO]),
        ]
        for half in range(2):
            at = slice(HI * half, HI * half + HI)
            loads += [
                (b.a_neg[at, 1, :], a["a_log"][LO:D]),
                (b.wd[at, 1:2], a["w_d"][LO:D]), (b.bd[at, 1:2], a["b_d"][LO:D]),
                (b.wg[at, 1 + half, :], a["wg_t"][LO:D]), (b.ws_g[at, 1 + half, :], a["ws_g"][LO:D]),
                (b.ws_u[at, 1 + half, :], a["ws_u"][LO:D]),
            ]
            col = slice(64 + 16 * half, 65 + 16 * half)
            loads += [(b.wbc[:, half, col], a["w_1"][0:LO]), (b.wbc[at, 2, col], a["w_1"][LO:D])]
            for c in range(2):
                col = slice(32 * c + 16 * half, 32 * c + 16 * half + 16)
                loads += [
                    (b.wbc[:, half, col], a["w_bc_t"][0:LO, 16 * c:16 * c + 16]),
                    (b.wbc[at, 2, col], a["w_bc_t"][LO:D, 16 * c:16 * c + 16]),
                    (b.bc_bias[16 * half:16 * half + 16, c:c + 1], a["b_bc"][16 * c:16 * c + 16]),
                ]
        with nc.Block() as block:

            @block.gpsimd
            def _(pool):
                nc.gpsimd.iota(slot_int, [[1, CAP]], base=0, channel_multiplier=0).then_inc(counted, 1)
                nc.gpsimd.iota(lane_int, [[0, 1]], base=0, channel_multiplier=B).then_inc(counted, 1)
                pool.wait_ge(filled, len(zero_tiles))
                for tile in (b.ident, b.ident_bf):
                    nc.gpsimd.affine_select(out=tile[:], in_=tile[:], compare_op=ALU.not_equal, fill=1.0, base=0,
                                            pattern=[[-1, 128]], channel_multiplier=1).then_inc(made, 1)
                for part in range(3):
                    pool.wait_ge(made, 2 + part)
                    rows = b.pick[32 * part:32 * part + 32, :]
                    nc.gpsimd.affine_select(out=rows, in_=rows, compare_op=ALU.not_equal, fill=1.0, base=0,
                                            pattern=[[-1, 32]], channel_multiplier=1).then_inc(made, 1)
                pool.wait_ge(made, 5)

            @block.sync
            def _(sp):
                sp.wait_ge(filled, len(zero_tiles))
                for to, source in loads[0::2]:
                    sp.dma_start(to, source).then_inc(loaded, 16)
                for k in range(2):
                    rows = slice(T_ALL + HALF * k, T_ALL + HALF * k + HALF)
                    sp.dma_start(dram_x[rows], b.zeros[0:HALF, 0:XW]).then_inc(padded, 16)
                    sp.dma_start(out[rows], b.zeros[0:HALF, 0:D]).then_inc(padded, 16)
                sp.wait_ge(padded, 64)

            @block.vector
            def _(dve):
                done = [0]

                def step(ins):
                    done[0] += 1
                    ins.then_inc(prepared, 1)
                    dve.wait_ge(prepared, done[0])

                for tile in zero_tiles:
                    nc.vector.memset(tile, 0.0).then_inc(filled, 1)
                dve.wait_ge(counted, 2)
                nc.vector.tensor_copy(b.slot[:], slot_int)
                nc.vector.tensor_copy(b.lane[:], lane_int)
                step(nc.vector.memset(b.ones[:], 1.0))
                step(nc.vector.memset(mean_w, 1.0 / PATCH))
                step(nc.vector.memset(b.w_tok[:, :, D:D + 2], 1.0))
                dve.wait_ge(loaded, 16 * len(loads))
                for c in range(PC):
                    step(nc.vector.tensor_scalar(b.w_tok[:, c, 0:D], w_raw[:, c, :], ln_w[:, c:c + 1], None, ALU.mult))
                for c in range(PC):
                    step(nc.vector.tensor_scalar(b.xf[:].rearrange("p a b -> p (a b)")[:, 128 * c:128 * c + 128],
                                                 b.ones[:], ln_b[:, c:c + 1], None, ALU.mult))
                dve.wait_ge(mean_full, 1)
                step(nc.vector.tensor_tensor(b.w_tok[:, :, 0:D], b.w_tok[:, :, 0:D],
                                             b.ps[:, 0, 0:D].unsqueeze(1).broadcast_to([128, PC, D]), ALU.subtract))
                dve.wait_ge(bias_full, 1)
                for k in range(2):
                    step(nc.vector.tensor_tensor(b.pos[:, k, :], b.pos[:, k, :], b.ps[0:ROWS[0], 1, 0:D], ALU.add))
                    step(nc.vector.tensor_tensor(b.pos[:, k, :], b.pos[:, k, :], b_tok, ALU.add))
                dve.wait_ge(made, 5)
                for half in range(2):
                    step(nc.vector.tensor_copy(b.pick2[:, :, HI * half:HI * half + HI],
                                               b.pick[:, N * half:N * half + N].unsqueeze(2).broadcast_to([96, N, HI])))
                dve.wait_ge(a_exp, 1)
                step(nc.vector.tensor_scalar(b.a_neg[:], b.a_neg[:], -1.0, None, ALU.mult))
                step(nc.vector.scalar_tensor_tensor(b.bd[:], b.wd[:], b1, b.bd[:], ALU.mult, ALU.add))
                step(nc.vector.tensor_scalar(b.ws_d[:], b.ws_d[:], 0.5, None, ALU.mult))

            @block.scalar
            def _(act):
                act.wait_ge(filled, len(zero_tiles))
                for to, source in loads[1::2]:
                    act.dma_start(to, source).then_inc(loaded, 16)
                act.wait_ge(loaded, 16 * len(loads))
                nc.scalar.activation(b.a_neg[:], b.a_neg[:], ACT.Exp).then_inc(a_exp, 1)

            @block.tensor
            def _(pe):
                pe.wait_ge(prepared, 3 + PC)
                for c in range(PC):
                    mm = nc.tensor.matmul(b.ps[:, 0, 0:D], mean_w, b.w_tok[:, c, 0:D], start=(c == 0), stop=(c == PC - 1))
                mm.then_inc(mean_full, 1)
                pe.wait_ge(prepared, 3 + 2 * PC)
                for c in range(PC):
                    wide = b.xf[:].rearrange("p a b -> p (a b)")[:, 128 * c:128 * c + ROWS[0]]
                    mm = nc.tensor.matmul(b.ps[0:ROWS[0], 1, 0:D], wide, w_raw[:, c, :], start=(c == 0), stop=(c == PC - 1))
                mm.then_inc(bias_full, 1)


def phase1(nc, ctx, a, out, dram_x, dram_cnt, ident, found):
    b = Buffers(nc, ctx, ident, found)
    prepare(nc, ctx, a, out, dram_x, b)
    sem = lambda name: ctx.enter_context(nc.semaphore(name))
    ps, stat = b.ps, b.stat
    flat = ps[:].rearrange("p b c -> p (b c)")
    b_bank, c_bank = 0, 2 * 512
    gu_ps = ps[0:HC, 4:6, 0:L]
    work, sums = ps[:, 6, :], ps[:, 7, :]

    x_loaded, sq_ready, sq_used = sem("x_loaded"), sem("sq_ready"), sem("sq_used")
    txt_loaded = [sem(f"txt_loaded{p}") for p in range(2)]
    work_full, work_free = sem("work_full"), sem("work_free")
    sums_full, sums_free = sem("sums_full"), sem("sums_free")
    emb_var, emb_log, emb_r0, emb_done = sem("emb_var"), sem("emb_log"), sem("emb_r0"), sem("emb_done")
    ln_var = [sem(f"ln{k}_var") for k in (1, 2)]
    ln_log = [sem(f"ln{k}_log") for k in (1, 2)]
    ln_r0 = [sem(f"ln{k}_r0") for k in (1, 2)]
    ln_scale = [sem(f"ln{k}_scale") for k in (1, 2)]
    ln_done = [sem(f"ln{k}_done") for k in (1, 2)]
    parts_ready = sem("parts_ready")
    soft_abs, soft_exp, soft_ready, du_ready = sem("soft_abs"), sem("soft_exp"), sem("soft_ready"), sem("du_ready")
    decay_ready, scan_done = sem("decay_ready"), sem("scan_done")
    b_full, b_copied, input_ready = sem("b_full"), sem("b_copied"), sem("input_ready")
    c_full, c_used, y_added = sem("c_full"), sem("c_used"), sem("y_added")
    resid_done = sem("resid_done")
    mask_ready, factor_ready, cnt_ready = sem("mask_ready"), sem("factor_ready"), sem("cnt_ready")
    block_step, find_ready = sem("block_step"), sem("find_ready")
    g_full, th_ready, g_used = sem("g_full"), sem("th_ready"), sem("g_used")
    u_full, inter_ready, out_ready = sem("u_full"), sem("inter_ready"), sem("out_ready")
    out_stored = [[sem(f"out_stored{p}{k}") for k in range(3)] for p in range(2)]
    rows_stored, cnt_stored = sem("rows_stored"), sem("cnt_stored")
    waited = sem("waited")
    LINKS = {"emb": 7, "ln1": 5, "ln2": 5, "bc": 4, "soft": 1, "choose": 5, "weigh": 4}
    chains = {k: sem(f"chain_{k}") for k in LINKS}

    class Chain:

        def __init__(self, eng, name, t, start=0):
            self.eng, self.sem, self.base, self.n = eng, chains[name], LINKS[name] * t.v, start

        def __call__(self, ins, alone=False):
            self.n += 1
            ins.then_inc(self.sem, 1)
            self.eng.wait_ge(self.sem, self.base + self.n)
            if alone:
                self.eng.sem_inc(waited, 1)

    def token_rows(dram, t, k):
        return dram[bass.ds(t.v * (2 * L), 2 * L)].rearrange("(b r) d -> r b d", b=2)[OFF[k]:OFF[k] + ROWS[k]]

    with nc.Block() as block:

        @block.sync
        def _(sp):
            def body(i, todo, use):
                for kind, lag, k in todo:
                    t = i.plus(-lag)
                    if kind == "load_x":
                        wait(sp, emb_var, t.v)
                        sp.dma_start(b.x_in[:], a["x"][bass.ds(t.v * 2, 2)].rearrange("b p c t -> p b c t")).then_inc(x_loaded, 16)
                    elif kind == "load_txt":
                        wait(sp, resid_done, t.v - 1)
                        sp.dma_start(b.h[t.p][:, :, 2, :], a["txt"][bass.ds(t.v * 2, 2)].rearrange("b r d -> r b d")).then_inc(txt_loaded[t.p], 16)
                    elif kind == "store_out":
                        sp.wait_ge(sums_free, use("down", k))
                        sp.dma_start(token_rows(out, t, k), b.h2[t.p][0:ROWS[k], :, k, :]).then_inc(out_stored[t.p][k], 16)
                    elif kind == "store_mid":
                        sp.wait_ge(factor_ready, t.v + 1)
                        for c in range(3):
                            sp.dma_start(token_rows(dram_x, t, c), b.x2[0:ROWS[c], :, c, :]).then_inc(rows_stored, 16)
                        sp.wait_ge(cnt_ready, t.v + 1)
                        sp.dma_start(dram_cnt.rearrange("(e b) l -> e b l", e=E)[:, bass.ds(t.v * 2, 2), :],
                                     b.cnt[:].rearrange("e (b l) -> e b l", b=2)).then_inc(cnt_stored, 16)

            run_bodies(sp, "sp", body)
            for p in range(2):
                for k in range(3):
                    sp.wait_ge(out_stored[p][k], 16 * PAIRS // 2)
            sp.wait_ge(rows_stored, 48 * PAIRS)
            sp.wait_ge(cnt_stored, 16 * PAIRS)

        @block.gpsimd
        def _(pool):
            def body(i, todo, use):
                for kind, lag, n in todo:
                    t = i.plus(-lag)
                    if kind == "fill_b":
                        if n == 0:
                            pool.wait_ge(du_ready, t.v + 1)
                        pool.wait_ge(b_copied, N * t.v + n + 1)
                        wait(pool, y_added, 15 * t.v + (max(n - 4, 1) if n >= 4 else n - 3))
                        nc.gpsimd.tensor_tensor(b.state[n % 4][:], b.du[t.p][:], b.b_wide[n % 2][:], ALU.mult).then_inc(input_ready, 1)
                    elif kind == "fill_c" and n > 0:
                        pool.wait_ge(c_used, N * t.v + n + 1)
                        y = b.y[t.p][:]
                        if n == 1:
                            wait(pool, resid_done, t.v - 1)
                            nc.gpsimd.tensor_tensor(y, b.state[0][:], b.state[1][:], ALU.add).then_inc(y_added, 1)
                        else:
                            pool.wait_ge(y_added, 15 * t.v + n - 1)
                            nc.gpsimd.tensor_tensor(y, y, b.state[n % 4][:], ALU.add).then_inc(y_added, 1)

            run_bodies(pool, "pool", body)

        @block.scalar
        def _(act):
            def rsqrt_guess(m, rows, cols, var_sem, log_sem, out_sem, t):
                act.wait_ge(var_sem, t.v + 1)
                nc.scalar.activation(stat[0:rows, m, 5, 0:cols], stat[0:rows, m, 4, 0:cols], ACT.Ln).then_inc(log_sem, 1)
                act.wait_ge(log_sem, t.v + 1)
                nc.scalar.activation(stat[0:rows, m, 5, 0:cols], stat[0:rows, m, 5, 0:cols], ACT.Exp, scale=-0.5).then_inc(out_sem, 1)

            def body(i, todo, use):
                for kind, lag, k in todo:
                    t = i.plus(-lag)
                    if kind == "decay":
                        if k == 0:
                            act.wait_ge(du_ready, t.v + 1)
                        wait(act, scan_done, N * t.v + k - 1)
                        to = b.decay[k % 2]
                        nc.scalar.activation(to[:, 0:2, 1:L], b.delta[t.p][:, 0:2, 1:L], ACT.Exp, scale=b.a_neg[:, 0, k:k + 1])
                        nc.scalar.activation(to[:, 2, 1:L], b.delta[t.p][:, 2, 1:L], ACT.Exp, scale=b.a_neg[:, 1, k:k + 1]).then_inc(decay_ready, 1)
                    elif kind == "fill_b":
                        act.wait_ge(b_full, N * t.v + k + 1)
                        wait(act, input_ready, N * t.v + k - 1)
                        nc.scalar.activation(b.b_wide[k % 2][:].rearrange("p a t -> p (a t)"), flat[:, b_bank:b_bank + 3 * L], ACT.Copy).then_inc(b_copied, 1)
                    elif kind == "emb_a":
                        act.wait_ge(x_loaded, 16 * t.v + 16)
                        wait(act, sq_used, 2 * t.v + k)
                        nc.scalar.activation(b.x_sq[:], b.x_in[:, k], ACT.Square).then_inc(sq_ready, 1)
                    elif kind == "emb":
                        act.wait_ge(sums_full, use(kind, k))
                        if k == 0:
                            wait(act, emb_done, t.v)
                        nc.scalar.activation(b.emb[:, k].rearrange("p a b -> p (a b)"), sums[0:ROWS[0], 0:392], ACT.Copy).then_inc(sums_free, 1)
                    elif kind == "emb_stats":
                        rsqrt_guess(0, ROWS[0], 4, emb_var, emb_log, emb_r0, t)
                    elif kind in ("ln1_stats", "ln2_stats"):
                        m = int(kind[2]) - 1
                        rsqrt_guess(m + 1, 128, 6, ln_var[m], ln_log[m], ln_r0[m], t)
                    elif kind in ("ln1_apply", "ln2_apply"):
                        m = int(kind[2]) - 1
                        act.wait_ge(ln_scale[m], t.v + 1)
                        if m == 0:
                            wait(act, du_ready, t.v)
                            source, to, width = b.h[t.p], b.xn, LO
                        else:
                            wait(act, cnt_ready, t.v)
                            wait(act, rows_stored, 48 * t.v)
                            source, to, width = b.h2[t.p], b.x2, D
                        for q in range(2):
                            for c in range(3):
                                at = 3 * q + c
                                norm = {"scale": stat[:, m + 1, 3, at:at + 1], "bias": stat[:, m + 1, 2, at:at + 1]}
                                nc.scalar.activation(b.xm[m][:, c, q, :], source[:, q, c, LO:D], ACT.Identity, **norm)
                                last = nc.scalar.activation(to[:, q, c, 0:width], source[:, q, c, 0:width], ACT.Identity, **norm)
                        last.then_inc(ln_done[m], 1)
                    elif kind == "x1_turn":
                        act.wait_ge(work_full, use(kind, k))
                        if k == 0:
                            wait(act, du_ready, t.v)
                        nc.scalar.activation(b.xf[:, k, :], work[:, 0:L], ACT.Copy).then_inc(work_free, 1)
                    elif kind == "x2_turn":
                        act.wait_ge(work_full, use(kind, k))
                        if k == 0:
                            wait(act, u_full, 2 * NJ * (t.v - 1))
                        nc.scalar.activation(b.x2f[t.p][:, k, :], work[:, 0:L], ACT.Copy).then_inc(work_free, 1)
                    elif kind == "bc_values":
                        act.wait_ge(work_full, use(kind, k))
                        wait(act, parts_ready, t.v)
                        nc.scalar.activation(b.bcv[:, 0, :], work[0:32, 0:L], ACT.Identity, bias=b.bc_bias[:, 0:1])
                        nc.scalar.activation(b.bcv[:, 1, :], work[32:64, 0:L], ACT.Identity, bias=b.bc_bias[:, 1:2])
                        nc.scalar.activation(b.bcv[:, 2, :], work[64:96, 0:L], ACT.Copy).then_inc(work_free, 1)
                    elif kind == "step_size":
                        col = 1 if k == 2 else 0
                        act.wait_ge(work_full, use(kind, k))
                        if k == 0:
                            wait(act, du_ready, t.v)
                            wait(act, decay_ready, N * (t.v - 1))
                        scale, bias = b.wd[:, col:col + 1], b.bd[:, col:col + 1]
                        nc.scalar.activation(b.soft[:, k, :], work[:, 0:L], ACT.Abs, scale=scale, bias=bias).then_inc(soft_abs, 1)
                        nc.scalar.activation(b.delta[t.p][:, k, :], work[:, 0:L], ACT.Relu, scale=scale, bias=bias).then_inc(work_free, 1)
                    elif kind == "softplus":
                        act.wait_ge(soft_abs, 3 * t.v + 3)
                        nc.scalar.activation(b.soft[:], b.soft[:], ACT.Exp, scale=-1.0).then_inc(soft_exp, 1)
                        act.wait_ge(soft_exp, t.v + 1)
                        nc.scalar.activation(b.soft[:], b.soft[:], ACT.Ln, bias=1.0).then_inc(soft_ready, 1)
                    elif kind == "gate":
                        act.wait_ge(work_full, use(kind, k))
                        if k == 0:
                            wait(act, factor_ready, t.v)
                        nc.scalar.activation(b.gt[0:98, 3 * k:3 * k + 2, :], work[0:98, 0:256].rearrange("p (k e) -> p k e", k=2), ACT.Tanh, scale=0.5)
                        nc.scalar.activation(b.gt[:, 3 * k + 2, :], work[:, 256:384], ACT.Tanh, scale=0.5).then_inc(work_free, 1)
                    elif kind == "up_g":
                        act.wait_ge(g_full, 2 * NJ * t.v + k + 1)
                        wait(act, g_used, 2 * NJ * t.v + k - 1)
                        nc.scalar.activation(b.th[:, k % 2], gu_ps[:, k % 2], ACT.Tanh, scale=0.5).then_inc(th_ready, 1)

            run_bodies(act, "act", body)

        @block.vector
        def _(dve):
            def newton(m, rows, cols, link):
                s = stat[0:rows, m, :, 0:cols]
                link(nc.vector.tensor_tensor(s[:, 0, :], s[:, 5, :], s[:, 5, :], ALU.mult))
                link(nc.vector.scalar_tensor_tensor(s[:, 1, :], s[:, 0, :], -0.5, s[:, 4, :], ALU.mult, ALU.mult))
                link(nc.vector.scalar_tensor_tensor(s[:, 3, :], s[:, 1, :], 1.5, s[:, 5, :], ALU.add, ALU.mult))
                return s[:, 3, :]

            def body(i, todo, use):
                for kind, lag, k in todo:
                    t = i.plus(-lag)
                    if kind == "scan":
                        dve.wait_ge(decay_ready, N * t.v + k + 1)
                        dve.wait_ge(input_ready, N * t.v + k + 1)
                        s = b.state[k % 4][:].rearrange("p a t -> p (a t)")
                        nc.vector.tensor_tensor_scan(s, b.decay[k % 2][:].rearrange("p a t -> p (a t)"), s, 0.0,
                                                     ALU.mult, ALU.add).then_inc(scan_done, 1)
                    elif kind == "fill_c":
                        dve.wait_ge(c_full, N * t.v + k + 1)
                        dve.wait_ge(scan_done, N * t.v + k + 1)
                        s = b.state[k % 4][:].rearrange("p a t -> p (a t)")
                        nc.vector.tensor_tensor(s, s, flat[:, c_bank:c_bank + 3 * L], ALU.mult).then_inc(c_used, 1)
                    elif kind == "down":
                        dve.wait_ge(sums_full, use(kind, k))
                        r, to = ROWS[k], b.h2[t.p]
                        ins = nc.vector.tensor_tensor(to[0:r, :, k, :], to[0:r, :, k, :], sums[0:r, 0:2 * D].rearrange("p (b d) -> p b d", b=2), ALU.add)
                        ins.then_inc(sums_free, 1)
                        if k == 2:
                            dve.wait_ge(sums_free, use(kind, k))
                            nc.vector.memset(stat[0:1, 0, 2, 4:5], 0.0).then_inc(out_ready, 1)
                    elif kind == "resid":
                        dve.wait_ge(work_full, use(kind, k))
                        wait(dve, out_stored[t.p][k], 16 * t.h)
                        r = ROWS[k]
                        nc.vector.tensor_tensor(b.h2[t.p][0:r, :, k, 0:LO], b.h[t.p][0:r, :, k, 0:LO],
                                                work[0:r, 0:2 * LO].rearrange("p (b d) -> p b d", b=2), ALU.add)
                        nc.vector.tensor_tensor(b.h2[t.p][0:r, :, k, LO:D], b.h[t.p][0:r, :, k, LO:D],
                                                work[0:r, 2 * LO:2 * LO + 2 * HI].rearrange("p (b d) -> p b d", b=2), ALU.add).then_inc(work_free, 1)
                        if k == 2:
                            dve.wait_ge(work_free, use(kind, k))
                            nc.vector.memset(stat[0:1, 0, 2, 5:6], 0.0).then_inc(resid_done, 1)
                    elif kind == "emb_stats":
                        dve.wait_ge(sums_free, use("emb", 1))
                        link = Chain(dve, "emb", t)
                        col = lambda c: b.emb[:, :, :, c:c + 1].rearrange("p b k c -> p (b k) c")[:, :, 0]
                        s = stat[0:ROWS[0], 0, :, 0:4]
                        link(nc.vector.tensor_scalar(s[:, 0, :], col(D), 1.0 / PATCH, None, ALU.mult))
                        link(nc.vector.tensor_tensor(s[:, 1, :], s[:, 0, :], s[:, 0, :], ALU.mult))
                        link(nc.vector.scalar_tensor_tensor(s[:, 2, :], col(D + 2), 1.0 / PATCH, s[:, 1, :], ALU.mult, ALU.subtract))
                        nc.vector.tensor_scalar(s[:, 4, :], s[:, 2, :], 0.0, EPS, ALU.max, ALU.add).then_inc(emb_var, 1)
                    elif kind == "emb_scale":
                        dve.wait_ge(emb_r0, t.v + 1)
                        wait(dve, resid_done, t.v - 1)
                        link = Chain(dve, "emb", t, 3)
                        r = newton(0, ROWS[0], 4, link).rearrange("p (b k) -> p b k", b=2).unsqueeze(3).broadcast_to([ROWS[0], 2, 2, D])
                        to = b.h[t.p][0:ROWS[0], :, 0:2, :]
                        link(nc.vector.tensor_tensor(to, b.emb[:, :, :, 0:D], r, ALU.mult))
                        nc.vector.tensor_tensor(to, to, b.pos[:].unsqueeze(1).broadcast_to([ROWS[0], 2, 2, D]), ALU.add).then_inc(emb_done, 1)
                    elif kind in ("ln1_stats", "ln2_stats"):
                        m = int(kind[2]) - 1
                        if m == 0:
                            dve.wait_ge(emb_done, t.v + 1)
                            dve.wait_ge(txt_loaded[t.p], 16 * t.h + 16)
                            source = b.h[t.p]
                        else:
                            dve.wait_ge(resid_done, t.v + 1)
                            source = b.h2[t.p]
                        wait(dve, ln_done[m], t.v)
                        link = Chain(dve, kind[:3], t)
                        for at in range(6):
                            ins = nc.vector.bn_stats(b.moments[m][:, at, :], source[:, at // 3, at % 3, :])
                        link(ins, alone=True)
                        for at in range(6):
                            ins = nc.vector.bn_aggr(b.mean_var[m][:, at, :], b.moments[m][:, at, :])
                        link(ins)
                        nc.vector.tensor_scalar(stat[:, m + 1, 4, :], b.mean_var[m][:, :, 1], EPS, None, ALU.add).then_inc(ln_var[m], 1)
                    elif kind in ("ln1_apply", "ln2_apply"):
                        m = int(kind[2]) - 1
                        dve.wait_ge(ln_r0[m], t.v + 1)
                        link = Chain(dve, kind[:3], t, 2)
                        r = newton(m + 1, 128, 6, link)
                        nc.vector.scalar_tensor_tensor(stat[:, m + 1, 2, :], b.mean_var[m][:, :, 0], -1.0, r, ALU.mult, ALU.mult).then_inc(ln_scale[m], 1)
                    elif kind == "bc_values":
                        dve.wait_ge(work_free, use(kind, k))
                        wait(dve, c_full, N * (t.v - 1))
                        p, v = b.parts[t.p], b.bcv
                        link = Chain(dve, "bc", t)
                        link(nc.vector.tensor_copy(p[0:32], v))
                        link(nc.vector.tensor_tensor(v, v, p[0:32], ALU.subtract))
                        link(nc.vector.tensor_copy(b.mid_part[:], v))
                        nc.vector.tensor_copy(p[32:64], b.mid_part[:])
                        link(nc.vector.tensor_tensor(v, v, b.mid_part[:], ALU.subtract))
                        nc.vector.tensor_copy(p[64:96], v).then_inc(parts_ready, 1)
                    elif kind == "softplus":
                        dve.wait_ge(soft_ready, t.v + 1)
                        dve.wait_ge(work_free, use("step_size", 2))
                        wait(dve, input_ready, N * (t.v - 1))
                        link = Chain(dve, "soft", t)
                        link(nc.vector.tensor_tensor(b.delta[t.p][:], b.delta[t.p][:], b.soft[:], ALU.add))
                        nc.vector.tensor_tensor(b.du[t.p][:], b.delta[t.p][:], b.xf[:], ALU.mult).then_inc(du_ready, 1)
                    elif kind == "choose":
                        link = Chain(dve, "choose", t, (0, 2, 4)[k])
                        if k == 0:
                            dve.wait_ge(work_free, use("gate", 1, 1))
                            link(nc.vector.tensor_scalar(b.gt[:], b.gt[:], 0.5, 0.5, ALU.mult, ALU.add))
                            link(nc.vector.tensor_tensor(b.ch[:], b.gt[:], b.e_bias[:].unsqueeze(1).broadcast_to([128, 6, E]), ALU.add), alone=True)
                        elif k == 1:
                            for c in range(6):
                                ins = nc.vector.max(b.top8[:, c, :], b.ch[:, c, :])
                            link(ins)
                            link(nc.vector.memset(b.top8[:, :, TOPK:8], -BIG), alone=True)
                        else:
                            for c in range(6):
                                ins = nc.vector.match_replace(b.ch[:, c, :], b.top8[:, c, :], b.ch[:, c, :], BIG)
                            link(ins)
                            wait(dve, cnt_ready, t.v)
                            nc.vector.tensor_scalar(b.mask[:], b.ch[:], BIG / 2, None, ALU.is_ge).then_inc(mask_ready, 1)
                    elif kind == "weigh":
                        link = Chain(dve, "weigh", t, (0, 1)[k])
                        den = b.top8[:, :, 0]
                        if k == 0:
                            dve.wait_ge(mask_ready, t.v + 1)
                            link(nc.vector.tensor_tensor(b.ch[:], b.gt[:], b.mask[:], ALU.mult))
                        else:
                            link(nc.vector.tensor_reduce(den, b.ch[:], AX.X, ALU.add))
                            link(nc.vector.tensor_scalar(den, den, 1e-20, None, ALU.add))
                            link(nc.vector.reciprocal(b.top8[:, :, 1], den))
                            nc.vector.tensor_scalar(b.x2[:, :, :, D], b.top8[:, :, 1].rearrange("p (b k) -> p b k", b=2), SCALE / 4, None, ALU.mult).then_inc(factor_ready, 1)
                    elif kind == "count":
                        dve.wait_ge(work_full, use(kind, k))
                        wait(dve, cnt_ready, t.v)
                        wait(dve, cnt_stored, 16 * t.v)
                        nc.vector.tensor_tensor_scan(b.cnt[:], work.bitcast(BF16)[:, 0:2 * L], b.zeros[:, 0:1].broadcast_to([E, 2 * L]), b.run[:, 0:1], ALU.add, ALU.add).then_inc(work_free, 1)
                        dve.wait_ge(work_free, use(kind, k))
                        nc.vector.tensor_copy(b.run[:], b.cnt[:, 2 * L - 1:2 * L])
                        for q in range(2):
                            if q == 1:
                                dve.wait_ge(block_step, t.v + 1)
                            ins = nc.vector.scalar_tensor_tensor(b.block_of[:, 0, :], b.slot[:], b.cnt[:, L * q + L - 1:L * q + L], b.block_of[:, 0, :], ALU.is_ge, ALU.add)
                            ins.then_inc((block_step, cnt_ready)[q], 1)
                    elif kind == "find_a":
                        dve.wait_ge(cnt_ready, PAIRS)
                        nc.vector.tensor_scalar(b.block_of[:, 0, :], b.block_of[:, 0, :], B - 1.0, None, ALU.min).then_inc(find_ready, 1)
                        dve.wait_ge(find_ready, 1)
                        nc.vector.tensor_scalar(b.block_of[:, 1, :], b.block_of[:, 0, :], b.lane[:, 0:1], None, ALU.add).then_inc(find_ready, 1)
                    elif kind == "find":
                        dve.wait_ge(work_full, use(kind, k))
                        nc.vector.tensor_scalar(b.base[:], work[0:HALF, 0:2 * E].rearrange("p (q e) -> p q e", q=2), float(L), None, ALU.mult)
                        nc.vector.tensor_copy(b.row[:], work[0:HALF, 2 * E:4 * E].rearrange("p (q e) -> p q e", q=2)).then_inc(work_free, 1)
                    elif kind == "up_g":
                        dve.wait_ge(th_ready, 2 * NJ * t.v + k + 1)
                        wait(dve, inter_ready, 2 * NJ * t.v + k - 1)
                        nc.vector.scalar_tensor_tensor(b.ag[:, k % 2], b.th[:, k % 2], 1.0, gu_ps[:, k % 2], ALU.add, ALU.mult).then_inc(g_used, 1)
                    elif kind == "up_u":
                        dve.wait_ge(u_full, 2 * NJ * t.v + k + 1)
                        dve.wait_ge(g_used, 2 * NJ * t.v + k + 1)
                        if k == 0:
                            wait(dve, out_ready, t.v)
                        nc.vector.tensor_tensor(b.inter[:, k // 2, k % 2], b.ag[:, k % 2], gu_ps[:, k % 2], ALU.mult).then_inc(inter_ready, 1)

            run_bodies(dve, "dve", body)

        @block.tensor
        def _(pe):
            def up(weights, t, k):
                q, to, cols = k % 2, gu_ps[:, k % 2, :], slice(HC * (k // 2), HC * (k // 2) + HC)
                nc.tensor.matmul(to, weights[:, 0, cols], b.x2f[t.p][:, q, :], start=True, stop=False)
                return nc.tensor.matmul(to, weights[:, 1 + q, cols], b.x2f[t.p][:, 2, :], start=False, stop=True)

            def spread(t, n, c, bank):
                rhs, edge = b.parts[t.p][:, c, :], 512 - L
                row = lambda q: b.pick[:, 16 * q + n:16 * q + n + 1].broadcast_to([96, 128])
                to = lambda first, last: flat[:, bank + first:bank + last]
                nc.tensor.matmul(to(0, L), row(0), rhs, start=True, stop=True)
                nc.tensor.matmul(to(L, 512), row(1), rhs[:, 0:edge], start=True, stop=True)
                nc.tensor.matmul(to(512, 2 * L), row(1), rhs[:, edge:L], start=True, stop=True)
                return nc.tensor.matmul(to(2 * L, 3 * L), b.pick2[:, n, :], rhs, start=True, stop=True)

            def body(i, todo, use):
                for kind, lag, k in todo:
                    t = i.plus(-lag)
                    if BANK.get(kind) == WORK:
                        wait(pe, work_free, use(kind, k) - 1)
                    elif kind in ("down_a", "emb_a"):
                        wait(pe, sums_free, use(kind[:-2], k) - 1)
                    if kind == "fill_b":
                        if k == 0:
                            pe.wait_ge(parts_ready, t.v + 1)
                        wait(pe, b_copied, N * t.v + k)
                        spread(t, k, 0, b_bank).then_inc(b_full, 1)
                    elif kind == "fill_c":
                        wait(pe, c_used, N * t.v + k)
                        spread(t, k, 1, c_bank).then_inc(c_full, 1)
                    elif kind in ("down_a", "down"):
                        pe.wait_ge(inter_ready, 2 * NJ * (t.v + 1))
                        q = 0 if kind == "down_a" else 1
                        for j in range(NJ):
                            mm = nc.tensor.matmul(sums[0:ROWS[k], D * q:D * q + D], b.inter[:, j, q, OFF[k]:OFF[k] + ROWS[k]], b.ws_d[:, j, :],
                                                  start=(j == 0), stop=(j == NJ - 1))
                        if q == 1:
                            mm.then_inc(sums_full, 1)
                    elif kind == "resid":
                        pe.wait_ge(y_added, 15 * (t.v + 1))
                        for q in range(3):
                            mm = nc.tensor.transpose(work[0:ROWS[k], 128 * q:128 * q + 128], b.y[t.p][:, q, OFF[k]:OFF[k] + ROWS[k]], b.ident[:])
                        mm.then_inc(work_full, 1)
                    elif kind in ("x1_turn", "x2_turn"):
                        m = int(kind[1]) - 1
                        pe.wait_ge(ln_done[m], t.v + 1)
                        x = (b.xn, b.x2)[m]
                        for c in range(3):
                            r = ROWS[c]
                            source = x[0:r, k, c, 0:LO] if k < 2 else b.xm[m][0:r, c].rearrange("p b d -> p (b d)")
                            mm = nc.tensor.transpose(work[:, OFF[c]:OFF[c] + r], source, b.ident[0:r, 0:r])
                        mm.then_inc(work_full, 1)
                    elif kind == "gate":
                        for c in range(3):
                            to, at = work[0:ROWS[c], E * c:E * c + E], slice(OFF[c], OFF[c] + ROWS[c])
                            nc.tensor.matmul(to, b.x2f[t.p][:, k, at], b.wg[:, 0, :], start=True, stop=False)
                            mm = nc.tensor.matmul(to, b.x2f[t.p][:, 2, at], b.wg[:, 1 + k, :], start=False, stop=True)
                        mm.then_inc(work_full, 1)
                    elif kind == "count":
                        pe.wait_ge(mask_ready, t.v + 1)
                        turned = work.bitcast(BF16)
                        for q in range(2):
                            for c in range(3):
                                r = ROWS[c]
                                mm = nc.tensor.transpose(turned[:, L * q + OFF[c]:L * q + OFF[c] + r], b.mask[0:r, 3 * q + c, :], b.ident_bf[0:r, 0:r])
                        mm.then_inc(work_full, 1)
                    elif kind == "find":
                        pe.wait_ge(find_ready, 2)
                        for c in range(2):
                            for q in range(2):
                                mm = nc.tensor.transpose(work[0:HALF, (2 * c + q) * E:(2 * c + q + 1) * E], b.block_of[:, c, HALF * q:HALF * q + HALF], b.ident[:])
                        mm.then_inc(work_full, 1)
                    elif kind in ("emb_a", "emb"):
                        pe.wait_ge(sq_ready, 2 * t.v + k + 1)
                        c = 0 if kind == "emb_a" else 1
                        at = slice(98 * c, 98 * c + 98)
                        for f in range(PC):
                            mm = nc.tensor.matmul(sums[0:98, 196 * c + D + 2:196 * c + D + 4], b.x_sq[:, f, at], b.ones[:, 0:2], start=(f == 0), stop=(f == PC - 1))
                        if c == 1:
                            mm.then_inc(sq_used, 1)
                        for f in range(PC):
                            mm = nc.tensor.matmul(sums[0:98, 196 * c:196 * c + D + 2], b.x_in[:, k, f, at], b.w_tok[:, f, :], start=(f == 0), stop=(f == PC - 1))
                        if c == 1:
                            mm.then_inc(sums_full, 1)
                    elif kind == "bc_values":
                        for q in range(3):
                            mm = nc.tensor.matmul(work[0:96, 0:L], b.wbc[:, q, :], b.xf[:, q, :], start=(q == 0), stop=(q == 2))
                        mm.then_inc(work_full, 1)
                    elif kind == "step_size":
                        if k == 0:
                            pe.wait_ge(parts_ready, t.v + 1)
                        pick = b.pick[:, 16 * k:16 * k + 1].broadcast_to([96, 128]) if k < 2 else b.pick2[:, 0, :]
                        mm = nc.tensor.matmul(work[:, 0:L], pick, b.parts[t.p][:, 2, :], start=True, stop=True)
                        mm.then_inc(work_full, 1)
                    elif kind == "up_g":
                        wait(pe, inter_ready, 2 * NJ * t.v + k - 1)
                        up(b.ws_g, t, k).then_inc(g_full, 1)
                    elif kind == "up_u":
                        pe.wait_ge(g_used, 2 * NJ * t.v + k + 1)
                        up(b.ws_u, t, k).then_inc(u_full, 1)

            run_bodies(pe, "pe", body)


EXPERT_ORDER = [
    ("load_up", -1), ("token", -2), ("row", -3), ("up_g", 0), ("turn", -1), ("down", 1), ("load_down", -1),
    ("up_u", 0), ("scatter", 1), ("gate", -1),
]
E_FIRST, E_FROM, E_TO, E_LAST = -3, 3, 125, E


def run_experts(eng, body):
    def todo(i):
        return [x for x in EXPERT_ORDER if 0 <= i - x[1] < E]

    for i in range(E_FIRST, E_FROM):
        body(Turn.fixed(i), todo(i))
    with eng.Fori(0, (E_TO - E_FROM) // 2) as r:
        for q in range(2):
            start = Turn.fixed(E_FROM + q)
            body(Turn(start.v + 2 * r, start.p, start.h + r), EXPERT_ORDER)
    for i in range(E_TO, E_LAST + 1):
        body(Turn.fixed(i), todo(i))


def phase2(nc, ctx, a, out, dram_x, dram_cnt, ident, found):
    sb = lambda name, shape, dt=F32: ctx.enter_context(nc.sbuf_tensor(name, shape, dt))
    sem = lambda name: ctx.enter_context(nc.semaphore(name))
    KC = D // 2
    base, row = found
    slot_int = sb("slot_int", [HALF, 2], U32)
    tokens = sb("tokens", [HALF, 2, E])
    two = lambda name, shape, dt=F32: [sb(f"{name}{p}", shape, dt) for p in range(2)]
    row_idx, gather_idx, scatter_idx = (two(n, [HALF, 2], U32) for n in ("row_idx", "gather_idx", "scatter_idx"))
    counts = two("counts", [HALF, 2, L])
    passed = sb("passed", [HALF, 2, L])
    tk = sb("tk", [HALF, 3, 2])
    xg = two("xg", [HALF, 2, XW])
    xgt = two("xgt", [KC, 2, CAP])
    w_up = two("w_up", [KC, 2, 2 * HID + 1])
    w_down = two("w_down", [HC, NF, D])
    tw = sb("tw", [HALF, 2])
    weight = two("weight", [HALF, 2])
    th = sb("e_th", [HC, 2, 2 * CAP])
    ag = sb("e_ag", [HC, 2, 2 * CAP])
    inter = sb("e_inter", [HC, 2, 2 * CAP])
    yo = two("yo", [HALF, 2, D])
    ps = ctx.enter_context(nc.psum_tensor("e_ps", [128, 8, 512], F32))
    g_ps, u_ps = ps[0:HC, 0:2, 0:2 * CAP], ps[0:HC, 2:4, 0:2 * CAP]

    slots_counted = sem("slots_counted")
    with nc.Block() as block:

        @block.gpsimd
        def _(pool):
            nc.gpsimd.iota(slot_int[:], [[HALF, 2]], base=0, channel_multiplier=1).then_inc(slots_counted, 1)

        @block.vector
        def _(dve):
            dve.wait_ge(slots_counted, 1)
            nc.vector.tensor_copy(tk[:, 0, :], slot_int[:])

    up_loaded = [sem(f"up_loaded{p}") for p in range(2)]
    down_loaded = [sem(f"down_loaded{p}") for p in range(2)]
    row_ready, counts_loaded = sem("row_ready"), [sem(f"counts_loaded{p}") for p in range(2)]
    passed_ready, sum_ready, token_steps = sem("passed_ready"), sem("sum_ready"), sem("token_steps")
    token_ready, x_gathered = sem("token_ready"), [sem(f"x_gathered{p}") for p in range(2)]
    turn_full, xgt_ready, gate_full, tw_ready, weight_ready = (sem(n) for n in ("turn_full", "xgt_ready", "gate_full", "tw_ready", "weight_ready"))
    e_g_full, e_th_ready, e_g_used, e_u_full, e_inter_ready = (sem(n) for n in ("e_g_full", "e_th_ready", "e_g_used", "e_u_full", "e_inter_ready"))
    down_full, yo_ready, scatter_ready = sem("down_full"), sem("yo_ready"), sem("scatter_ready")
    added = [sem(f"added{p}") for p in range(2)]
    waited = sem("e_waited")

    with nc.Block() as block:

        @block.sync
        def _(sp):
            def body(i, todo):
                for kind, lag in todo:
                    t = i.plus(-lag)
                    if kind == "load_up":
                        wait(sp, e_u_full, t.v - 1)
                        sp.dma_start(w_up[t.p][:], a["we_up"][bass.ds(t.v, 1)].rearrange("o p c f -> p (o c) f")).then_inc(up_loaded[t.p], 16)
                    elif kind == "load_down":
                        wait(sp, down_full, t.v - 1)
                        sp.dma_start(w_down[t.p][:], a["we_down"][bass.ds(t.v, 1)].rearrange("o p c f -> p (o c) f")).then_inc(down_loaded[t.p], 16)

            run_experts(sp, body)

        @block.gpsimd
        def _(pool):
            def body(i, todo):
                for kind, lag in todo:
                    t = i.plus(-lag)
                    if kind == "row":
                        pool.wait_ge(row_ready, t.v + 1)
                        wait(pool, passed_ready, t.v - 1)
                        pool.sem_inc(waited, 1)
                        for q in range(2):
                            nc.gpsimd.indirect_dma_start(counts[t.p][:, q, :], None, dram_cnt, bass.IndirectOffsetOnAxis(ap=row_idx[t.p][:, q:q + 1], axis=0)).then_inc(counts_loaded[t.p], 16)
                    elif kind == "token":
                        pool.wait_ge(token_ready, t.v + 1)
                        wait(pool, weight_ready, t.v - 1)
                        pool.sem_inc(waited, 1)
                        for q in range(2):
                            nc.gpsimd.indirect_dma_start(xg[t.p][:, q, :], None, dram_x, bass.IndirectOffsetOnAxis(ap=gather_idx[t.p][:, q:q + 1], axis=0)).then_inc(x_gathered[t.p], 16)
                    elif kind == "scatter":
                        pool.wait_ge(scatter_ready, t.v + 1)
                        pool.wait_ge(yo_ready, t.v + 1)
                        before = t.plus(-1)
                        wait(pool, added[before.p], 32 * before.h + 32)
                        pool.sem_inc(waited, 1)
                        for q in range(2):
                            nc.gpsimd.indirect_dma_start(out, bass.IndirectOffsetOnAxis(ap=scatter_idx[t.p][:, q:q + 1], axis=0), yo[t.p][:, q, :], None, compute_op=ALU.add).then_inc(added[t.p], 16)

            run_experts(pool, body)
            for p in range(2):
                pool.wait_ge(added[p], 32 * E // 2)

        @block.scalar
        def _(act):
            def body(i, todo):
                for kind, lag in todo:
                    t = i.plus(-lag)
                    if kind == "turn":
                        act.wait_ge(turn_full, t.v + 1)
                        wait(act, e_u_full, t.v - 1)
                        nc.scalar.activation(xgt[t.p][:].rearrange("p c s -> p (c s)"), ps[0:KC, 5, 0:2 * CAP], ACT.Copy).then_inc(xgt_ready, 1)
                    elif kind == "gate":
                        act.wait_ge(gate_full, t.v + 1)
                        wait(act, weight_ready, t.v)
                        nc.scalar.activation(tw[:], ps[0:HALF, 6, 0:2], ACT.Tanh, scale=0.5).then_inc(tw_ready, 1)
                    elif kind == "up_g":
                        act.wait_ge(e_g_full, t.v + 1)
                        wait(act, e_g_used, t.v)
                        nc.scalar.activation(th[:], g_ps, ACT.Tanh, scale=0.5).then_inc(e_th_ready, 1)

            run_experts(act, body)

        @block.vector
        def _(dve):
            def body(i, todo):
                for kind, lag in todo:
                    t = i.plus(-lag)
                    if kind == "row":
                        wait(dve, counts_loaded[t.p], 32 * t.h)
                        nc.vector.tensor_copy(row_idx[t.p][:], row[:, :, bass.ds(t.v, 1)].rearrange("p q o -> p (q o)")).then_inc(row_ready, 1)
                    elif kind == "token":
                        dve.wait_ge(counts_loaded[t.p], 32 * t.h + 32)
                        slots = tk[:, 0, :].unsqueeze(2).broadcast_to([HALF, 2, L])
                        nc.vector.tensor_tensor(passed[:], counts[t.p][:], slots, ALU.is_le).then_inc(passed_ready, 1)
                        dve.wait_ge(passed_ready, t.v + 1)
                        nc.vector.tensor_reduce(tk[:, 1, :], passed[:], AX.X, ALU.add).then_inc(sum_ready, 1)
                        dve.wait_ge(sum_ready, t.v + 1)
                        nc.vector.tensor_tensor(tk[:, 1, :], tk[:, 1, :], base[:, :, bass.ds(t.v, 1)].rearrange("p q o -> p (q o)"), ALU.add).then_inc(token_steps, 1)
                        dve.wait_ge(token_steps, 2 * t.v + 1)
                        nc.vector.scalar_tensor_tensor(tk[:, 2, :], tk[:, 1, :], float(T_ALL), tk[:, 0, :], ALU.is_ge, ALU.mult).then_inc(token_steps, 1)
                        dve.wait_ge(token_steps, 2 * t.v + 2)
                        wait(dve, x_gathered[t.p], 32 * t.h)
                        nc.vector.tensor_tensor(tokens[:, :, bass.ds(t.v, 1)].rearrange("p q o -> p (q o)"), tk[:, 1, :], tk[:, 2, :], ALU.add)
                        nc.vector.tensor_tensor(gather_idx[t.p][:], tk[:, 1, :], tk[:, 2, :], ALU.add).then_inc(token_ready, 1)
                    elif kind == "up_g":
                        dve.wait_ge(e_th_ready, t.v + 1)
                        wait(dve, e_inter_ready, t.v)
                        nc.vector.scalar_tensor_tensor(ag[:], th[:], 1.0, g_ps, ALU.add, ALU.mult).then_inc(e_g_used, 1)
                    elif kind == "down":
                        dve.wait_ge(down_full, t.v + 1)
                        dve.wait_ge(weight_ready, t.v + 1)
                        wait(dve, added[t.p], 32 * t.h)
                        nc.vector.tensor_tensor(yo[t.p][:], ps[0:HALF, 4, 0:2 * D].rearrange("p (q d) -> p q d", q=2),
                                                weight[t.p][:].unsqueeze(2).broadcast_to([HALF, 2, D]), ALU.mult).then_inc(yo_ready, 1)
                        nc.vector.tensor_copy(scatter_idx[t.p][:], tokens[:, :, bass.ds(t.v, 1)].rearrange("p q o -> p (q o)")).then_inc(scatter_ready, 1)
                    elif kind == "up_u":
                        dve.wait_ge(e_u_full, t.v + 1)
                        dve.wait_ge(e_g_used, t.v + 1)
                        wait(dve, down_full, t.v)
                        nc.vector.tensor_tensor(inter[:], ag[:], u_ps, ALU.mult).then_inc(e_inter_ready, 1)
                    elif kind == "gate":
                        dve.wait_ge(tw_ready, t.v + 1)
                        dve.wait_ge(x_gathered[t.p], 32 * t.h + 32)
                        wait(dve, yo_ready, t.v - 1)
                        nc.vector.scalar_tensor_tensor(weight[t.p][:], tw[:], 1.0, xg[t.p][:, :, D], ALU.add, ALU.mult).then_inc(weight_ready, 1)

            run_experts(dve, body)

        @block.tensor
        def _(pe):
            def apply(to_bank, t, first):
                for f in range(NF):
                    for c in range(2):
                        mm = nc.tensor.matmul(ps[0:HC, to_bank + f // 2, CAP * (f % 2):CAP * (f % 2) + CAP],
                                              w_up[t.p][:, c, first + HC * f:first + HC * f + HC], xgt[t.p][:, c, :], start=(c == 0), stop=(c == 1))
                return mm

            def body(i, todo):
                for kind, lag in todo:
                    t = i.plus(-lag)
                    if kind == "turn":
                        pe.wait_ge(x_gathered[t.p], 32 * t.h + 32)
                        wait(pe, xgt_ready, t.v)
                        for c in range(2):
                            for q in range(2):
                                mm = nc.tensor.transpose(ps[0:KC, 5, CAP * c + HALF * q:CAP * c + HALF * q + HALF], xg[t.p][:, q, KC * c:KC * c + KC], ident[0:HALF, 0:HALF])
                        mm.then_inc(turn_full, 1)
                    elif kind == "gate":
                        pe.wait_ge(xgt_ready, t.v + 1)
                        pe.wait_ge(up_loaded[t.p], 16 * t.h + 16)
                        wait(pe, tw_ready, t.v)
                        for q in range(2):
                            for c in range(2):
                                mm = nc.tensor.matmul(ps[0:HALF, 6, q:q + 1], xgt[t.p][:, c, HALF * q:HALF * q + HALF], w_up[t.p][:, c, 2 * HID:2 * HID + 1], start=(c == 0), stop=(c == 1))
                        mm.then_inc(gate_full, 1)
                    elif kind == "up_g":
                        wait(pe, e_g_used, t.v)
                        apply(0, t, 0).then_inc(e_g_full, 1)
                    elif kind == "up_u":
                        wait(pe, e_inter_ready, t.v)
                        apply(2, t, HID).then_inc(e_u_full, 1)
                    elif kind == "down":
                        pe.wait_ge(e_inter_ready, t.v + 1)
                        pe.wait_ge(down_loaded[t.p], 16 * t.h + 16)
                        wait(pe, yo_ready, t.v)
                        for q in range(2):
                            for f in range(NF):
                                at = CAP * (f % 2) + HALF * q
                                mm = nc.tensor.matmul(ps[0:HALF, 4, D * q:D * q + D], inter[:, f // 2, at:at + HALF], w_down[t.p][:, f, :], start=(f == 0), stop=(f == NF - 1))
                        mm.then_inc(down_full, 1)

            run_experts(pe, body)


def _layout(i):
    import numpy as np

    x = np.asarray(i["x"]).reshape(B, 3, 14, 16, 14, 16).transpose(0, 3, 5, 1, 2, 4).reshape(B, PC, 128, IMG).transpose(0, 2, 1, 3)
    up = np.concatenate([np.asarray(i["L0_ffn_W_gate_up"]), np.asarray(i["L0_ffn_Wg"])[:, :, None]], axis=2)
    n = lambda k: np.asarray(i["L0_" + k])
    return {
        "x": x,
        "txt": np.asarray(i["txt"]),
        "ln_w": n("tok_ln_w").reshape(PC, 128).T,
        "ln_b": n("tok_ln_b").reshape(PC, 128).T,
        "w_tok": n("tok_W").reshape(PC, 128, D).transpose(1, 0, 2),
        "b_tok": n("tok_b").reshape(1, D),
        "pos": n("tok_pos_emd").reshape(2, 98, D).transpose(1, 0, 2),
        "a_log": n("attn_A_log"),
        "w_bc_t": n("attn_W_bc").T,
        "b_bc": n("attn_b_bc").reshape(2 * N, 1),
        "w_1": n("attn_W_1").reshape(D, 1),
        "b_1": n("attn_b_1").reshape(1, 1),
        "w_d": n("attn_W_d").reshape(D, 1),
        "b_d": n("attn_b_d").reshape(D, 1),
        "wg_t": n("ffn_Wg").T,
        "e_bias": n("ffn_e_bias").reshape(1, E),
        "we_up": up.reshape(E, 2, 96, 2 * HID + 1).transpose(0, 2, 1, 3),
        "we_down": n("ffn_W_down").reshape(E, NF, HC, D).transpose(0, 2, 1, 3),
        "ws_g": n("ffn_Wsg"),
        "ws_u": n("ffn_Wsu"),
        "ws_d": n("ffn_Wsd").reshape(NJ, HC, D).transpose(1, 0, 2),
    }


def kernel(**inputs):
    import numpy as np
    import concourse.bacc as bacc
    from concourse.bass_utils import run_bass_kernel_spmd

    nc = bacc.Bacc("TRN2", target_bir_lowering=False, num_devices=1)
    arrays, args = {}, {}
    for name, value in _layout(inputs).items():
        arrays[f"in_{name}"] = np.ascontiguousarray(value)
        args[name] = nc.dram_tensor(f"in_{name}", value.shape, mybir.dt.from_np(value.dtype), kind="ExternalInput").ap()
    out = nc.dram_tensor("out_rows", (T_ALL + CAP, D), F32, kind="ExternalOutput").ap()
    build(nc, args, out)
    got = run_bass_kernel_spmd(nc, [arrays], core_ids=[0]).results[0]["out_rows"]
    return got[0:T_ALL].reshape(B, L, D)
```
